# Optimizing a Trainium2 kernel written in Bass

```python
import numpy as np
import jax
import jax.numpy as jnp

def _softmax(x, axis=-1):
    return jax.nn.softmax(x, axis=axis)

def _gelu(x):
    return jax.nn.gelu(x, approximate=True)

def _silu(x):
    return jax.nn.silu(x)

def _sigmoid(x):
    return jax.nn.sigmoid(x)

def _layernorm(x, axis=-1, eps=1e-05):
    m = jnp.mean(x, axis=axis, keepdims=True)
    v = jnp.var(x, axis=axis, keepdims=True)
    return (x - m) / jnp.sqrt(v + eps)

def _scatter_add(tgt, idx, src, axis=0):
    return tgt.at[idx].add(src)

def _segment_sum(src, seg, n):
    return jax.ops.segment_sum(src, seg, n)
kernel_name = 'mk_recurrent_d2_jaxref_r4_4890a3'

def setup_inputs(seed: int=0):
    np.random.seed(seed)
    _w = jnp.asarray

    def _L0_attn_setup():
        import math
        import jax, jax.numpy as jnp
        import numpy as np
        BLOCK = 64

        def build_slope_tensor(n_heads):

            def p2(n):
                start = 2.0 ** (-2.0 ** (-(math.log2(n) - 3)))
                return [start * start ** i for i in range(n)]
            if math.log2(n_heads).is_integer():
                s = p2(n_heads)
            else:
                closest = 2 ** math.floor(math.log2(n_heads))
                s = p2(closest) + p2(2 * closest)[0::2][:n_heads - closest]
            return jnp.asarray(np.array(s, dtype=np.float32))

        def lightning_attn(q, k, v, slopes, block=BLOCK):
            B, H, N, d = q.shape
            nc = N // block
            i = jnp.arange(block, dtype=q.dtype)
            diff = i[:, None] - i[None, :]
            intra_decay = jnp.where(diff >= 0, jnp.exp(-slopes[:, None, None] * diff), 0.0)
            q_decay = jnp.exp(-slopes[:, None] * i[None, :])
            k_decay = jnp.exp(-slopes[:, None] * (block - i[None, :]))
            blk_decay = jnp.exp(-slopes * block)

            def to_chunks(t):
                return t.reshape(B, H, nc, block, d).transpose(2, 0, 1, 3, 4)
            qc, kc, vc = (to_chunks(q), to_chunks(k), to_chunks(v))

            def body(S, xs):
                qb, kb, vb = xs
                scores = jnp.einsum('bhid,bhjd->bhij', qb, kb) * intra_decay[None]
                o_intra = jnp.einsum('bhij,bhjd->bhid', scores, vb)
                o_inter = jnp.einsum('bhid,bhde->bhie', qb * q_decay[None, :, :, None], S)
                S_new = blk_decay[None, :, None, None] * S + jnp.einsum('bhjd,bhje->bhde', kb * k_decay[None, :, :, None], vb)
                return (S_new, o_intra + o_inter)
            S0 = jnp.zeros((B, H, d, d), dtype=q.dtype)
            _, o = jax.lax.scan(body, S0, (qc, kc, vc))
            return o.transpose(1, 2, 0, 3, 4).reshape(B, H, N, d)
        key = jax.random.key(seed)
        k1, k2, k3 = jax.random.split(key, 3)
        dim, num_heads = (512, 16)
        B, N = (2, 1024)
        x = jax.random.normal(k1, (B, N, dim), dtype=jnp.float32)
        Wqkv = jax.random.normal(k2, (dim, 3 * dim), dtype=jnp.float32) / math.sqrt(dim)
        bqkv = jnp.zeros((3 * dim,), dtype=jnp.float32)
        Wout = jax.random.normal(k3, (dim, dim), dtype=jnp.float32) / math.sqrt(dim)
        bout = jnp.zeros((dim,), dtype=jnp.float32)
        slopes = build_slope_tensor(num_heads)
        return {'x': x, 'Wqkv': Wqkv, 'bqkv': bqkv, 'Wout': Wout, 'bout': bout, 'slopes': slopes}
    _L0_attn_in = _L0_attn_setup()

    def _L0_ffn_setup():
        import jax, jax.numpy as jnp
        import numpy as np
        EPS = 1e-06
        Q_B = 128.0

        def layer_norm(x):
            mean = jnp.mean(x, axis=-1, keepdims=True)
            var = jnp.var(x, axis=-1, keepdims=True)
            return (x - mean) / jnp.sqrt(var + EPS)

        def absmax_quant(x):
            gamma = jnp.max(jnp.abs(x), axis=-1, keepdims=True)
            x_hat = jnp.clip(x * Q_B / gamma, -Q_B + EPS, Q_B - EPS)
            return x_hat * gamma / Q_B

        def ternarize_weights(w):
            gamma = jnp.mean(jnp.abs(w))
            return jnp.sign(jnp.round(w / (gamma + EPS))) * gamma

        def bitlinear(x, w):
            xn = layer_norm(x)
            x_hat = xn + jax.lax.stop_gradient(absmax_quant(xn) - xn)
            w_hat = w + jax.lax.stop_gradient(ternarize_weights(w) - w)
            return jnp.einsum('bsd,od->bso', x_hat, w_hat)
        key = jax.random.key(seed)
        k1, k2, k3 = jax.random.split(key, 3)
        B, S, D = (4, 512, 512)
        x = jax.random.normal(k1, (B, S, D), dtype=jnp.float32)
        w_fc = jax.random.normal(k2, (4 * D, D), dtype=jnp.float32) / np.sqrt(D)
        w_proj = jax.random.normal(k3, (D, 4 * D), dtype=jnp.float32) / np.sqrt(4 * D)
        return {'x': x, 'w_fc': w_fc, 'w_proj': w_proj}
    _L0_ffn_in = _L0_ffn_setup()

    def _L1_attn_setup():
        import jax, jax.numpy as jnp
        import numpy as np
        import math
        B, T, DIM, NH = (2, 512, 512, 16)
        HD = DIM // NH

        def rotate_half(x):
            h = x.shape[-1] // 2
            return jnp.concatenate([-x[..., h:], x[..., :h]], axis=-1)

        def rope_tables(t_len, rot_dim, base=10000.0, dtype=jnp.float32):
            inv_freq = 1.0 / base ** (jnp.arange(0, rot_dim, 2, dtype=dtype) / rot_dim)
            t = jnp.arange(t_len, dtype=dtype)
            ang = jnp.einsum('i,j->ij', t, inv_freq)
            return (jnp.sin(ang), jnp.cos(ang))

        def apply_rope(q, k, sin, cos):
            h = q.shape[-1] // 2
            q1, q2 = (q[..., :h], q[..., h:])
            k1, k2 = (k[..., :h], k[..., h:])
            sin = sin[None, None]
            cos = cos[None, None]
            q1r = q1 * cos + rotate_half(q1) * sin
            k1r = k1 * cos + rotate_half(k1) * sin
            return (jnp.concatenate([q1r, q2], axis=-1), jnp.concatenate([k1r, k2], axis=-1))
        key = jax.random.key(seed)
        ks = jax.random.split(key, 5)
        s = 1.0 / math.sqrt(DIM)
        return {'x': jax.random.normal(ks[0], (B, T, DIM), jnp.float32), 'wq': jax.random.normal(ks[1], (DIM, DIM), jnp.float32) * s, 'wk': jax.random.normal(ks[2], (DIM, DIM), jnp.float32) * s, 'wv': jax.random.normal(ks[3], (DIM, DIM), jnp.float32) * s, 'wo': jax.random.normal(ks[4], (DIM, DIM), jnp.float32) * s}
    _L1_attn_in = _L1_attn_setup()

    def _L1_ffn_setup():
        import jax, jax.numpy as jnp
        import numpy as np
        DIM = 512
        HID = 1408
        ZERO_POINT = 128.0

        def _qlinear(x, wq, scale):
            W = (wq.astype(jnp.float32) - ZERO_POINT) * scale[:, None]
            return jnp.einsum('bsd,hd->bsh', x, W)
        key = jax.random.key(seed)
        ks = jax.random.split(key, 7)
        B, S = (4, 512)
        sg = jax.random.uniform(ks[1], (HID,)) * (0.02 / np.sqrt(DIM)) + 0.0001
        su = jax.random.uniform(ks[3], (HID,)) * (0.02 / np.sqrt(DIM)) + 0.0001
        sd = jax.random.uniform(ks[5], (DIM,)) * (0.02 / np.sqrt(HID)) + 0.0001
        return {'x': jax.random.normal(ks[0], (B, S, DIM), dtype=jnp.float32), 'wq_gate': jax.random.randint(ks[2], (HID, DIM), 0, 64, dtype=jnp.int32), 's_gate': sg, 'wq_up': jax.random.randint(ks[4], (HID, DIM), 0, 64, dtype=jnp.int32), 's_up': su, 'wq_down': jax.random.randint(ks[6], (DIM, HID), 0, 64, dtype=jnp.int32), 's_down': sd}
    _L1_ffn_in = _L1_ffn_setup()
    _d = {'L0_attn_x': _L0_attn_in['x'], 'L0_attn_Wqkv': _L0_attn_in['Wqkv'], 'L0_attn_bqkv': _L0_attn_in['bqkv'], 'L0_attn_Wout': _L0_attn_in['Wout'], 'L0_attn_bout': _L0_attn_in['bout'], 'L0_attn_slopes': _L0_attn_in['slopes'], 'L0_ffn_w_fc': _L0_ffn_in['w_fc'], 'L0_ffn_w_proj': _L0_ffn_in['w_proj'], 'L1_attn_wq': _L1_attn_in['wq'], 'L1_attn_wk': _L1_attn_in['wk'], 'L1_attn_wv': _L1_attn_in['wv'], 'L1_attn_wo': _L1_attn_in['wo'], 'L1_ffn_wq_gate': _L1_ffn_in['wq_gate'], 'L1_ffn_s_gate': _L1_ffn_in['s_gate'], 'L1_ffn_wq_up': _L1_ffn_in['wq_up'], 'L1_ffn_s_up': _L1_ffn_in['s_up'], 'L1_ffn_wq_down': _L1_ffn_in['wq_down'], 'L1_ffn_s_down': _L1_ffn_in['s_down']}
    _x0 = _d['L0_attn_x']
    _d['L0_attn_x'] = jax.random.normal(jax.random.fold_in(jax.random.key(seed), 1), (4, 1024, 512), dtype=_x0.dtype)
    del _x0
    return _d

def reference(L0_attn_x, L0_attn_Wqkv, L0_attn_bqkv, L0_attn_Wout, L0_attn_bout, L0_attn_slopes, L0_ffn_w_fc, L0_ffn_w_proj, L1_attn_wq, L1_attn_wk, L1_attn_wv, L1_attn_wo, L1_ffn_wq_gate, L1_ffn_s_gate, L1_ffn_wq_up, L1_ffn_s_up, L1_ffn_wq_down, L1_ffn_s_down):

    def _L0_attn_ref(x, Wqkv, bqkv, Wout, bout, slopes):
        import math
        import jax, jax.numpy as jnp
        import numpy as np
        BLOCK = 64

        def build_slope_tensor(n_heads):

            def p2(n):
                start = 2.0 ** (-2.0 ** (-(math.log2(n) - 3)))
                return [start * start ** i for i in range(n)]
            if math.log2(n_heads).is_integer():
                s = p2(n_heads)
            else:
                closest = 2 ** math.floor(math.log2(n_heads))
                s = p2(closest) + p2(2 * closest)[0::2][:n_heads - closest]
            return jnp.asarray(np.array(s, dtype=np.float32))

        def lightning_attn(q, k, v, slopes, block=BLOCK):
            B, H, N, d = q.shape
            nc = N // block
            i = jnp.arange(block, dtype=q.dtype)
            diff = i[:, None] - i[None, :]
            intra_decay = jnp.where(diff >= 0, jnp.exp(-slopes[:, None, None] * diff), 0.0)
            q_decay = jnp.exp(-slopes[:, None] * i[None, :])
            k_decay = jnp.exp(-slopes[:, None] * (block - i[None, :]))
            blk_decay = jnp.exp(-slopes * block)

            def to_chunks(t):
                return t.reshape(B, H, nc, block, d).transpose(2, 0, 1, 3, 4)
            qc, kc, vc = (to_chunks(q), to_chunks(k), to_chunks(v))

            def body(S, xs):
                qb, kb, vb = xs
                scores = jnp.einsum('bhid,bhjd->bhij', qb, kb) * intra_decay[None]
                o_intra = jnp.einsum('bhij,bhjd->bhid', scores, vb)
                o_inter = jnp.einsum('bhid,bhde->bhie', qb * q_decay[None, :, :, None], S)
                S_new = blk_decay[None, :, None, None] * S + jnp.einsum('bhjd,bhje->bhde', kb * k_decay[None, :, :, None], vb)
                return (S_new, o_intra + o_inter)
            S0 = jnp.zeros((B, H, d, d), dtype=q.dtype)
            _, o = jax.lax.scan(body, S0, (qc, kc, vc))
            return o.transpose(1, 2, 0, 3, 4).reshape(B, H, N, d)
        B, N, C = x.shape
        H = slopes.shape[0]
        hd = C // H
        qkv = (x @ Wqkv + bqkv).reshape(B, N, 3, H, hd)
        qkv = qkv.transpose(2, 0, 3, 1, 4)
        q, k, v = (qkv[0], qkv[1], qkv[2])
        attn = lightning_attn(q, k, v, slopes)
        out = attn.transpose(0, 2, 1, 3).reshape(B, N, C)
        return out @ Wout + bout

    def _L0_ffn_ref(x, w_fc, w_proj):
        import jax, jax.numpy as jnp
        import numpy as np
        EPS = 1e-06
        Q_B = 128.0

        def layer_norm(x):
            mean = jnp.mean(x, axis=-1, keepdims=True)
            var = jnp.var(x, axis=-1, keepdims=True)
            return (x - mean) / jnp.sqrt(var + EPS)

        def absmax_quant(x):
            gamma = jnp.max(jnp.abs(x), axis=-1, keepdims=True)
            x_hat = jnp.clip(x * Q_B / gamma, -Q_B + EPS, Q_B - EPS)
            return x_hat * gamma / Q_B

        def ternarize_weights(w):
            gamma = jnp.mean(jnp.abs(w))
            return jnp.sign(jnp.round(w / (gamma + EPS))) * gamma

        def bitlinear(x, w):
            xn = layer_norm(x)
            x_hat = xn + jax.lax.stop_gradient(absmax_quant(xn) - xn)
            w_hat = w + jax.lax.stop_gradient(ternarize_weights(w) - w)
            return jnp.einsum('bsd,od->bso', x_hat, w_hat)
        h = bitlinear(x, w_fc)
        h = jax.nn.gelu(h, approximate=False)
        return bitlinear(h, w_proj)

    def _L1_attn_ref(x, wq, wk, wv, wo):
        import jax, jax.numpy as jnp
        import numpy as np
        import math
        B, T, DIM, NH = (2, 512, 512, 16)
        HD = DIM // NH

        def rotate_half(x):
            h = x.shape[-1] // 2
            return jnp.concatenate([-x[..., h:], x[..., :h]], axis=-1)

        def rope_tables(t_len, rot_dim, base=10000.0, dtype=jnp.float32):
            inv_freq = 1.0 / base ** (jnp.arange(0, rot_dim, 2, dtype=dtype) / rot_dim)
            t = jnp.arange(t_len, dtype=dtype)
            ang = jnp.einsum('i,j->ij', t, inv_freq)
            return (jnp.sin(ang), jnp.cos(ang))

        def apply_rope(q, k, sin, cos):
            h = q.shape[-1] // 2
            q1, q2 = (q[..., :h], q[..., h:])
            k1, k2 = (k[..., :h], k[..., h:])
            sin = sin[None, None]
            cos = cos[None, None]
            q1r = q1 * cos + rotate_half(q1) * sin
            k1r = k1 * cos + rotate_half(k1) * sin
            return (jnp.concatenate([q1r, q2], axis=-1), jnp.concatenate([k1r, k2], axis=-1))
        b, t, c = x.shape

        def proj(w):
            return (x @ w.T).reshape(b, t, NH, HD).transpose(0, 2, 1, 3)
        q, k, v = (proj(wq), proj(wk), proj(wv))
        sin, cos = rope_tables(t, HD, dtype=x.dtype)
        q, k = apply_rope(q, k, sin, cos)
        att = jnp.einsum('bhqd,bhkd->bhqk', q, k) * (1.0 / math.sqrt(HD))
        att = jax.nn.softmax(att, axis=-1)
        y = jnp.einsum('bhqk,bhkd->bhqd', att, v)
        y = y.transpose(0, 2, 1, 3).reshape(b, t, c)
        return y @ wo.T

    def _L1_ffn_ref(x, wq_gate, s_gate, wq_up, s_up, wq_down, s_down):
        import jax, jax.numpy as jnp
        import numpy as np
        DIM = 512
        HID = 1408
        ZERO_POINT = 128.0

        def _qlinear(x, wq, scale):
            W = (wq.astype(jnp.float32) - ZERO_POINT) * scale[:, None]
            return jnp.einsum('bsd,hd->bsh', x, W)
        gate = _qlinear(x, wq_gate, s_gate)
        gate = jax.nn.silu(gate)
        up = _qlinear(x, wq_up, s_up)
        return _qlinear(gate * up, wq_down, s_down)
    x = L0_attn_x
    xn = _layernorm(x, axis=-1)
    s = _L0_attn_ref(xn, L0_attn_Wqkv, L0_attn_bqkv, L0_attn_Wout, L0_attn_bout, L0_attn_slopes)
    g = _silu(_L0_ffn_ref(xn, L0_ffn_w_fc, L0_ffn_w_proj))
    x = x + s * g
    xn = _layernorm(x, axis=-1)
    s = _L1_attn_ref(xn, L1_attn_wq, L1_attn_wk, L1_attn_wv, L1_attn_wo)
    g = _silu(_L1_ffn_ref(xn, L1_ffn_wq_gate, L1_ffn_s_gate, L1_ffn_wq_up, L1_ffn_s_up, L1_ffn_wq_down, L1_ffn_s_down))
    x = x + s * g
    return x

_drawn_inputs = setup_inputs


def setup_inputs(seed=0):
    import zlib

    import numpy as np

    out = dict(_drawn_inputs(seed))
    spreads = {'L0_attn_bqkv': (0.0, 0.1), 'L0_attn_bout': (0.0, 0.8)}
    factors = {'L1_attn_wq': 8.0,
     'L1_attn_wk': 8.0,
     'L1_attn_wv': 8.0,
     'L1_attn_wo': 8.0,
     'L1_ffn_s_gate': 8.0,
     'L1_ffn_s_up': 8.0,
     'L1_ffn_s_down': 8.0}
    for name, (base, spread) in spreads.items():
        noise = np.random.default_rng([zlib.crc32(name.encode()), seed]).standard_normal(out[name].shape)
        drawn = base * np.exp(spread * noise) if base else spread * noise
        out[name] = jnp.asarray(drawn.astype(out[name].dtype))
    for name, factor in factors.items():
        out[name] = (out[name] * factor).astype(out[name].dtype)
    return out
```

```python
import concourse.bass as bass
from concourse import mybir
from contextlib import ExitStack

F32 = mybir.dt.float32
F32R = mybir.dt.float32r
I32 = mybir.dt.int32
ALU = mybir.AluOpType
ACT = mybir.ActivationFunctionType
AX = mybir.AxisListType

P = 128
BATCH, SEQ, DIM, HEADS = 4, 1024, 512, 16
HD = DIM // HEADS
TOKENS = BATCH * SEQ
CHUNKS = TOKENS // P
CPB = SEQ // P
KD = DIM // P
HPG = P // HD
GROUPS = HEADS // HPG
FC = 4 * DIM
HID = 1408
ZERO_POINT = 128.0
ATT_SCALE = HD ** -0.5


def need(eng, sem, count):
    if isinstance(count, int) and count <= 0:
        return
    eng.wait_ge(sem, count)


def live(c, n):
    return not isinstance(c, int) or 0 <= c < n


def ticks(eng, first, loop_from, loop_to, last, tick):
    for t in range(first, loop_from):
        tick(t, t % 2)
    with eng.Fori(0, (loop_to - loop_from) // 2) as i:
        for p in range(2):
            tick(2 * i + (loop_from + p), (loop_from + p) % 2)
    for t in range(loop_to, last + 1):
        tick(t, t % 2)


def fp32(ap):
    return ap.bitcast(F32)


def three_pass(pe, out, a_hi, a_lo, w_hi, w_lo, slices, bank_done):
    n = 0
    for k in range(slices):
        for a, w in ((a_hi, w_hi), (a_lo, w_hi), (a_hi, w_lo)):
            mm = pe.matmul(out, a(k), w(k), start=(n == 0), stop=(n == 3 * slices - 1))
            n += 1
    mm.then_inc(bank_done, 1)


def two_pass(pe, out, a_hi, a_lo, w, ks, first, last):
    for k in ks:
        for n, a in enumerate((a_hi, a_lo)):
            mm = pe.matmul(out, a(k), w(k), start=(first and k == ks[0] and n == 0),
                           stop=(last and k == ks[-1] and n == 1))
    return mm


def cap(count, most):
    return min(count, most) if isinstance(count, int) else count


def layer0_attention(nc, x, Wqkv, bqkv, Wout, bout, slopes, s_out):
    x_t = x.rearrange("b (c p) d -> (b c) p d", p=P)
    s_t = s_out.rearrange("(c p) d -> c p d", p=P)
    QKV = 3 * DIM
    with ExitStack() as ctx:
        sb = lambda name, shape, dt=F32: ctx.enter_context(nc.sbuf_tensor(f"l0_attn_{name}", shape, dt))
        sem = lambda name: ctx.enter_context(nc.semaphore(f"l0_attn_{name}"))
        wq_hi, wq_lo = (sb(f"wqkv_{n}", [P, KD, QKV], F32R) for n in ("hi", "lo"))
        wo_hi, wo_lo = (sb(f"wout_{n}", [P, KD, DIM], F32R) for n in ("hi", "lo"))
        bias = sb("bias", [P, QKV])
        bias_out = sb("bias_out", [P, DIM])
        ident = sb("ident", [P, P])
        decay = sb("decay", [P, HEADS, P])
        q_decay = sb("q_decay", [P, GROUPS, P])
        k_decay = sb("k_decay", [P, HEADS])
        blk_decay = sb("blk_decay", [P, GROUPS])
        own_head = sb("own_head", [P, GROUPS, P])
        keep = sb("keep", [P, CHUNKS])
        bn_eps = sb("ln_eps", [P, 1])
        minus_half = sb("minus_half", [P, 1])

        with ExitStack() as prep:
            psb = lambda name, shape, dt=F32: prep.enter_context(nc.sbuf_tensor(f"l0_attn_{name}", shape, dt))
            raw_q = psb("raw_q", [P, 2, QKV])
            raw_o = psb("raw_o", [P, KD, DIM])
            dist = psb("dist", [P, P])
            pos = psb("pos", [P, P])
            left = psb("left", [P, 1])
            slope_row = psb("slope_row", [P, HEADS])
            slope_col = psb("slope_col", [P, GROUPS])
            psem = lambda name: prep.enter_context(nc.semaphore(f"l0_attn_{name}"))
            raw_in, raw_o_in, small_in = psem("raw_in"), psem("raw_o_in"), psem("small_in")
            raw_used, w_split, iotas, scaled, decays = (psem(n) for n in ("raw_used", "w_split", "iotas", "scaled", "decays"))
            made = psem("made")
            block = prep.enter_context(nc.Block())
            wq_t = Wqkv.rearrange("(k p) n -> p k n", p=P)

            @block.sync
            def _(sp):
                sp.dma_start(raw_q[:, :, :], wq_t[:, 0:2, :]).then_inc(raw_in, 16)
                sp.dma_start(raw_o[:, :, :], Wout.rearrange("(k p) n -> p k n", p=P)).then_inc(raw_o_in, 16)
                sp.wait_ge(raw_used, 1)
                sp.dma_start(raw_q[:, :, :], wq_t[:, 2:4, :]).then_inc(raw_in, 16)

            @block.scalar
            def _(act):
                act.dma_start(slope_row[:, :], slopes.rearrange("(a h) -> a h", a=1).to_broadcast([P, HEADS])).then_inc(small_in, 16)
                for h in range(HPG):
                    act.dma_start(slope_col[HD * h:HD * h + HD, :],
                                  slopes.rearrange("(a g h) -> h a g", a=1, h=HPG)[h].to_broadcast([HD, GROUPS]),
                                  allow_slow_non_contiguous=True).then_inc(small_in, 16)
                act.dma_start(bias[:, :], bqkv.rearrange("(a n) -> a n", a=1).to_broadcast([P, QKV])).then_inc(small_in, 16)
                act.dma_start(bias_out[:, :], bout.rearrange("(a n) -> a n", a=1).to_broadcast([P, DIM])).then_inc(small_in, 16)
                act.wait_ge(small_in, 16 * (HPG + 3))
                act.wait_ge(iotas, 4)
                act.wait_ge(scaled, 1)
                for h in range(HEADS):
                    act.activation(decay[:, h, :], dist[:, :], ACT.Exp, scale=slope_row[:, h:h + 1]).then_inc(decays, 1)
                for g in range(GROUPS):
                    act.activation(q_decay[:, g, :], pos[:, :], ACT.Exp, scale=slope_col[:, g:g + 1]).then_inc(decays, 1)
                act.activation(k_decay[:, :], slope_row[:, :], ACT.Exp, scale=left[:, 0:1]).then_inc(decays, 1)
                act.activation(blk_decay[:, :], slope_col[:, :], ACT.Exp, scale=float(P)).then_inc(decays, 1)

            @block.gpsimd
            def _(pool):
                pool.iota(dist[:, :], [[1, P]], base=0, channel_multiplier=-1,
                          allow_small_or_imprecise_dtypes=True).then_inc(made, 1)
                pool.wait_ge(made, 1)
                pool.tensor_scalar(dist[:, :], dist[:, :], 0.0, None, ALU.max).then_inc(iotas, 1)
                pool.iota(pos[:, :], [[1, P]], base=0, channel_multiplier=0,
                          allow_small_or_imprecise_dtypes=True).then_inc(iotas, 1)
                pool.iota(left[:, :], [[0, 1]], base=P, channel_multiplier=-1,
                          allow_small_or_imprecise_dtypes=True).then_inc(iotas, 1)
                pool.memset(ident[:, :], 0.0).then_inc(made, 1)
                pool.memset(own_head[:, :, :], 1.0).then_inc(made, 1)
                pool.memset(bn_eps[:, :], 1e-5)
                pool.memset(minus_half[:, :], -0.5)
                pool.memset(keep[:, :], 1.0).then_inc(iotas, 1)
                pool.wait_ge(made, 3)
                pool.wait_ge(iotas, 4)
                pool.memset(keep[:, CPB - 1::CPB], 0.0)
                pool.affine_select(out=ident[:, :], in_=ident[:, :], compare_op=ALU.not_equal, fill=1.0,
                                   base=0, pattern=[[-1, P]], channel_multiplier=1)
                v = own_head[:, :, :].rearrange("p g (h e) -> p g h e", h=HPG)
                pool.affine_select(out=v, in_=v, compare_op=ALU.is_ge, fill=0.0, base=0,
                                   pattern=[[0, GROUPS], [-HD, HPG], [0, HD]], channel_multiplier=1).then_inc(made, 1)
                pool.wait_ge(made, 4)
                pool.affine_select(out=v, in_=v, compare_op=ALU.is_ge, fill=0.0, base=HD - 1,
                                   pattern=[[0, GROUPS], [HD, HPG], [0, HD]], channel_multiplier=-1)
                pool.wait_ge(decays, HEADS)
                pool.affine_select(out=decay[:, :, :], in_=decay[:, :, :], compare_op=ALU.is_ge, fill=0.0,
                                   base=0, pattern=[[0, HEADS], [1, P]], channel_multiplier=-1)

            @block.vector
            def _(dve):
                dve.wait_ge(small_in, 16 * (HPG + 3))
                dve.tensor_scalar(slope_row[:, :], slope_row[:, :], -1.0, None, ALU.mult)
                dve.tensor_scalar(slope_col[:, :], slope_col[:, :], -1.0, None, ALU.mult).then_inc(scaled, 1)
                for half in range(2):
                    dve.wait_ge(raw_in, 16 * (half + 1))
                    w = slice(2 * half, 2 * half + 2)
                    dve.tensor_copy(wq_hi[:, w, :], raw_q[:, :, :]).then_inc(w_split, 1)
                    dve.wait_ge(w_split, half + 1)
                    dve.tensor_tensor(wq_lo[:, w, :], raw_q[:, :, :], fp32(wq_hi[:, w, :]), ALU.subtract).then_inc(raw_used, 1)
                dve.wait_ge(raw_o_in, 16)
                dve.tensor_copy(wo_hi[:, :, :], raw_o[:, :, :]).then_inc(w_split, 1)
                dve.wait_ge(w_split, 3)
                dve.tensor_tensor(wo_lo[:, :, :], raw_o[:, :, :], fp32(wo_hi[:, :, :]), ALU.subtract)

        two = lambda name, shape, dt=F32: [sb(f"{name}{i}", shape, dt) for i in range(2)]
        xin = two("xin", [P, DIM])
        stats = two("stats", [P, 6])
        mean_var = two("mean_var", [P, 2])
        rstd = two("rstd", [P, 1])
        xn = two("xn", [P, DIM])
        xt_hi, xt_lo = two("xt_hi", [P, KD, P], F32R), two("xt_lo", [P, KD, P], F32R)
        qkv = two("qkv", [P, QKV])
        k_dec = two("k_dec", [P, DIM])
        q_dec = two("q_dec", [P, GROUPS, P])
        kt = two("kt", [P, GROUPS, P])
        q_wide = two("q_wide", [P, GROUPS, HPG, P])
        masked = two("masked", [P, GROUPS, HPG, P])
        state = two("state", [P, GROUPS, P])
        state_new = sb("state_new", [P, GROUPS, P])
        ot_hi, ot_lo = two("ot_hi", [P, GROUPS, P], F32R), two("ot_lo", [P, GROUPS, P], F32R)
        s_sb = two("s_sb", [P, DIM])
        ps = lambda name, shape: ctx.enter_context(nc.psum_tensor(f"l0_attn_{name}", shape, F32))
        ps_proj = [ps(f"ps_proj{i}", [P, DIM]) for i in range(2)]
        ps_turn = [ps(f"ps_turn{i}", [P, 4, P]) for i in range(2)]
        ps_score = [ps(f"ps_score{i}", [P, HPG, P]) for i in range(2)]
        ps_state = ps("ps_state", [P, GROUPS, P])
        ps_o = ps("ps_o", [P, GROUPS, P])

        x_in = [sem(f"x_in{i}") for i in range(2)]
        s_stored = [sem(f"s_stored{i}") for i in range(2)]
        zeroed, ln_step, rstd_ready, xn_ready = sem("zeroed"), sem("ln_step"), sem("rstd_ready"), sem("xn_ready")
        proj_done = sem("proj_done")
        turn_done = sem("turn_done")
        xt_hi_ready, xt_lo_ready = sem("xt_hi_ready"), sem("xt_lo_ready")
        qkv_ready, k_dec_ready, qt_ready, kt_ready, q_dec_ready = (sem(n) for n in ("qkv_ready", "k_dec_ready", "qt_ready", "kt_ready", "q_dec_ready"))
        score_done, masked_ready = sem("score_done"), sem("masked_ready")
        upd_done, st_step, state_ready = sem("upd_done"), sem("st_step"), sem("state_ready")
        o_done, ot_hi_ready, ot_lo_ready = sem("o_done"), sem("ot_hi_ready"), sem("ot_lo_ready")
        s_ready = sem("s_ready")
        block = ctx.enter_context(nc.Block())
        sched = (-2, 4, CHUNKS - 2, CHUNKS + 1)
        PQ, PK, PV, PO = range(4)
        TQ, TK, TX = range(3)

        def proj_use(t, which):
            early = 3 * t + which if isinstance(t, int) and t < 2 else 4 * t + which - 2
            if isinstance(t, int) and t >= CHUNKS:
                early = 4 * CHUNKS - 2 + (t - CHUNKS)
            return early

        def turn_use(t, which):
            if isinstance(t, int) and t < 1:
                return t + 1
            if isinstance(t, int) and t == CHUNKS - 1:
                return 2 + 3 * (t - 1) + which
            if isinstance(t, int) and t >= CHUNKS:
                return 2 + 3 * (CHUNKS - 2) + 2 * (t - CHUNKS + 1) + which
            return 3 * t - 1 + which

        def proj_bank(t, p, which):
            return (proj_use(t, which) if isinstance(t, int) else 4 * p + which - 2) % 2

        def turn_bank(t, p, which):
            return (turn_use(t, which) if isinstance(t, int) else 3 * p - 1 + which) % 2

        @block.sync
        def _(sp):
            def tick(t, p):
                c = t + 3
                if live(c, CHUNKS):
                    need(sp, xn_ready, c - 1)
                    sp.dma_start(xin[(p + 1) % 2][:, :], x_t[c]).then_inc(x_in[(p + 1) % 2], 16)
                c = t - 2
                if live(c, CHUNKS):
                    need(sp, s_ready, c + 1)
                    sp.dma_start(s_t[c], s_sb[p][:, :]).then_inc(s_stored[p], 16)
            ticks(sp, -3, 4, CHUNKS - 4, CHUNKS + 1, tick)
            for p in range(2):
                sp.wait_ge(s_stored[p], 16 * CHUNKS // 2)

        @block.gpsimd
        def _(pool):
            def tick(t, p):
                c = t + 2
                if live(c, CHUNKS):
                    b = p
                    need(pool, ln_step, 2 * c + 2)
                    pool.tensor_tensor(rstd[b][:, :], mean_var[b][:, 1:2], bn_eps[:, :], ALU.add).then_inc(rstd_ready, 1)
                    need(pool, rstd_ready, 2 * c + 1)
                    pool.tensor_tensor(rstd[b][:, :], rstd[b][:, :], minus_half[:, :], ALU.pow).then_inc(rstd_ready, 1)
                c = t
                if live(c, CHUNKS):
                    need(pool, qkv_ready, 3 * c + 2)
                    need(pool, upd_done, c - 1)
                    kh = qkv[p][:, DIM:2 * DIM].rearrange("p (h d) -> p h d", h=HEADS)
                    pool.tensor_tensor(k_dec[p][:, :].rearrange("p (h d) -> p h d", h=HEADS), kh,
                                       k_decay[:, :].rearrange("p (h a) -> p h a", a=1).to_broadcast([P, HEADS, HD]),
                                       ALU.mult).then_inc(k_dec_ready, 1)
            ticks(pool, *sched, tick)

        @block.scalar
        def _(act):
            def tick(t, p):
                c, b = t - 1, (p + 1) % 2
                if live(c, CHUNKS):
                    use = turn_use(t, TQ)
                    need(act, turn_done, use + 1)
                    need(act, zeroed, 1)
                    need(act, score_done, GROUPS * (c - 1))
                    src = ps_turn[turn_bank(t, p, TQ)]
                    for h in range(HPG):
                        r = slice(HD * h, HD * h + HD)
                        ins = act.activation(q_wide[b][r, :, h, :], src[r, :, :], ACT.Copy)
                    ins.then_inc(qt_ready, 1)
                    need(act, turn_done, use + 2)
                    act.activation(kt[b][:, :, :], ps_turn[turn_bank(t, p, TK)][:, :, :], ACT.Copy).then_inc(kt_ready, 1)
                c, b = t + 1, (p + 1) % 2
                if live(c, CHUNKS):
                    need(act, turn_done, turn_use(t, TX) + 1)
                    need(act, qkv_ready, 3 * (c - 1))
                    act.activation(xt_hi[b][:, :, :], ps_turn[turn_bank(t, p, TX)][:, :, :], ACT.Copy).then_inc(xt_hi_ready, 1)
                c, b = t - 1, (p + 1) % 2
                if live(c, CHUNKS):
                    need(act, o_done, c + 1)
                    need(act, s_ready, c - 1)
                    act.activation(ot_hi[b][:, :, :], ps_o[:, :, :], ACT.Copy).then_inc(ot_hi_ready, 1)
            ticks(act, *sched, tick)

        @block.vector
        def _(dve):
            for b in range(2):
                dve.memset(q_wide[b][:, :, :, :], 0.0)
            dve.memset(state[1][:, :, :], 0.0)
            dve.memset(state[0][:, :, :], 0.0).then_inc(zeroed, 1)

            def evacuate(t, p, which):
                need(dve, proj_done, proj_use(t, which) + 1)
                if which == PV:
                    need(dve, o_done, t - 1)
                cols = slice(DIM * which, DIM * which + DIM)
                dve.tensor_tensor(qkv[p][:, cols], ps_proj[proj_bank(t, p, which)][:, :], bias[:, cols],
                                  ALU.add).then_inc(qkv_ready, 1)

            def tick(t, p):
                if live(t, CHUNKS):
                    evacuate(t, p, PQ)
                c, b = t - 1, (p + 1) % 2
                if live(c, CHUNKS):
                    need(dve, qt_ready, c + 1)
                    need(dve, o_done, c - 1)
                    dve.tensor_tensor(q_dec[b][:, :, :], ps_turn[turn_bank(t, p, TQ)][:, :, :], q_decay[:, :, :],
                                      ALU.mult).then_inc(q_dec_ready, 1)
                c = t + 2
                if live(c, CHUNKS):
                    need(dve, x_in[p], 8 * (c - p) + 16)
                    dve.bn_stats(stats[p][:, :], xin[p][:, :]).then_inc(ln_step, 1)
                    need(dve, ln_step, 2 * c + 1)
                if live(t, CHUNKS):
                    need(dve, k_dec_ready, t - 1)
                    evacuate(t, p, PK)
                if live(c, CHUNKS):
                    dve.bn_aggr(mean_var[p][:, :], stats[p][:, :]).then_inc(ln_step, 1)
                c = t + 1
                if live(c, CHUNKS):
                    need(dve, xt_hi_ready, c + 1)
                    dve.tensor_tensor(xt_lo[(p + 1) % 2][:, :, :], ps_turn[turn_bank(t, p, TX)][:, :, :],
                                      fp32(xt_hi[(p + 1) % 2][:, :, :]), ALU.subtract).then_inc(xt_lo_ready, 1)
                if live(t, CHUNKS):
                    evacuate(t, p, PV)
                c = t + 2
                if live(c, CHUNKS):
                    need(dve, rstd_ready, 2 * c + 2)
                    need(dve, ln_step, 2 * c + 2)
                    need(dve, xt_hi_ready, c - 1)
                    dve.tensor_scalar(xn[p][:, :], xin[p][:, :], mean_var[p][:, 0:1], rstd[p][:, 0:1],
                                      ALU.subtract, ALU.mult).then_inc(xn_ready, 1)
                c, b = t - 1, (p + 1) % 2
                if live(c, CHUNKS):
                    for g in range(GROUPS):
                        need(dve, score_done, GROUPS * c + g + 1)
                        dve.tensor_tensor(masked[b][:, g, :, :], ps_score[g % 2][:, :, :],
                                          decay[:, HPG * g:HPG * g + HPG, :], ALU.mult).then_inc(masked_ready, 1)
                c = t - 2
                if live(c, CHUNKS):
                    need(dve, proj_done, proj_use(t, PO) + 1)
                    need(dve, s_stored[p], 8 * (c - p))
                    dve.tensor_tensor(s_sb[p][:, :], ps_proj[proj_bank(t, p, PO)][:, :], bias_out[:, :],
                                      ALU.add).then_inc(s_ready, 1)
                c, b = t - 1, (p + 1) % 2
                if live(c, CHUNKS):
                    need(dve, upd_done, c + 1)
                    kp = keep[:, bass.ds(c, 1)] if not isinstance(c, int) else keep[:, c:c + 1]
                    dve.scalar_tensor_tensor(out=state_new[:, :, :], in0=ps_state[:, :, :], scalar=kp, in1=own_head[:, :, :],
                                             op0=ALU.mult, op1=ALU.mult).then_inc(st_step, 1)
                    need(dve, state_ready, c)
                    need(dve, o_done, c)
                    dve.scalar_tensor_tensor(out=state[1 - b][:, :, :], in0=state[b][:, :, :], scalar=kp,
                                             in1=blk_decay[:, :].rearrange("p (g a) -> p g a", a=1).to_broadcast([P, GROUPS, P]),
                                             op0=ALU.mult, op1=ALU.mult).then_inc(st_step, 1)
                    need(dve, st_step, 2 * c + 2)
                    dve.tensor_tensor(state[1 - b][:, :, :], state[1 - b][:, :, :], state_new[:, :, :],
                                      ALU.add).then_inc(state_ready, 1)
                    need(dve, ot_hi_ready, c + 1)
                    dve.tensor_tensor(ot_lo[b][:, :, :], ps_o[:, :, :], fp32(ot_hi[b][:, :, :]),
                                      ALU.subtract).then_inc(ot_lo_ready, 1)
            ticks(dve, *sched, tick)

        @block.tensor
        def _(pe):
            def turn(t, p, which, src, waits):
                use = turn_use(t, which)
                for s, n in waits:
                    need(pe, s, n)
                bank = ps_turn[turn_bank(t, p, which)]
                for k in range(4):
                    mm = pe.transpose(bank[:, k, :], src[:, k * P:(k + 1) * P], ident[:, :])
                mm.then_inc(turn_done, 1)

            def project(t, p, which):
                w = slice(DIM * which, DIM * which + DIM)
                three_pass(pe, ps_proj[proj_bank(t, p, which)][:, :],
                           lambda k: xt_hi[p][:, k, :], lambda k: xt_lo[p][:, k, :],
                           lambda k: wq_hi[:, k, w], lambda k: wq_lo[:, k, w], KD, proj_done)

            def tick(t, p):
                q = (p + 1) % 2
                if live(t, CHUNKS):
                    need(pe, xt_lo_ready, t + 1)
                    need(pe, xt_hi_ready, t + 1)
                    need(pe, qkv_ready, 3 * t - 1)
                    need(pe, qkv_ready, 3 * t)
                    need(pe, s_ready, t - 2)
                    project(t, p, PQ)
                c = t - 1
                if live(c, CHUNKS):
                    need(pe, kt_ready, c)
                    need(pe, q_dec_ready, c)
                    need(pe, xt_lo_ready, t if not isinstance(t, int) else min(t, CHUNKS))
                    turn(t, p, TQ, qkv[q][:, 0:DIM], [(qkv_ready, 3 * c + 1)])
                    if not isinstance(t, int) or t < CHUNKS:
                        need(pe, xt_lo_ready, t + 1)
                    turn(t, p, TK, qkv[q][:, DIM:2 * DIM], [(qkv_ready, 3 * c + 2)])
                if live(t, CHUNKS):
                    need(pe, s_ready, t - 2)
                    need(pe, s_ready, t - 2)
                    project(t, p, PK)
                c = t + 1
                if live(c, CHUNKS):
                    need(pe, q_dec_ready, t)
                    need(pe, qt_ready, t)
                    need(pe, xt_lo_ready, t)
                    turn(t, p, TX, xn[q], [(xn_ready, c + 1)])
                c = t - 1
                if live(c, CHUNKS):
                    need(pe, k_dec_ready, c + 1)
                    need(pe, qkv_ready, 3 * c + 3)
                    need(pe, st_step, 2 * c - 1)
                    for g in range(GROUPS):
                        gs = slice(P * g, P * g + P)
                        mm = pe.matmul(ps_state[:, g, :], k_dec[q][:, gs], qkv[q][:, 2 * DIM + P * g:2 * DIM + P * g + P],
                                       start=True, stop=True)
                    mm.then_inc(upd_done, 1)
                if live(t, CHUNKS):
                    need(pe, qkv_ready, 3 * t + 1)
                    project(t, p, PV)
                c = t - 1
                if live(c, CHUNKS):
                    need(pe, qt_ready, c + 1)
                    need(pe, kt_ready, c + 1)
                    for g in range(GROUPS):
                        need(pe, masked_ready, GROUPS * c + g - 1)
                        pe.matmul(ps_score[g % 2][:, :, :], kt[q][:, g, :], q_wide[q][:, g, :, :],
                                  start=True, stop=True).then_inc(score_done, 1)
                c = t - 2
                if live(c, CHUNKS):
                    need(pe, ot_lo_ready, c + 1)
                    need(pe, qkv_ready, 3 * t + 2) if live(t, CHUNKS) else None
                    if isinstance(t, int) and t >= CHUNKS:
                        need(pe, qkv_ready, 3 * CHUNKS)
                        need(pe, s_ready, c - 1)
                    three_pass(pe, ps_proj[proj_bank(t, p, PO)][:, :],
                               lambda k: ot_hi[p][:, k, :], lambda k: ot_lo[p][:, k, :],
                               lambda k: wo_hi[:, k, :], lambda k: wo_lo[:, k, :], KD, proj_done)
                c = t - 1
                if live(c, CHUNKS):
                    need(pe, zeroed, 1)
                    need(pe, state_ready, c)
                    need(pe, q_dec_ready, c + 1)
                    need(pe, ot_lo_ready, c)
                    need(pe, masked_ready, GROUPS * c + GROUPS)
                    for g in range(GROUPS):
                        pe.matmul(ps_o[:, g, :], state[q][:, g, :], q_dec[q][:, g, :], start=True, stop=False,
                                  skip_group_check=True)
                        for h in range(HPG):
                            v = 2 * DIM + P * g + HD * h
                            mm = pe.matmul(ps_o[HD * h:HD * h + HD, g, :], qkv[q][:, v:v + HD], masked[q][:, g, h, :],
                                           start=False, stop=(h == HPG - 1), skip_group_check=True)
                    mm.then_inc(o_done, 1)
            ticks(pe, *sched, tick)


def layer0_ffn(nc, x, s_in, w_fcT, w_projT, x1_out, xt_out):
    x_t = x.rearrange("b (c p) d -> (b c) p d", p=P)
    s_t = s_in.rearrange("(c p) d -> c p d", p=P)
    x1_t = x1_out.rearrange("(c p) d -> c p d", p=P)
    KF = FC // P
    NF = FC // DIM
    Q = 128.0
    with ExitStack() as ctx:
        sb = lambda name, shape, dt=F32: ctx.enter_context(nc.sbuf_tensor(f"l0_ffn_{name}", shape, dt))
        sem = lambda name: ctx.enter_context(nc.semaphore(f"l0_ffn_{name}"))
        t_fc = sb("t_fc", [P, KD, FC], F32R)
        t_proj = sb("t_proj", [P, KF, DIM], F32R)
        gamma_w = sb("gamma_w", [P, 2])
        ident = sb("ident", [P, P])
        eps5, eps6, minus_half, minus_one = (sb(n, [P, 1]) for n in ("eps5", "eps6", "minus_half", "minus_one"))

        with ExitStack() as prep:
            psb = lambda name, shape, dt=F32: prep.enter_context(nc.sbuf_tensor(f"l0_ffn_{name}", shape, dt))
            psem = lambda name: prep.enter_context(nc.semaphore(f"l0_ffn_{name}"))
            raws = [psb("raw_fc", [P, KD, FC]), psb("raw_proj", [P, KF, DIM])]
            parts = psb("parts", [P, 2, KF])
            sums = psb("sums", [P, 2])
            ones = psb("ones", [P, P])
            limit = psb("limit", [P, 2, 2])
            ps_sum = prep.enter_context(nc.psum_tensor("ps_sum", [P, 2], F32))
            raw_in = [psem("raw_fc_in"), psem("raw_proj_in")]
            made, w_step, total_done = psem("made"), psem("w_step"), psem("total_done")
            block = prep.enter_context(nc.Block())

            @block.sync
            def _(sp):
                sp.dma_start(raws[0][:, :, :], w_fcT.rearrange("(k p) n -> p k n", p=P)).then_inc(raw_in[0], 16)
                sp.dma_start(raws[1][:, :, :], w_projT.rearrange("(k p) n -> p k n", p=P)).then_inc(raw_in[1], 16)

            @block.gpsimd
            def _(pool):
                pool.memset(ident[:, :], 0.0).then_inc(made, 1)
                pool.memset(ones[:, :], 1.0).then_inc(made, 1)
                pool.memset(eps5[:, :], 1e-5)
                pool.memset(eps6[:, :], 1e-6)
                pool.memset(minus_half[:, :], -0.5)
                pool.memset(minus_one[:, :], -1.0)
                pool.wait_ge(made, 2)
                pool.affine_select(out=ident[:, :], in_=ident[:, :], compare_op=ALU.not_equal, fill=1.0,
                                   base=0, pattern=[[-1, P]], channel_multiplier=1)

            @block.tensor
            def _(pe):
                pe.wait_ge(made, 2)
                for m in range(2):
                    pe.wait_ge(w_step, 2 * m + 2)
                    pe.matmul(ps_sum[:, m:m + 1], ones[:, :], sums[:, m:m + 1], start=True, stop=True).then_inc(total_done, 1)

            @block.vector
            def _(dve):
                for m in range(2):
                    dve.wait_ge(raw_in[m], 16)
                    flat = raws[m][:, :, :].rearrange("p k n -> p (k n)").rearrange("p (a n) -> p a n", a=KF)
                    dve.tensor_reduce(parts[:, m, :], flat, AX.X, ALU.add, apply_absolute_value=True).then_inc(w_step, 1)
                    dve.wait_ge(w_step, 2 * m + 1)
                    dve.tensor_reduce(sums[:, m:m + 1], parts[:, m, :], AX.X, ALU.add).then_inc(w_step, 1)
                dve.wait_ge(total_done, 2)
                dve.tensor_scalar(gamma_w[:, :], ps_sum[:, :], 1.0 / (DIM * FC), None, ALU.mult).then_inc(w_step, 1)
                dve.wait_ge(w_step, 5)
                dve.tensor_scalar(limit[:, 0, :], gamma_w[:, :], 1e-6, 0.5, ALU.add, ALU.mult)
                dve.tensor_scalar(limit[:, 1, :], gamma_w[:, :], 1e-6, -0.5, ALU.add, ALU.mult).then_inc(w_step, 1)
                for m, t in enumerate((t_fc, t_proj)):
                    dve.wait_ge(w_step, 6 + m)
                    dve.tensor_scalar(t[:, :, :], raws[m][:, :, :], limit[:, 1, m:m + 1], None, ALU.is_lt).then_inc(w_step, 1)
                    dve.wait_ge(w_step, 7 + m)
                    dve.scalar_tensor_tensor(out=t[:, :, :], in0=raws[m][:, :, :], scalar=limit[:, 0, m:m + 1],
                                             in1=fp32(t[:, :, :]), op0=ALU.is_gt, op1=ALU.subtract)

        two = lambda name, shape, dt=F32: [sb(f"{name}{i}", shape, dt) for i in range(2)]
        xa = two("xa", [P, DIM])
        xn = two("xn", [P, DIM])
        xnn = two("xnn", [P, DIM])
        codes = two("codes", [P, DIM])
        ct_hi, ct_lo = two("ct_hi", [P, KD, P], F32R), two("ct_lo", [P, KD, P], F32R)
        h = two("h", [P, FC])
        hn = two("hn", [P, FC])
        ht_hi, ht_lo = two("ht_hi", [P, KF, P], F32R), two("ht_lo", [P, KF, P], F32R)
        xb, s_sb, gate = two("xb", [P, DIM]), two("s_sb", [P, DIM]), two("gate", [P, DIM])
        x1 = two("x1", [P, DIM])
        xn1 = two("xn1", [P, DIM])
        xt1 = two("xt1", [P, 2, KD, P], F32R)
        st_a, st_b, st_f = two("st_a", [P, 6]), two("st_b", [P, 6]), two("st_f", [P, 6])
        st_h = two("st_h", [P, NF, 6])
        mv_a, mv_b, mv_h, mv_f = (two(n, [P, 2]) for n in ("mv_a", "mv_b", "mv_h", "mv_f"))
        r_a, r_b, r_h, r_f = (two(n, [P, 1]) for n in ("r_a", "r_b", "r_h", "r_f"))
        nmr_h = two("nmr_h", [P, 1])
        gam1, inv1, scale1, gam2, inv2, scale2 = (two(n, [P, 1]) for n in ("gam1", "inv1", "scale1", "gam2", "inv2", "scale2"))
        ps = lambda name, shape: ctx.enter_context(nc.psum_tensor(f"l0_ffn_{name}", shape, F32))
        ps_fc = [ps(f"ps_fc{i}", [P, DIM]) for i in range(2)]
        ps_turn = [ps(f"ps_turn{i}", [P, 4, P]) for i in range(2)]
        ps_out = [ps(f"ps_out{i}", [P, DIM]) for i in range(2)]

        xa_in, xs_in, x1_stored, xt_stored = ([sem(f"{n}{i}") for i in range(2)] for n in ("xa_in", "xs_in", "x1_stored", "xt_stored"))
        ln_a, ln_b, ln_h, quant_h, last = (sem(n) for n in ("ln_a", "ln_b", "ln_h", "quant_h", "last"))
        rstd_a, rstd_b, rstd_h, rstd_f = (sem(n) for n in ("rstd_a", "rstd_b", "rstd_h", "rstd_f"))
        c_turned, ct_hi_ready, ct_lo_ready = sem("c_turned"), sem("ct_hi_ready"), sem("ct_lo_ready")
        fc_done, gelu_done, hn_ready, h_scaled, h_clipped = (sem(n) for n in ("fc_done", "gelu_done", "hn_ready", "h_scaled", "h_clipped"))
        h_turned, ht_hi_ready, ht_lo_ready = sem("h_turned"), sem("ht_hi_ready"), sem("ht_lo_ready")
        out_done, gate_ready = sem("out_done"), sem("gate_ready")
        f_turned, xt1_hi_ready, xt1_lo_ready = sem("f_turned"), sem("xt1_hi_ready"), sem("xt1_lo_ready")
        block = ctx.enter_context(nc.Block())
        A_STAT, A_MV, A_XN, A_STAT2, A_MV2, A_N = 1, 2, 3, 4, 5, 5
        B_XNN, B_GAM, B_INV, B_SCALED, B_CODES, B_SC, B_N = 1, 2, 3, 4, 5, 6, 6
        H_N = NF + 1
        G_GAM, G_RCP, G_INV, G_SC, G_N = 1, 2, 3, 4, 4
        F_MUL, F_X1, F_STAT, F_MV, F_XN, F_N = 1, 2, 3, 4, 5, 5
        sched = (-3, 6, CHUNKS - 4, CHUNKS + 3)

        @block.sync
        def _(sp):
            def tick(t, p):
                c, b = t + 4, p
                if live(c, CHUNKS):
                    need(sp, ln_a, A_N * (c - 2) + A_XN)
                    sp.dma_start(xa[b][:, :], x_t[c]).then_inc(xa_in[b], 16)
                c, b = t - 2, p
                if live(c, CHUNKS):
                    need(sp, last, F_N * (c - 2) + F_X1)
                    sp.dma_start(xb[b][:, :], x_t[c]).then_inc(xs_in[b], 16)
                    sp.dma_start(s_sb[b][:, :], s_t[c]).then_inc(xs_in[b], 16)
                c, b = t - 3, 1 - p
                if live(c, CHUNKS):
                    need(sp, last, F_N * c + F_X1)
                    sp.dma_start(x1_t[c], x1[b][:, :]).then_inc(x1_stored[b], 16)
                c, b = t - 4, p
                if live(c, CHUNKS):
                    need(sp, xt1_lo_ready, c + 1)
                    need(sp, xt1_hi_ready, c + 1)
                    sp.dma_start(xt_out[c], fp32(xt1[b][:, :, :, :]).rearrange("p h k n -> p (h k n)")).then_inc(xt_stored[b], 16)
            ticks(sp, -4, 6, CHUNKS - 4, CHUNKS + 3, tick)
            for b in range(2):
                sp.wait_ge(x1_stored[b], 8 * CHUNKS)
                sp.wait_ge(xt_stored[b], 8 * CHUNKS)

        @block.gpsimd
        def _(pool):
            def rstd(c, r, mv, eps, waits, counts, per):
                for w, n in waits:
                    need(pool, w, n)
                pool.tensor_tensor(r[:, :], mv[:, 1:2], eps[:, :], ALU.add).then_inc(counts, 1)
                need(pool, counts, per * c + 1)
                pool.tensor_tensor(r[:, :], r[:, :], minus_half[:, :], ALU.pow).then_inc(counts, 1)

            def tick(t, p):
                c, b = t - 3, 1 - p
                if live(c, CHUNKS):
                    rstd(c, r_f[b], mv_f[b], eps5, [(last, F_N * c + F_MV)], rstd_f, 2)
                c, b = t + 3, 1 - p
                if live(c, CHUNKS):
                    rstd(c, r_a[b], mv_a[b], eps5, [(ln_a, A_N * c + A_MV)], rstd_a, 2)
                    rstd(c, r_b[b], mv_b[b], eps6, [(ln_a, A_N * c + A_MV2), (ln_b, B_N * (c - 2) + B_XNN)], rstd_b, 2)
                c, b = t, p
                if live(c, CHUNKS):
                    rstd(c, r_h[b], mv_h[b], eps6, [(ln_h, H_N * c + H_N), (hn_ready, c - 1)], rstd_h, 4)
                    need(pool, rstd_h, 4 * c + 2)
                    pool.tensor_tensor(nmr_h[b][:, :], mv_h[b][:, 0:1], r_h[b][:, :], ALU.mult).then_inc(rstd_h, 1)
                    need(pool, rstd_h, 4 * c + 3)
                    pool.tensor_tensor(nmr_h[b][:, :], nmr_h[b][:, :], minus_one[:, :], ALU.mult).then_inc(rstd_h, 1)
            ticks(pool, *sched, tick)

        @block.scalar
        def _(act):
            def tick(t, p):
                c, b = t - 3, 1 - p
                if live(c, CHUNKS):
                    need(act, out_done, c + 1)
                    need(act, quant_h, G_N * c + G_SC)
                    need(act, last, F_N * (c - 2) + F_MUL)
                    act.activation(gate[b][:, :], ps_out[b][:, :], ACT.Silu, scale=scale2[b][:, 0:1]).then_inc(gate_ready, 1)
                c, b = t - 1, 1 - p
                if live(c, CHUNKS):
                    need(act, rstd_h, 4 * c + 4)
                    need(act, h_turned, NF * (c - 1))
                    act.activation(hn[b][:, :], h[b][:, :], ACT.Identity, bias=nmr_h[b][:, 0:1], scale=r_h[b][:, 0:1]).then_inc(hn_ready, 1)
                for n in range(NF):
                    if live(t, CHUNKS):
                        need(act, fc_done, NF * t + n + 1)
                        need(act, ln_b, B_N * t + B_SC)
                        need(act, hn_ready, t - 1)
                        act.activation(h[p][:, DIM * n:DIM * n + DIM], ps_fc[n % 2][:, :], ACT.Gelu,
                                       scale=scale1[p][:, 0:1]).then_inc(gelu_done, 1)
                    c = t - 2
                    if live(c, CHUNKS):
                        need(act, h_turned, NF * c + n + 1)
                        need(act, out_done, c - 1)
                        act.activation(ht_hi[p][:, 4 * n:4 * n + 4, :], ps_turn[n % 2][:, :, :], ACT.Copy).then_inc(ht_hi_ready, 1)
                c, b = t + 1, 1 - p
                if live(c, CHUNKS):
                    need(act, c_turned, c + 1)
                    need(act, fc_done, NF * (c - 1))
                    act.activation(ct_hi[b][:, :, :], ps_turn[0][:, :, :], ACT.Copy).then_inc(ct_hi_ready, 1)
                c, b = t - 1, 1 - p
                if live(c, CHUNKS):
                    need(act, quant_h, G_N * c + G_INV)
                    act.activation(hn[b][:, :], hn[b][:, :], ACT.Copy, scale=inv2[b][:, 0:1]).then_inc(h_scaled, 1)
                c, b = t - 4, p
                if live(c, CHUNKS):
                    need(act, f_turned, c + 1)
                    need(act, xt_stored[b], 8 * (c - b))
                    act.activation(xt1[b][:, 0, :, :], ps_turn[1][:, :, :], ACT.Copy).then_inc(xt1_hi_ready, 1)
            ticks(act, *sched, tick)

        @block.vector
        def _(dve):
            def tick(t, p):
                f, fb = t - 3, 1 - p
                a, ab = t + 3, 1 - p
                q, qb = t + 2, p
                if live(f, CHUNKS):
                    need(dve, gate_ready, f + 1)
                    need(dve, xs_in[fb], 16 * (f - fb) + 32)
                    dve.tensor_tensor(gate[fb][:, :], gate[fb][:, :], s_sb[fb][:, :], ALU.mult).then_inc(last, 1)
                    need(dve, last, F_N * f + F_MUL)
                    need(dve, x1_stored[fb], 8 * (f - fb))
                    dve.tensor_tensor(x1[fb][:, :], gate[fb][:, :], xb[fb][:, :], ALU.add).then_inc(last, 1)
                    need(dve, last, F_N * f + F_X1)
                    dve.bn_stats(st_f[fb][:, :], x1[fb][:, :]).then_inc(last, 1)
                if live(a, CHUNKS):
                    need(dve, xa_in[ab], 8 * (a - ab) + 16)
                    dve.bn_stats(st_a[ab][:, :], xa[ab][:, :]).then_inc(ln_a, 1)
                if live(f, CHUNKS):
                    need(dve, last, F_N * f + F_STAT)
                if live(a, CHUNKS):
                    need(dve, ln_a, A_N * a + A_STAT)
                if live(q, CHUNKS):
                    need(dve, rstd_b, 2 * q + 2)
                    need(dve, ln_b, B_N * (q - 1))
                    dve.tensor_scalar(xnn[qb][:, :], xn[qb][:, :], mv_b[qb][:, 0:1], r_b[qb][:, 0:1],
                                      ALU.subtract, ALU.mult).then_inc(ln_b, 1)
                if live(f, CHUNKS):
                    dve.bn_aggr(mv_f[fb][:, :], st_f[fb][:, :]).then_inc(last, 1)
                if live(a, CHUNKS):
                    dve.bn_aggr(mv_a[ab][:, :], st_a[ab][:, :]).then_inc(ln_a, 1)
                if live(q, CHUNKS):
                    need(dve, ln_b, B_N * q + B_XNN)
                    dve.tensor_reduce(gam1[qb][:, :], xnn[qb][:, :], AX.X, ALU.max, apply_absolute_value=True).then_inc(ln_b, 1)
                    need(dve, ln_b, B_N * q + B_GAM)
                    dve.reciprocal(inv1[qb][:, :], gam1[qb][:, :]).then_inc(ln_b, 1)
                    need(dve, ln_b, B_N * q + B_INV)
                    dve.tensor_scalar(xnn[qb][:, :], xnn[qb][:, :], inv1[qb][:, 0:1], Q, ALU.mult, ALU.mult).then_inc(ln_b, 1)
                    need(dve, ln_b, B_N * q + B_SCALED)
                    need(dve, c_turned, q - 1)
                    dve.tensor_scalar(codes[qb][:, :], xnn[qb][:, :], Q, -Q, ALU.min, ALU.max).then_inc(ln_b, 1)
                g, gb = t - 1, 1 - p
                if live(g, CHUNKS):
                    need(dve, hn_ready, g + 1)
                    dve.tensor_reduce(gam2[gb][:, :], hn[gb][:, :], AX.X, ALU.max, apply_absolute_value=True).then_inc(quant_h, 1)
                    need(dve, quant_h, G_N * g + G_GAM)
                    dve.reciprocal(inv2[gb][:, :], gam2[gb][:, :]).then_inc(quant_h, 1)
                    need(dve, quant_h, G_N * g + G_RCP)
                    dve.tensor_scalar(inv2[gb][:, :], inv2[gb][:, :], Q, None, ALU.mult).then_inc(quant_h, 1)
                    need(dve, gate_ready, g - 1)
                    dve.tensor_scalar(scale2[gb][:, :], gam2[gb][:, :], gamma_w[:, 1:2], 1.0 / Q, ALU.mult, ALU.mult).then_inc(quant_h, 1)
                for n in range(NF):
                    c = t - 2
                    if live(c, CHUNKS):
                        need(dve, ht_hi_ready, NF * c + n + 1)
                        dve.tensor_tensor(ht_lo[p][:, 4 * n:4 * n + 4, :], ps_turn[n % 2][:, :, :],
                                          fp32(ht_hi[p][:, 4 * n:4 * n + 4, :]), ALU.subtract).then_inc(ht_lo_ready, 1)
                    if live(t, CHUNKS):
                        need(dve, gelu_done, NF * t + n + 1)
                        dve.bn_stats(st_h[p][:, n, :], h[p][:, DIM * n:DIM * n + DIM]).then_inc(ln_h, 1)
                if live(a, CHUNKS):
                    need(dve, rstd_a, 2 * a + 2)
                    need(dve, ln_b, B_N * (a - 2) + B_XNN)
                    dve.tensor_scalar(xn[ab][:, :], xa[ab][:, :], mv_a[ab][:, 0:1], r_a[ab][:, 0:1],
                                      ALU.subtract, ALU.mult).then_inc(ln_a, 1)
                    need(dve, ln_a, A_N * a + A_XN)
                    dve.bn_stats(st_b[ab][:, :], xn[ab][:, :]).then_inc(ln_a, 1)
                if live(t, CHUNKS):
                    need(dve, ln_h, H_N * t + NF)
                if live(a, CHUNKS):
                    need(dve, ln_a, A_N * a + A_STAT2)
                c = t + 1
                if live(c, CHUNKS):
                    need(dve, ct_hi_ready, c + 1)
                    dve.tensor_tensor(ct_lo[1 - p][:, :, :], ps_turn[0][:, :, :], fp32(ct_hi[1 - p][:, :, :]),
                                      ALU.subtract).then_inc(ct_lo_ready, 1)
                if live(t, CHUNKS):
                    dve.bn_aggr(mv_h[p][:, :], st_h[p][:, :, :].rearrange("p n s -> p (n s)")).then_inc(ln_h, 1)
                if live(a, CHUNKS):
                    dve.bn_aggr(mv_b[ab][:, :], st_b[ab][:, :]).then_inc(ln_a, 1)
                if live(q, CHUNKS):
                    need(dve, gelu_done, NF * (q - 1))
                    dve.tensor_scalar(scale1[qb][:, :], gam1[qb][:, :], gamma_w[:, 0:1], 1.0 / Q, ALU.mult, ALU.mult).then_inc(ln_b, 1)
                if live(f, CHUNKS):
                    need(dve, rstd_f, 2 * f + 2)
                    need(dve, f_turned, f - 1)
                    dve.tensor_scalar(xn1[fb][:, :], x1[fb][:, :], mv_f[fb][:, 0:1], r_f[fb][:, 0:1],
                                      ALU.subtract, ALU.mult).then_inc(last, 1)
                if live(g, CHUNKS):
                    need(dve, h_scaled, g + 1)
                    dve.tensor_scalar(hn[gb][:, :], hn[gb][:, :], Q, -Q, ALU.min, ALU.max).then_inc(h_clipped, 1)
                c = t - 4
                if live(c, CHUNKS):
                    need(dve, xt1_hi_ready, c + 1)
                    dve.tensor_tensor(xt1[p][:, 1, :, :], ps_turn[1][:, :, :], fp32(xt1[p][:, 0, :, :]),
                                      ALU.subtract).then_inc(xt1_lo_ready, 1)
            ticks(dve, *sched, tick)

        @block.tensor
        def _(pe):
            def turn(bank, src, done):
                for k in range(4):
                    mm = pe.transpose(bank[:, k, :], src[:, k * P:(k + 1) * P], ident[:, :])
                mm.then_inc(done, 1)

            def tick(t, p):
                for n in range(NF):
                    if live(t, CHUNKS):
                        need(pe, ct_hi_ready, t + 1)
                        need(pe, ct_lo_ready, t + 1)
                        need(pe, gelu_done, NF * t + n - 1)
                        two_pass(pe, ps_fc[n % 2][:, :], lambda k: ct_hi[p][:, k, :], lambda k: ct_lo[p][:, k, :],
                                 lambda k: t_fc[:, k, DIM * n:DIM * n + DIM], range(KD), True, True).then_inc(fc_done, 1)
                    c = t - 2
                    if live(c, CHUNKS):
                        need(pe, h_clipped, c + 1)
                        if n == 0:
                            need(pe, ct_lo_ready, cap(t + 1, CHUNKS))
                        elif n == 1:
                            need(pe, xt1_lo_ready, t - 4)
                        else:
                            need(pe, ht_lo_ready, NF * c + n - 1)
                        turn(ps_turn[n % 2], hn[p][:, DIM * n:DIM * n + DIM], h_turned)
                c = t + 1
                if live(c, CHUNKS):
                    need(pe, ln_b, B_N * c + B_CODES)
                    need(pe, ct_lo_ready, c)
                    need(pe, ht_lo_ready, NF * (t - 2) + 3)
                    turn(ps_turn[0], codes[1 - p], c_turned)
                c = t - 2
                if live(c, CHUNKS):
                    need(pe, gate_ready, c - 1)
                    for n in range(NF):
                        need(pe, ht_lo_ready, NF * c + n + 1)
                        mm = two_pass(pe, ps_out[p][:, :], lambda k: ht_hi[p][:, k, :], lambda k: ht_lo[p][:, k, :],
                                      lambda k: t_proj[:, k, :], range(4 * n, 4 * n + 4), n == 0, n == NF - 1)
                    mm.then_inc(out_done, 1)
                c = t - 4
                if live(c, CHUNKS):
                    need(pe, last, F_N * c + F_XN)
                    need(pe, xt1_lo_ready, c)
                    need(pe, ht_lo_ready, NF * cap(t - 1, CHUNKS))
                    turn(ps_turn[1], xn1[p], f_turned)
            ticks(pe, *sched, tick)


def layer1_attention(nc, xt_in, wqkvT, rope_cos, rope_sin, yt_out):
    NT = BATCH * GROUPS
    G3 = 3 * P
    QB = SEQ // DIM
    UNITS = QB * 2 * CPB
    AUG = 3 * HD
    with ExitStack() as ctx:
        sb = lambda name, shape, dt=F32: ctx.enter_context(nc.sbuf_tensor(f"l1_attn_{name}", shape, dt))
        sem = lambda name: ctx.enter_context(nc.semaphore(f"l1_attn_{name}"))
        w_hi, w_lo = (sb(f"wqkv_{n}", [P, KD, GROUPS, G3], F32R) for n in ("hi", "lo"))
        cos_t, sin_t = sb("cos_t", [P, CPB, HD // 2]), sb("sin_t", [P, CPB, HD // 2])
        ident, ones = sb("ident", [P, P]), sb("ones", [P, HD])
        two = lambda name, shape, dt=F32: [sb(f"{name}{i}", shape, dt) for i in range(2)]
        q_tok, k_tok = two("q_tok", [P, HPG, P]), two("k_tok", [P, HPG, P])
        minus_max = sb("minus_max", [P, CPB, P])
        with ExitStack() as prep:
            psb = lambda name, shape, dt=F32: prep.enter_context(nc.sbuf_tensor(f"l1_attn_{name}", shape, dt))
            psem = lambda name: prep.enter_context(nc.semaphore(f"l1_attn_{name}"))
            raw = psb("raw", [P, KD, GROUPS, G3])
            raw_in, made, split, tabs_in = psem("raw_in"), psem("made"), psem("split"), psem("tabs_in")
            block = prep.enter_context(nc.Block())

            @block.sync
            def _(sp):
                sp.dma_start(raw[:, :, :, :], wqkvT.rearrange("(k p) g n -> p k g n", p=P)).then_inc(raw_in, 16)
                sp.dma_start(cos_t[:, :, :], rope_cos.rearrange("(c p) f -> p c f", p=P)).then_inc(tabs_in, 16)
                sp.dma_start(sin_t[:, :, :], rope_sin.rearrange("(c p) f -> p c f", p=P)).then_inc(tabs_in, 16)
                sp.wait_ge(tabs_in, 32)

            @block.gpsimd
            def _(pool):
                pool.memset(ident[:, :], 0.0).then_inc(made, 1)
                pool.memset(ones[:, :], 1.0)
                pool.memset(minus_max[:, :, :], 0.0)
                for b in range(2):
                    pool.memset(q_tok[b][:, :, :], 0.0)
                    pool.memset(k_tok[b][:, :, :], 0.0).then_inc(made, 1)
                pool.wait_ge(made, 3)
                for b in range(2):
                    for h in range(HPG):
                        pool.memset(k_tok[b][:, h, AUG + h:AUG + h + 1], 1.0)
                pool.affine_select(out=ident[:, :], in_=ident[:, :], compare_op=ALU.not_equal, fill=1.0,
                                   base=0, pattern=[[-1, P]], channel_multiplier=1)

            @block.vector
            def _(dve):
                dve.wait_ge(raw_in, 16)
                dve.tensor_copy(w_hi[:, :, :, :], raw[:, :, :, :]).then_inc(split, 1)
                dve.wait_ge(split, 1)
                dve.tensor_tensor(w_lo[:, :, :, :], raw[:, :, :, :], fp32(w_hi[:, :, :, :]), ALU.subtract)

        xt = two("xt", [P, 2, KD, P], F32R)
        qk = two("qk", [P, 2, HPG, HD])
        turned_part, swapped = sb("turned_part", [P, 2, HPG, HD // 2]), sb("swapped", [P, 2, HPG, HD // 2])
        q_st, k_st = two("q_st", [P, HPG, SEQ], F32R), two("k_st", [P, HPG, SEQ], F32R)
        v = two("v", [P, CPB, P])
        maxima = sb("maxima", [P, CPB, HPG, 2])
        probs = two("probs", [P, 2, DIM])
        y_sb, den, y_out = two("y_sb", [P, DIM]), two("den", [P, DIM]), two("y_out", [P, DIM])
        ps = lambda name, shape: ctx.enter_context(nc.psum_tensor(f"l1_attn_{name}", shape, F32))
        ps_work = [ps(f"ps_work{i}", [P, 4, P]) for i in range(2)]
        ps_sc = [ps(f"ps_sc{i}", [P, 2, DIM]) for i in range(2)]
        ps_y, ps_den = ps("ps_y", [P, DIM]), ps("ps_den", [P, DIM])

        xt_ld, y_stored = ([sem(f"{n}{i}") for i in range(2)] for n in ("xt_ld", "y_stored"))
        work_done, work_read = ([sem(f"{n}{i}") for i in range(2)] for n in ("work_done", "work_read"))
        qk_copied, rope_step, stacked, max_ready = (sem(n) for n in ("qk_copied", "rope_step", "stacked", "max_ready"))
        score_done, exp_done, pv_done = sem("score_done"), sem("exp_done"), sem("pv_done")
        y_copied, y_step, y_ready = sem("y_copied"), sem("y_step"), sem("y_ready")
        block = ctx.enter_context(nc.Block())

        N_MAX = CPB * HPG * 2

        def extras(u):
            out = []
            if u == 2:
                out.append(("turn", 1))
            if u < 2 * CPB and u % 2 == 0:
                out.append(("proj", u // 2))
            if 3 <= u < 2 * CPB + 2 and u % 2 == 1:
                out += [("q", (u - 3) // 2), ("k", (u - 3) // 2)]
            first = 2 * CPB + 2
            for a in range(N_MAX):
                if u == first + a * (UNITS - first) // N_MAX:
                    out.append(("max", a))
                    if a == N_MAX // 2 + 9:
                        out.append(("turn", 0))
            return out

        per_tick = [e for u in range(UNITS) for e in extras(u)]
        assert len(per_tick) % 2 == 0

        def work(m, e):
            k = per_tick.index(e)
            if isinstance(m, int) and m == 0:
                k -= (k > per_tick.index(("turn", 1)))
                return k % 2, k // 2
            k -= 1
            return k % 2, len(per_tick) // 2 * m + k // 2

        def exists(m, e):
            return live(m - 1, NT) if e == ("turn", 1) else live(m, NT)

        def par(m, p, back=0):
            return (p + back) % 2

        sched = (0, 2, NT, NT)
        LAST = 2 * CPB

        @block.sync
        def _(sp):
            def tick(m, p):
                for c in range(CPB):
                    if live(m, NT):
                        b = c % 2
                        src = sp.snap(m // GROUPS * CPB + c) if not isinstance(m, int) else m // GROUPS * CPB + c
                        need(sp, qk_copied, CPB * m + c - 1)
                        sp.dma_start(fp32(xt[b][:, :, :, :]).rearrange("p h k n -> p (h k n)"), xt_in[src]).then_inc(xt_ld[b], 16)
                    if c == 2 and live(m - 2, NT):
                        store(m - 2, 1)
                    if c == CPB - 1 and live(m - 1, NT):
                        store(m - 1, 0)

            def store(g, qb):
                four = SEQ // P // QB
                at = g // GROUPS * CPB + qb * four
                grp = g % GROUPS
                if not isinstance(g, int):
                    at, grp = sp.snap(at), sp.snap(grp)
                need(sp, y_ready, QB * g + qb + 1)
                sp.dma_start(yt_out[bass.ds(at, four), :, bass.ds(grp, 1), :].rearrange("c p a n -> p c (a n)"),
                             y_out[qb][:, :].rearrange("p (c n) -> p c n", n=P)).then_inc(y_stored[qb], 16)
            ticks(sp, *sched, tick)
            store(NT - 1, 1)
            for b in range(2):
                sp.wait_ge(y_stored[b], 16 * NT)

        @block.scalar
        def _(act):
            def copy_out(g, qb):
                need(act, pv_done, UNITS * g + LAST * (qb + 1))
                need(act, y_ready, QB * (g - 1) + qb + 1)
                half = slice(0, P // 2), slice(P // 2, P)
                act.activation(den[qb][half[0], :], ps_den[half[1], :], ACT.Copy)
                act.activation(den[qb][half[1], :], ps_den[half[0], :], ACT.Copy)
                act.activation(y_sb[qb][:, :], ps_y[:, :], ACT.Copy).then_inc(y_copied, 1)

            def tick(m, p):
                a = m - 1
                for u in range(UNITS):
                    if live(a, NT):
                        need(act, score_done, UNITS * a + u + 1)
                        need(act, pv_done, UNITS * a + u - 1)
                        act.activation(probs[u % 2][:, :, :], ps_sc[u % 2][:, :, :], ACT.Exp, scale=ATT_SCALE).then_inc(exp_done, 1)
                    if u == 0 and live(a - 1, NT):
                        copy_out(a - 1, 1)
                    if u == LAST and live(a, NT):
                        copy_out(a, 0)
                    for e in extras(u):
                        if not exists(m, e):
                            continue
                        kind, c = e
                        bank, before = work(m, e)
                        src = ps_work[bank]
                        if kind == "proj":
                            b = c % 2
                            need(act, work_done[bank], before + 1)
                            need(act, stacked, 2 * (CPB * m + c - 1))
                            act.activation(qk[b][:, :, :, :].rearrange("p a h d -> p (a h d)"), src[:, 0:2, :].rearrange("p a n -> p (a n)"), ACT.Copy).then_inc(qk_copied, 1)
                            act.activation(v[par(m, p)][:, c, :], src[:, 2, :], ACT.Copy).then_inc(work_read[bank], 1)
                        elif kind in "qk":
                            rows = slice(0, AUG) if kind == "q" else slice(0, P)
                            dst = (q_st if kind == "q" else k_st)[par(m, p)]
                            need(act, work_done[bank], before + 1)
                            act.activation(dst[rows, :, P * c:P * c + P], src[rows, :, :], ACT.Copy).then_inc(work_read[bank], 1)
                        elif kind == "turn":
                            dst = q_st[par(m, p, c)]
                            need(act, work_done[bank], before + 1)
                            for h in range(HPG):
                                ins = act.activation(dst[AUG:P, h, DIM * c:DIM * c + DIM], src[AUG:P, :, :].rearrange("p a n -> p (a n)"), ACT.Copy)
                            ins.then_inc(work_read[bank], 1)
            ticks(act, *sched, tick)
            copy_out(NT - 1, 1)

        @block.vector
        def _(dve):
            R = HD // 2
            S = 5

            def chunk(m, p, c):
                b, n = c % 2, CPB * m + c
                x = qk[b]
                sc = lambda t, lo, hi: t[:, c, lo:hi].rearrange("p (a f) -> p a f", a=1)
                flat = lambda ap: ap.rearrange("p a h d -> p (a h) d")
                need(dve, qk_copied, n + 1)
                dve.tensor_tensor(flat(turned_part[:, :, :, :]), flat(x[:, :, :, 0:R]), sc(cos_t, 0, R).to_broadcast([P, 2 * HPG, R]), ALU.mult).then_inc(rope_step, 1)
                dve.tensor_tensor(flat(swapped[:, :, :, 0:R // 2]), flat(x[:, :, :, R // 2:R]), sc(sin_t, 0, R // 2).to_broadcast([P, 2 * HPG, R // 2]), ALU.mult).then_inc(rope_step, 1)
                dve.tensor_tensor(flat(swapped[:, :, :, R // 2:R]), flat(x[:, :, :, 0:R // 2]), sc(sin_t, R // 2, R).to_broadcast([P, 2 * HPG, R // 2]), ALU.mult).then_inc(rope_step, 1)
                need(dve, rope_step, S * n + 3)
                dve.tensor_tensor(flat(x[:, :, :, 0:R]), flat(turned_part[:, :, :, :]), flat(swapped[:, :, :, :]), ALU.add).then_inc(rope_step, 1)
                need(dve, rope_step, S * n + 4)
                if not (isinstance(m, int) and m == 0 and c < 2):
                    bank, before = work(m, ("k", c - 2)) if c >= 2 else work(m - 1, ("k", CPB + c - 2))
                    need(dve, work_done[bank], before + 1)
                qs, ks = q_tok[b], k_tok[b]
                q2 = qs[:, :, 0:2 * HD].bitcast(F32R).rearrange("p h (t d) -> p h t d", t=2)
                dve.tensor_copy(q2, x[:, 0, :, :].rearrange("p h (t d) -> p h t d", t=1).to_broadcast([P, HPG, 2, HD]))
                for part in (0, 2):
                    ins = dve.tensor_copy(ks[:, :, HD * part:HD * part + HD].bitcast(F32R), x[:, 1, :, :])
                ins.then_inc(rope_step, 1)
                need(dve, rope_step, S * n + 5)
                dve.tensor_tensor(qs[:, :, 2 * HD:3 * HD].bitcast(F32R), x[:, 0, :, :], qs[:, :, 0:HD], ALU.subtract).then_inc(stacked, 1)
                dve.tensor_tensor(ks[:, :, HD:2 * HD].bitcast(F32R), x[:, 1, :, :], ks[:, :, 0:HD], ALU.subtract).then_inc(stacked, 1)

            def normalise(g, qb):
                n = QB * g + qb
                need(dve, y_copied, n + 1)
                dve.reciprocal(den[qb][:, :], den[qb][:, :]).then_inc(y_step, 1)
                need(dve, y_step, n + 1)
                need(dve, y_stored[qb], 16 * g)
                dve.tensor_tensor(y_out[qb][:, :], y_sb[qb][:, :], den[qb][:, :], ALU.mult).then_inc(y_ready, 1)

            def tick(m, p):
                for u in range(UNITS):
                    if u == 5 and live(m - 2, NT):
                        normalise(m - 2, 1)
                    if u == LAST + 4 and live(m - 1, NT):
                        normalise(m - 1, 0)
                    for e in extras(u):
                        if not exists(m, e):
                            continue
                        kind, c = e
                        if kind == "proj":
                            chunk(m, p, c)
                        elif kind == "max":
                            bank, before = work(m, e)
                            j, h, half = c // (2 * HPG), c // 2 % HPG, c % 2
                            need(dve, work_done[bank], before + 1)
                            dve.tensor_reduce(maxima[:, j, h, half:half + 1], ps_work[bank][:, :, :].rearrange("p a n -> p (a n)"),
                                              AX.X, ALU.max).then_inc(work_read[bank], 1)
                            if c % (N_MAX // QB) == N_MAX // QB - 1:
                                qb = c // (N_MAX // QB)
                                js = slice(CPB // QB * qb, CPB // QB * (qb + 1))
                                need(dve, work_read[bank], before + 1)
                                need(dve, work_read[1 - bank], work(m, ("max", c - 1))[1] + 1)
                                if not (isinstance(m, int) and m == 0):
                                    bk, bf = work(m if qb else m - 1, ("turn", qb))
                                    need(dve, work_done[bk], bf + 1)
                                dve.tensor_reduce(minus_max[:, js, AUG:AUG + HPG], maxima[:, js, :, :], AX.X, ALU.max,
                                                  negate=True).then_inc(max_ready, 1)
            ticks(dve, *sched, tick)
            normalise(NT - 1, 1)

        @block.tensor
        def _(pe):
            def pv(g, p, u):
                qb, pair, kt = u // LAST, u // CPB % 2, u % CPB
                need(pe, exp_done, UNITS * g + u + 1)
                if u % LAST == 0:
                    need(pe, y_copied, QB * g + qb)
                for i in range(2):
                    h = 2 * pair + i
                    pe.matmul(ps_y[HD * h:HD * h + HD, :], v[p][:, kt, HD * h:HD * h + HD], probs[u % 2][:, i, :],
                              start=(kt == 0), stop=(kt == CPB - 1), skip_group_check=True)
                for i in range(2):
                    h = (2 * pair + i + 2) % HPG
                    mm = pe.matmul(ps_den[HD * h:HD * h + HD, :], ones[:, :], probs[u % 2][:, i, :],
                                   start=(kt == 0), stop=(kt == CPB - 1), skip_group_check=True)
                mm.then_inc(pv_done, 1)

            def scores(g, p, u):
                qb, pair, kt = u // LAST, u // CPB % 2, u % CPB
                need(pe, exp_done, UNITS * g + u - 1)
                if u % LAST == 0:
                    m = g + 1 if qb else g
                    bank, before = work(m, ("turn", qb))
                    need(pe, work_read[bank], before + 1)
                for i in range(2):
                    h = 2 * pair + i
                    mm = pe.matmul(ps_sc[u % 2][:, i, :], k_st[p][:, h, P * kt:P * kt + P], q_st[p][:, h, DIM * qb:DIM * qb + DIM],
                                   start=True, stop=True)
                mm.then_inc(score_done, 1)

            def extra(m, p, e):
                kind, c = e
                bank, before = work(m, e)
                dst = ps_work[bank]
                need(pe, work_read[bank], before)
                if kind == "proj":
                    b, n = c % 2, CPB * m + c
                    g = m % GROUPS
                    need(pe, xt_ld[b], 16 * (CPB // 2 * m + c // 2 + 1))
                    cols = lambda w: (lambda k: w[:, k, bass.ds(g, 1), :].rearrange("p a n -> p (a n)"))
                    three_pass(pe, dst[:, 0:3, :].rearrange("p a n -> p (a n)"), lambda k: xt[b][:, 0, k, :], lambda k: xt[b][:, 1, k, :],
                               cols(w_hi), cols(w_lo), KD, work_done[bank])
                elif kind in "qk":
                    b, n = c % 2, CPB * m + c
                    need(pe, stacked, 2 * n + 2)
                    src, cols = (q_tok[b], AUG) if kind == "q" else (k_tok[b], P)
                    for h in range(HPG):
                        mm = pe.transpose(dst[0:cols, h, :], src[:, h, 0:cols], ident[:, :])
                    mm.then_inc(work_done[bank], 1)
                elif kind == "max":
                    j, h, half = c // (2 * HPG), c // 2 % HPG, c % 2
                    if c == 0:
                        for which in "qk":
                            bk, bf = work(m, (which, CPB - 1))
                            need(pe, work_read[bk], bf + 1)
                    pe.matmul(dst[:, :, :].rearrange("p a n -> p (a n)"), q_st[p][0:AUG, h, P * j:P * j + P], k_st[p][0:AUG, h, DIM * half:DIM * half + DIM],
                              start=True, stop=True).then_inc(work_done[bank], 1)
                else:
                    need(pe, max_ready, QB * (m - c) + c + 1)
                    for j in range(4):
                        mm = pe.transpose(dst[:, j, :], minus_max[:, 4 * c + j, :], ident[:, :])
                    mm.then_inc(work_done[bank], 1)

            def tick(m, p):
                q = 1 - p
                for u in range(UNITS):
                    if live(m - 1, NT):
                        scores(m - 1, q, u)
                    for e in extras(u):
                        if exists(m, e):
                            extra(m, p, e)
                    if u and live(m - 1, NT):
                        pv(m - 1, q, u - 1)
                    if u == 0 and live(m - 2, NT):
                        pv(m - 2, p, UNITS - 1)
            ticks(pe, *sched, tick)
            pv(NT - 1, (NT - 1) % 2, UNITS - 1)


def layer1_ffn(nc, x1_in, xt_in, yt_in, woT, gateT, upT, downT, s_gate, s_up, s_down, out):
    x1_t = x1_in.rearrange("(c p) d -> c p d", p=P)
    out_t = out.rearrange("b (c p) d -> (b c) p d", p=P)
    KH = HID // P
    cuts = [(0, DIM), (DIM, 2 * DIM), (2 * DIM, HID)]
    with ExitStack() as ctx:
        sb = lambda name, shape, dt=F32: ctx.enter_context(nc.sbuf_tensor(f"l1_ffn_{name}", shape, dt))
        sem = lambda name: ctx.enter_context(nc.semaphore(f"l1_ffn_{name}"))
        wo_hi, wo_lo = (sb(f"wo_{n}", [P, KD, DIM], F32R) for n in ("hi", "lo"))
        w_gu = sb("w_gu", [P, 2, KD, HID], F32R)
        w_down = sb("w_down", [P, KH, DIM], F32R)
        sc_gu = sb("sc_gu", [P, 2, HID])
        sc_down = sb("sc_down", [P, DIM])
        ident = sb("ident", [P, P])
        with ExitStack() as prep:
            psb = lambda name, shape, dt=F32: prep.enter_context(nc.sbuf_tensor(f"l1_ffn_{name}", shape, dt))
            psem = lambda name: prep.enter_context(nc.semaphore(f"l1_ffn_{name}"))
            raw_gu = psb("raw_gu", [P, 2, KD, HID], I32)
            raw_down = psb("raw_down", [P, KH, DIM], I32)
            raw_o = psb("raw_o", [P, KD, DIM])
            raw_in = [psem(f"raw_in{i}") for i in range(4)]
            made, split = psem("made"), psem("split")
            scales_in = psem("scales_in")
            block = prep.enter_context(nc.Block())

            @block.sync
            def _(sp):
                sp.dma_start(raw_gu[:, 0, :, :], gateT.rearrange("(k p) n -> p k n", p=P)).then_inc(raw_in[0], 16)
                sp.dma_start(raw_gu[:, 1, :, :], upT.rearrange("(k p) n -> p k n", p=P)).then_inc(raw_in[1], 16)
                sp.dma_start(raw_down[:, :, :], downT.rearrange("(k p) n -> p k n", p=P)).then_inc(raw_in[2], 16)
                sp.dma_start(raw_o[:, :, :], woT.rearrange("(k p) n -> p k n", p=P)).then_inc(raw_in[3], 16)
                sp.wait_ge(scales_in, 48)

            @block.scalar
            def _(act):
                act.dma_start(sc_gu[:, 0, :], s_gate.rearrange("(a n) -> a n", a=1).to_broadcast([P, HID])).then_inc(scales_in, 16)
                act.dma_start(sc_gu[:, 1, :], s_up.rearrange("(a n) -> a n", a=1).to_broadcast([P, HID])).then_inc(scales_in, 16)
                act.dma_start(sc_down[:, :], s_down.rearrange("(a n) -> a n", a=1).to_broadcast([P, DIM])).then_inc(scales_in, 16)

            @block.gpsimd
            def _(pool):
                pool.memset(ident[:, :], 0.0).then_inc(made, 1)
                pool.wait_ge(made, 1)
                pool.affine_select(out=ident[:, :], in_=ident[:, :], compare_op=ALU.not_equal, fill=1.0,
                                   base=0, pattern=[[-1, P]], channel_multiplier=1)

            @block.vector
            def _(dve):
                for i in range(2):
                    dve.wait_ge(raw_in[i], 16)
                    dve.tensor_scalar(w_gu[:, i, :, :], raw_gu[:, i, :, :], ZERO_POINT, None, ALU.subtract)
                dve.wait_ge(raw_in[2], 16)
                dve.tensor_scalar(w_down[:, :, :], raw_down[:, :, :], ZERO_POINT, None, ALU.subtract)
                dve.wait_ge(raw_in[3], 16)
                dve.tensor_copy(wo_hi[:, :, :], raw_o[:, :, :]).then_inc(split, 1)
                dve.wait_ge(split, 1)
                dve.tensor_tensor(wo_lo[:, :, :], raw_o[:, :, :], fp32(wo_hi[:, :, :]), ALU.subtract)

        two = lambda name, shape, dt=F32: [sb(f"{name}{i}", shape, dt) for i in range(2)]
        xt = two("xt", [P, 2, KD, P], F32R)
        yt = two("yt", [P, GROUPS, P])
        yt_hi, yt_lo = two("yt_hi", [P, GROUPS, P], F32R), two("yt_lo", [P, GROUPS, P], F32R)
        x1 = two("x1", [P, DIM])
        gate, up, mixed = two("gate", [P, HID]), two("up", [P, HID]), two("mixed", [P, HID])
        ht_hi, ht_lo = two("ht_hi", [P, KH, P], F32R), two("ht_lo", [P, KH, P], F32R)
        s_sb, g_sb, res = two("s_sb", [P, DIM]), two("g_sb", [P, DIM]), two("res", [P, DIM])
        ps = lambda name, shape: ctx.enter_context(nc.psum_tensor(f"l1_ffn_{name}", shape, F32))
        ps_gu = [ps(f"ps_gu{i}", [P, DIM]) for i in range(3)]
        ps_turn = [ps(f"ps_turn{i}", [P, 4, P]) for i in range(2)]
        ps_s = ps("ps_s", [P, DIM])
        ps_down = [ps(f"ps_down{i}", [P, DIM]) for i in range(2)]

        xt_ld, yt_ld, x1_ld, stored = ([sem(f"{n}{i}") for i in range(2)] for n in ("xt_ld", "yt_ld", "x1_ld", "stored"))
        yt_hi_ready, yt_lo_ready = sem("yt_hi_ready"), sem("yt_lo_ready")
        gu_done, gate_scaled, up_scaled, silu_done, mixed_ready = (sem(n) for n in ("gu_done", "gate_scaled", "up_scaled", "silu_done", "mixed_ready"))
        turned, ht_hi_ready, ht_lo_ready = sem("turned"), sem("ht_hi_ready"), sem("ht_lo_ready")
        s_done, s_ready, down_done, final, g_ready = (sem(n) for n in ("s_done", "s_ready", "down_done", "final", "g_ready"))
        block = ctx.enter_context(nc.Block())
        N = len(cuts)
        F_SCALED, F_MUL, F_ADD, F_N = 1, 2, 3, 3
        sched = (-1, 4, CHUNKS - 2, CHUNKS + 1)

        @block.sync
        def _(sp):
            def tick(t, p):
                c, b = t + 2, p
                if live(c, CHUNKS):
                    need(sp, gu_done, 2 * N * (c - 1))
                    sp.dma_start(fp32(xt[b][:, :, :, :]).rearrange("p h k n -> p (h k n)"), xt_in[c]).then_inc(xt_ld[b], 16)
                    need(sp, yt_lo_ready, c - 1)
                    sp.dma_start(yt[b][:, :, :], yt_in[c]).then_inc(yt_ld[b], 16)
                c, b = t, p
                if live(c, CHUNKS):
                    need(sp, final, F_N * (c - 1))
                    sp.dma_start(x1[b][:, :], x1_t[c]).then_inc(x1_ld[b], 16)
                c, b = t - 2, p
                if live(c, CHUNKS):
                    need(sp, final, F_N * c + F_ADD)
                    sp.dma_start(out_t[c], res[b][:, :]).then_inc(stored[b], 16)
            ticks(sp, -2, 4, CHUNKS - 2, CHUNKS + 1, tick)
            for b in range(2):
                sp.wait_ge(stored[b], 8 * CHUNKS)

        @block.gpsimd
        def _(pool):
            def tick(t, p):
                if live(t, CHUNKS):
                    for n, (lo, hi) in enumerate(cuts):
                        need(pool, silu_done, N * t + n + 1)
                        need(pool, up_scaled, N * t + n + 1)
                        need(pool, turned, N * (t - 1))
                        pool.tensor_tensor(mixed[p][:, lo:hi], gate[p][:, lo:hi], up[p][:, lo:hi], ALU.mult).then_inc(mixed_ready, 1)
            ticks(pool, *sched, tick)

        @block.scalar
        def _(act):
            def tick(t, p):
                c, b = t - 2, p
                if live(c, CHUNKS):
                    need(act, final, F_N * c + F_SCALED)
                    act.activation(g_sb[b][:, :], g_sb[b][:, :], ACT.Silu).then_inc(g_ready, 1)
                c, b = t + 1, 1 - p
                if live(c, CHUNKS):
                    need(act, yt_ld[b], 8 * (c - b) + 16)
                    need(act, s_done, c - 1)
                    act.activation(yt_hi[b][:, :, :], yt[b][:, :, :], ACT.Copy).then_inc(yt_hi_ready, 1)
                for n, (lo, hi) in enumerate(cuts):
                    if live(t, CHUNKS):
                        need(act, gate_scaled, N * t + n + 1)
                        act.activation(gate[p][:, lo:hi], gate[p][:, lo:hi], ACT.Silu).then_inc(silu_done, 1)
                    c, b = t - 1, 1 - p
                    if live(c, CHUNKS):
                        need(act, turned, N * c + n + 1)
                        need(act, down_done, c - 1)
                        act.activation(ht_hi[b][:, lo // P:hi // P, :], ps_turn[(N * b + n) % 2][:, 0:(hi - lo) // P, :], ACT.Copy).then_inc(ht_hi_ready, 1)
                if live(t, CHUNKS):
                    need(act, s_done, t + 1)
                    need(act, final, F_N * (t - 2) + F_MUL)
                    act.activation(s_sb[p][:, :], ps_s[:, :], ACT.Copy).then_inc(s_ready, 1)
            ticks(act, *sched, tick)

        @block.vector
        def _(dve):
            def tick(t, p):
                c, b = t - 2, p
                if live(c, CHUNKS):
                    need(dve, down_done, c + 1)
                    dve.tensor_tensor(g_sb[b][:, :], ps_down[b][:, :], sc_down[:, :], ALU.mult).then_inc(final, 1)
                cy, by = t + 1, 1 - p
                if live(cy, CHUNKS):
                    need(dve, yt_hi_ready, cy + 1)
                    need(dve, s_done, cy - 1)
                    dve.tensor_tensor(yt_lo[by][:, :, :], yt[by][:, :, :], fp32(yt_hi[by][:, :, :]), ALU.subtract).then_inc(yt_lo_ready, 1)
                for n, (lo, hi) in enumerate(cuts):
                    if live(t, CHUNKS):
                        if n == 0:
                            need(dve, mixed_ready, N * (t - 1))
                        need(dve, gu_done, 2 * (N * t + n) + 1)
                        dve.tensor_tensor(gate[p][:, lo:hi], ps_gu[2 * n % 3][:, 0:hi - lo], sc_gu[:, 0, lo:hi], ALU.mult).then_inc(gate_scaled, 1)
                        need(dve, gu_done, 2 * (N * t + n) + 2)
                        dve.tensor_tensor(up[p][:, lo:hi], ps_gu[(2 * n + 1) % 3][:, 0:hi - lo], sc_gu[:, 1, lo:hi], ALU.mult).then_inc(up_scaled, 1)
                    ct, bt = t - 1, 1 - p
                    if live(ct, CHUNKS):
                        need(dve, ht_hi_ready, N * ct + n + 1)
                        dve.tensor_tensor(ht_lo[bt][:, lo // P:hi // P, :], ps_turn[(N * bt + n) % 2][:, 0:(hi - lo) // P, :],
                                          fp32(ht_hi[bt][:, lo // P:hi // P, :]), ALU.subtract).then_inc(ht_lo_ready, 1)
                    if live(c, CHUNKS) and n == 0:
                        need(dve, g_ready, c + 1)
                        need(dve, s_ready, c + 1)
                        dve.tensor_tensor(g_sb[b][:, :], g_sb[b][:, :], s_sb[b][:, :], ALU.mult).then_inc(final, 1)
                    if live(c, CHUNKS) and n == 1:
                        need(dve, final, F_N * c + F_MUL)
                        need(dve, x1_ld[b], 8 * (c - b) + 16)
                        need(dve, stored[b], 8 * (c - b))
                        dve.tensor_tensor(res[b][:, :], g_sb[b][:, :], x1[b][:, :], ALU.add).then_inc(final, 1)
            ticks(dve, *sched, tick)

        @block.tensor
        def _(pe):
            def tick(t, p):
                q = 1 - p
                for n, (lo, hi) in enumerate(cuts):
                    if live(t, CHUNKS):
                        need(pe, xt_ld[p], 8 * (t - p) + 16)
                        for w in range(2):
                            use = 2 * n + w - 3
                            need(pe, (gate_scaled, up_scaled)[use % 2], N * t + (use // 2) + 1)
                            two_pass(pe, ps_gu[(2 * n + w) % 3][:, 0:hi - lo], lambda k: xt[p][:, 0, k, :], lambda k: xt[p][:, 1, k, :],
                                     lambda k: w_gu[:, w, k, lo:hi], range(KD), True, True).then_inc(gu_done, 1)
                    c = t - 1
                    if live(c, CHUNKS):
                        need(pe, mixed_ready, N * c + n + 1)
                        need(pe, ht_lo_ready, N * c + n - 1)
                        for k in range(lo // P, hi // P):
                            mm = pe.transpose(ps_turn[(N * q + n) % 2][:, k - lo // P, :], mixed[q][:, k * P:(k + 1) * P], ident[:, :])
                        mm.then_inc(turned, 1)
                if live(t, CHUNKS):
                    need(pe, yt_hi_ready, t + 1)
                    need(pe, yt_lo_ready, t + 1)
                    need(pe, s_ready, t)
                    three_pass(pe, ps_s[:, :], lambda k: yt_hi[p][:, k, :], lambda k: yt_lo[p][:, k, :],
                               lambda k: wo_hi[:, k, :], lambda k: wo_lo[:, k, :], KD, s_done)
                c = t - 1
                if live(c, CHUNKS):
                    need(pe, final, F_N * (c - 2) + F_SCALED)
                    for n, (lo, hi) in enumerate(cuts):
                        need(pe, ht_lo_ready, N * c + n + 1)
                        mm = two_pass(pe, ps_down[q][:, :], lambda k: ht_hi[q][:, k, :], lambda k: ht_lo[q][:, k, :],
                                      lambda k: w_down[:, k, :], range(lo // P, hi // P), n == 0, n == N - 1)
                    mm.then_inc(down_done, 1)
            ticks(pe, *sched, tick)


def layers(nc, x, Wqkv, bqkv, Wout, bout, slopes, w_fcT, w_projT, wqkvT, rope_cos, rope_sin, woT,
           gateT, s_gate, upT, s_up, downT, s_down, out):
    dram = lambda name, shape: nc.dram_tensor(name, shape, F32, kind="Internal").ap()
    s0 = dram("s0", [TOKENS, DIM])
    x1 = dram("x1_rows", [TOKENS, DIM])
    xt = dram("xt_chunks", [CHUNKS, P, 2 * KD * P])
    yt = dram("yt_chunks", [CHUNKS, P, GROUPS, P])
    layer0_attention(nc, x, Wqkv, bqkv, Wout, bout, slopes, s0)
    layer0_ffn(nc, x, s0, w_fcT, w_projT, x1, xt)
    layer1_attention(nc, xt, wqkvT, rope_cos, rope_sin, yt)
    layer1_ffn(nc, x1, xt, yt, woT, gateT, upT, downT, s_gate, s_up, s_down, out)


def rope_tables(np):
    inv_freq = (np.float32(1.0) / np.float32(10000.0) ** (np.arange(0, HD, 2, dtype=np.float32) / np.float32(HD))).astype(np.float32)
    angle = np.arange(SEQ, dtype=np.float32)[:, None] * inv_freq[None, :]
    sign = np.where(np.arange(HD // 2) < HD // 4, -1.0, 1.0).astype(np.float32)
    return np.cos(angle), np.sin(angle) * sign


def kernel(**inputs):
    import numpy as np
    import concourse.bacc as bacc
    from concourse import mybir as mb
    from concourse.bass_utils import run_bass_kernel_spmd

    a = {name: np.asarray(value) for name, value in inputs.items()}
    turned = lambda name: np.ascontiguousarray(a[name].T)
    wqkvT = np.stack([a[f"L1_attn_{n}"].T.reshape(DIM, GROUPS, P) for n in ("wq", "wk", "wv")], 2).reshape(DIM, GROUPS, 3 * P)
    cos, sin = rope_tables(np)
    laid_out = {
        "x": a["L0_attn_x"], "Wqkv": a["L0_attn_Wqkv"], "bqkv": a["L0_attn_bqkv"], "Wout": a["L0_attn_Wout"],
        "bout": a["L0_attn_bout"], "slopes": a["L0_attn_slopes"], "w_fcT": turned("L0_ffn_w_fc"),
        "w_projT": turned("L0_ffn_w_proj"), "wqkvT": wqkvT, "rope_cos": cos, "rope_sin": sin,
        "woT": turned("L1_attn_wo"), "gateT": turned("L1_ffn_wq_gate"), "s_gate": a["L1_ffn_s_gate"],
        "upT": turned("L1_ffn_wq_up"), "s_up": a["L1_ffn_s_up"], "downT": turned("L1_ffn_wq_down"),
        "s_down": a["L1_ffn_s_down"]}
    nc = bacc.Bacc("TRN2", target_bir_lowering=False, num_devices=1)
    arrays, args = {}, []
    for name, value in laid_out.items():
        arrays[f"in_{name}"] = np.ascontiguousarray(value)
        args.append(nc.dram_tensor(f"in_{name}", value.shape, mb.dt.from_np(value.dtype), kind="ExternalInput").ap())
    out = nc.dram_tensor("out_x", (BATCH, SEQ, DIM), mb.dt.float32, kind="ExternalOutput").ap()
    layers(nc, *args, out)
    result = run_bass_kernel_spmd(nc, [arrays], core_ids=[0])
    return result.results[0]["out_x"]
```

```python
import concourse.bass as bass
from concourse import mybir
from contextlib import ExitStack

F32 = mybir.dt.float32
F32R = mybir.dt.float32r
I32 = mybir.dt.int32
ALU = mybir.AluOpType
ACT = mybir.ActivationFunctionType
AX = mybir.AxisListType

P = 128
BATCH, SEQ, DIM, HEADS = 4, 1024, 512, 16
HD = DIM // HEADS
TOKENS = BATCH * SEQ
CHUNKS = TOKENS // P
CPB = SEQ // P
KD = DIM // P
HPG = P // HD
GROUPS = HEADS // HPG
FC = 4 * DIM
HID = 1408
ZERO_POINT = 128.0
ATT_SCALE = HD ** -0.5


def need(eng, sem, count):
    if isinstance(count, int) and count <= 0:
        return
    eng.wait_ge(sem, count)


def live(c, n):
    return not isinstance(c, int) or 0 <= c < n


def ticks(eng, first, loop_from, loop_to, last, tick):
    for t in range(first, loop_from):
        tick(t, t % 2)
    with eng.Fori(0, (loop_to - loop_from) // 2) as i:
        for p in range(2):
            tick(2 * i + (loop_from + p), (loop_from + p) % 2)
    for t in range(loop_to, last + 1):
        tick(t, t % 2)


def fp32(ap):
    return ap.bitcast(F32)


def three_pass(pe, out, a_hi, a_lo, w_hi, w_lo, slices, bank_done):
    n = 0
    for k in range(slices):
        for a, w in ((a_hi, w_hi), (a_lo, w_hi), (a_hi, w_lo)):
            mm = pe.matmul(out, a(k), w(k), start=(n == 0), stop=(n == 3 * slices - 1))
            n += 1
    mm.then_inc(bank_done, 1)


def two_pass(pe, out, a_hi, a_lo, w, ks, first, last):
    for k in ks:
        for n, a in enumerate((a_hi, a_lo)):
            mm = pe.matmul(out, a(k), w(k), start=(first and k == ks[0] and n == 0),
                           stop=(last and k == ks[-1] and n == 1))
    return mm


def cap(count, most):
    return min(count, most) if isinstance(count, int) else count


def layer0_attention(nc, x, Wqkv, bqkv, Wout, bout, slopes, s_out):
    x_t = x.rearrange("b (c p) d -> (b c) p d", p=P)
    s_t = s_out.rearrange("(c p) d -> c p d", p=P)
    QKV = 3 * DIM
    with ExitStack() as ctx:
        sb = lambda name, shape, dt=F32: ctx.enter_context(nc.sbuf_tensor(f"l0_attn_{name}", shape, dt))
        sem = lambda name: ctx.enter_context(nc.semaphore(f"l0_attn_{name}"))
        wq_hi, wq_lo = (sb(f"wqkv_{n}", [P, KD, QKV], F32R) for n in ("hi", "lo"))
        wo_hi, wo_lo = (sb(f"wout_{n}", [P, KD, DIM], F32R) for n in ("hi", "lo"))
        bias = sb("bias", [P, QKV])
        bias_out = sb("bias_out", [P, DIM])
        ident = sb("ident", [P, P])
        decay = sb("decay", [P, HEADS, P])
        q_decay = sb("q_decay", [P, GROUPS, P])
        k_decay = sb("k_decay", [P, HEADS])
        blk_decay = sb("blk_decay", [P, GROUPS])
        own_head = sb("own_head", [P, GROUPS, P])
        keep = sb("keep", [P, CHUNKS])
        bn_eps = sb("ln_eps", [P, 1])
        minus_half = sb("minus_half", [P, 1])

        with ExitStack() as prep:
            psb = lambda name, shape, dt=F32: prep.enter_context(nc.sbuf_tensor(f"l0_attn_{name}", shape, dt))
            raw_q = psb("raw_q", [P, 2, QKV])
            raw_o = psb("raw_o", [P, KD, DIM])
            dist = psb("dist", [P, P])
            pos = psb("pos", [P, P])
            left = psb("left", [P, 1])
            slope_row = psb("slope_row", [P, HEADS])
            slope_col = psb("slope_col", [P, GROUPS])
            psem = lambda name: prep.enter_context(nc.semaphore(f"l0_attn_{name}"))
            raw_in, raw_o_in, small_in = psem("raw_in"), psem("raw_o_in"), psem("small_in")
            raw_used, w_split, iotas, scaled, decays = (psem(n) for n in ("raw_used", "w_split", "iotas", "scaled", "decays"))
            made = psem("made")
            block = prep.enter_context(nc.Block())
            wq_t = Wqkv.rearrange("(k p) n -> p k n", p=P)

            @block.sync
            def _(sp):
                sp.dma_start(raw_q[:, :, :], wq_t[:, 0:2, :]).then_inc(raw_in, 16)
                sp.dma_start(raw_o[:, :, :], Wout.rearrange("(k p) n -> p k n", p=P)).then_inc(raw_o_in, 16)
                sp.wait_ge(raw_used, 1)
                sp.dma_start(raw_q[:, :, :], wq_t[:, 2:4, :]).then_inc(raw_in, 16)

            @block.scalar
            def _(act):
                act.dma_start(slope_row[:, :], slopes.rearrange("(a h) -> a h", a=1).to_broadcast([P, HEADS])).then_inc(small_in, 16)
                for h in range(HPG):
                    act.dma_start(slope_col[HD * h:HD * h + HD, :],
                                  slopes.rearrange("(a g h) -> h a g", a=1, h=HPG)[h].to_broadcast([HD, GROUPS]),
                                  allow_slow_non_contiguous=True).then_inc(small_in, 16)
                act.dma_start(bias[:, :], bqkv.rearrange("(a n) -> a n", a=1).to_broadcast([P, QKV])).then_inc(small_in, 16)
                act.dma_start(bias_out[:, :], bout.rearrange("(a n) -> a n", a=1).to_broadcast([P, DIM])).then_inc(small_in, 16)
                act.wait_ge(small_in, 16 * (HPG + 3))
                act.wait_ge(iotas, 4)
                act.wait_ge(scaled, 1)
                for h in range(HEADS):
                    act.activation(decay[:, h, :], dist[:, :], ACT.Exp, scale=slope_row[:, h:h + 1]).then_inc(decays, 1)
                for g in range(GROUPS):
                    act.activation(q_decay[:, g, :], pos[:, :], ACT.Exp, scale=slope_col[:, g:g + 1]).then_inc(decays, 1)
                act.activation(k_decay[:, :], slope_row[:, :], ACT.Exp, scale=left[:, 0:1]).then_inc(decays, 1)
                act.activation(blk_decay[:, :], slope_col[:, :], ACT.Exp, scale=float(P)).then_inc(decays, 1)

            @block.gpsimd
            def _(pool):
                pool.iota(dist[:, :], [[1, P]], base=0, channel_multiplier=-1,
                          allow_small_or_imprecise_dtypes=True).then_inc(made, 1)
                pool.wait_ge(made, 1)
                pool.tensor_scalar(dist[:, :], dist[:, :], 0.0, None, ALU.max).then_inc(iotas, 1)
                pool.iota(pos[:, :], [[1, P]], base=0, channel_multiplier=0,
                          allow_small_or_imprecise_dtypes=True).then_inc(iotas, 1)
                pool.iota(left[:, :], [[0, 1]], base=P, channel_multiplier=-1,
                          allow_small_or_imprecise_dtypes=True).then_inc(iotas, 1)
                pool.memset(ident[:, :], 0.0).then_inc(made, 1)
                pool.memset(own_head[:, :, :], 1.0).then_inc(made, 1)
                pool.memset(bn_eps[:, :], 1e-5)
                pool.memset(minus_half[:, :], -0.5)
                pool.memset(keep[:, :], 1.0).then_inc(iotas, 1)
                pool.wait_ge(made, 3)
                pool.wait_ge(iotas, 4)
                pool.memset(keep[:, CPB - 1::CPB], 0.0)
                pool.affine_select(out=ident[:, :], in_=ident[:, :], compare_op=ALU.not_equal, fill=1.0,
                                   base=0, pattern=[[-1, P]], channel_multiplier=1)
                v = own_head[:, :, :].rearrange("p g (h e) -> p g h e", h=HPG)
                pool.affine_select(out=v, in_=v, compare_op=ALU.is_ge, fill=0.0, base=0,
                                   pattern=[[0, GROUPS], [-HD, HPG], [0, HD]], channel_multiplier=1).then_inc(made, 1)
                pool.wait_ge(made, 4)
                pool.affine_select(out=v, in_=v, compare_op=ALU.is_ge, fill=0.0, base=HD - 1,
                                   pattern=[[0, GROUPS], [HD, HPG], [0, HD]], channel_multiplier=-1)
                pool.wait_ge(decays, HEADS)
                pool.affine_select(out=decay[:, :, :], in_=decay[:, :, :], compare_op=ALU.is_ge, fill=0.0,
                                   base=0, pattern=[[0, HEADS], [1, P]], channel_multiplier=-1)

            @block.vector
            def _(dve):
                dve.wait_ge(small_in, 16 * (HPG + 3))
                dve.tensor_scalar(slope_row[:, :], slope_row[:, :], -1.0, None, ALU.mult)
                dve.tensor_scalar(slope_col[:, :], slope_col[:, :], -1.0, None, ALU.mult).then_inc(scaled, 1)
                for half in range(2):
                    dve.wait_ge(raw_in, 16 * (half + 1))
                    w = slice(2 * half, 2 * half + 2)
                    dve.tensor_copy(wq_hi[:, w, :], raw_q[:, :, :]).then_inc(w_split, 1)
                    dve.wait_ge(w_split, half + 1)
                    dve.tensor_tensor(wq_lo[:, w, :], raw_q[:, :, :], fp32(wq_hi[:, w, :]), ALU.subtract).then_inc(raw_used, 1)
                dve.wait_ge(raw_o_in, 16)
                dve.tensor_copy(wo_hi[:, :, :], raw_o[:, :, :]).then_inc(w_split, 1)
                dve.wait_ge(w_split, 3)
                dve.tensor_tensor(wo_lo[:, :, :], raw_o[:, :, :], fp32(wo_hi[:, :, :]), ALU.subtract)

        two = lambda name, shape, dt=F32: [sb(f"{name}{i}", shape, dt) for i in range(2)]
        xin = two("xin", [P, DIM])
        stats = two("stats", [P, 6])
        mean_var = two("mean_var", [P, 2])
        rstd = two("rstd", [P, 1])
        xn = two("xn", [P, DIM])
        xt_hi, xt_lo = two("xt_hi", [P, KD, P], F32R), two("xt_lo", [P, KD, P], F32R)
        qkv = two("qkv", [P, QKV])
        k_dec = two("k_dec", [P, DIM])
        q_dec = two("q_dec", [P, GROUPS, P])
        kt = two("kt", [P, GROUPS, P])
        q_wide = two("q_wide", [P, GROUPS, HPG, P])
        masked = two("masked", [P, GROUPS, HPG, P])
        state = two("state", [P, GROUPS, P])
        state_new = sb("state_new", [P, GROUPS, P])
        ot_hi, ot_lo = two("ot_hi", [P, GROUPS, P], F32R), two("ot_lo", [P, GROUPS, P], F32R)
        s_sb = two("s_sb", [P, DIM])
        ps = lambda name, shape: ctx.enter_context(nc.psum_tensor(f"l0_attn_{name}", shape, F32))
        ps_proj = [ps(f"ps_proj{i}", [P, DIM]) for i in range(2)]
        ps_turn = [ps(f"ps_turn{i}", [P, 4, P]) for i in range(2)]
        ps_score = [ps(f"ps_score{i}", [P, HPG, P]) for i in range(2)]
        ps_state = ps("ps_state", [P, GROUPS, P])
        ps_o = ps("ps_o", [P, GROUPS, P])

        x_in = [sem(f"x_in{i}") for i in range(2)]
        s_stored = [sem(f"s_stored{i}") for i in range(2)]
        zeroed, ln_step, rstd_ready, xn_ready = sem("zeroed"), sem("ln_step"), sem("rstd_ready"), sem("xn_ready")
        proj_done = sem("proj_done")
        turn_done = sem("turn_done")
        xt_hi_ready, xt_lo_ready = sem("xt_hi_ready"), sem("xt_lo_ready")
        qkv_ready, k_dec_ready, qt_ready, kt_ready, q_dec_ready = (sem(n) for n in ("qkv_ready", "k_dec_ready", "qt_ready", "kt_ready", "q_dec_ready"))
        score_done, masked_ready = sem("score_done"), sem("masked_ready")
        upd_done, st_step, state_ready = sem("upd_done"), sem("st_step"), sem("state_ready")
        o_done, ot_hi_ready, ot_lo_ready = sem("o_done"), sem("ot_hi_ready"), sem("ot_lo_ready")
        s_ready = sem("s_ready")
        block = ctx.enter_context(nc.Block())
        sched = (-2, 4, CHUNKS - 2, CHUNKS + 1)
        PQ, PK, PV, PO = range(4)
        TQ, TK, TX = range(3)

        def proj_use(t, which):
            early = 3 * t + which if isinstance(t, int) and t < 2 else 4 * t + which - 2
            if isinstance(t, int) and t >= CHUNKS:
                early = 4 * CHUNKS - 2 + (t - CHUNKS)
            return early

        def turn_use(t, which):
            if isinstance(t, int) and t < 1:
                return t + 1
            if isinstance(t, int) and t == CHUNKS - 1:
                return 2 + 3 * (t - 1) + which
            if isinstance(t, int) and t >= CHUNKS:
                return 2 + 3 * (CHUNKS - 2) + 2 * (t - CHUNKS + 1) + which
            return 3 * t - 1 + which

        def proj_bank(t, p, which):
            return (proj_use(t, which) if isinstance(t, int) else 4 * p + which - 2) % 2

        def turn_bank(t, p, which):
            return (turn_use(t, which) if isinstance(t, int) else 3 * p - 1 + which) % 2

        @block.sync
        def _(sp):
            def tick(t, p):
                c = t + 3
                if live(c, CHUNKS):
                    need(sp, xn_ready, c - 1)
                    sp.dma_start(xin[(p + 1) % 2][:, :], x_t[c]).then_inc(x_in[(p + 1) % 2], 16)
                c = t - 2
                if live(c, CHUNKS):
                    need(sp, s_ready, c + 1)
                    sp.dma_start(s_t[c], s_sb[p][:, :]).then_inc(s_stored[p], 16)
            ticks(sp, -3, 4, CHUNKS - 4, CHUNKS + 1, tick)
            for p in range(2):
                sp.wait_ge(s_stored[p], 16 * CHUNKS // 2)

        @block.gpsimd
        def _(pool):
            def tick(t, p):
                c = t + 2
                if live(c, CHUNKS):
                    b = p
                    need(pool, ln_step, 2 * c + 2)
                    pool.tensor_tensor(rstd[b][:, :], mean_var[b][:, 1:2], bn_eps[:, :], ALU.add).then_inc(rstd_ready, 1)
                    need(pool, rstd_ready, 2 * c + 1)
                    pool.tensor_tensor(rstd[b][:, :], rstd[b][:, :], minus_half[:, :], ALU.pow).then_inc(rstd_ready, 1)
                c = t
                if live(c, CHUNKS):
                    need(pool, qkv_ready, 3 * c + 2)
                    need(pool, upd_done, c - 1)
                    kh = qkv[p][:, DIM:2 * DIM].rearrange("p (h d) -> p h d", h=HEADS)
                    pool.tensor_tensor(k_dec[p][:, :].rearrange("p (h d) -> p h d", h=HEADS), kh,
                                       k_decay[:, :].rearrange("p (h a) -> p h a", a=1).to_broadcast([P, HEADS, HD]),
                                       ALU.mult).then_inc(k_dec_ready, 1)
            ticks(pool, *sched, tick)

        @block.scalar
        def _(act):
            def tick(t, p):
                c, b = t - 1, (p + 1) % 2
                if live(c, CHUNKS):
                    use = turn_use(t, TQ)
                    need(act, turn_done, use + 1)
                    need(act, zeroed, 1)
                    need(act, score_done, GROUPS * (c - 1))
                    src = ps_turn[turn_bank(t, p, TQ)]
                    for h in range(HPG):
                        r = slice(HD * h, HD * h + HD)
                        ins = act.activation(q_wide[b][r, :, h, :], src[r, :, :], ACT.Copy)
                    ins.then_inc(qt_ready, 1)
                    need(act, turn_done, use + 2)
                    act.activation(kt[b][:, :, :], ps_turn[turn_bank(t, p, TK)][:, :, :], ACT.Copy).then_inc(kt_ready, 1)
                c, b = t + 1, (p + 1) % 2
                if live(c, CHUNKS):
                    need(act, turn_done, turn_use(t, TX) + 1)
                    need(act, qkv_ready, 3 * (c - 1))
                    act.activation(xt_hi[b][:, :, :], ps_turn[turn_bank(t, p, TX)][:, :, :], ACT.Copy).then_inc(xt_hi_ready, 1)
                c, b = t - 1, (p + 1) % 2
                if live(c, CHUNKS):
                    need(act, o_done, c + 1)
                    need(act, s_ready, c - 1)
                    act.activation(ot_hi[b][:, :, :], ps_o[:, :, :], ACT.Copy).then_inc(ot_hi_ready, 1)
            ticks(act, *sched, tick)

        @block.vector
        def _(dve):
            for b in range(2):
                dve.memset(q_wide[b][:, :, :, :], 0.0)
            dve.memset(state[1][:, :, :], 0.0)
            dve.memset(state[0][:, :, :], 0.0).then_inc(zeroed, 1)

            def evacuate(t, p, which):
                need(dve, proj_done, proj_use(t, which) + 1)
                if which == PV:
                    need(dve, o_done, t - 1)
                cols = slice(DIM * which, DIM * which + DIM)
                dve.tensor_tensor(qkv[p][:, cols], ps_proj[proj_bank(t, p, which)][:, :], bias[:, cols],
                                  ALU.add).then_inc(qkv_ready, 1)

            def tick(t, p):
                if live(t, CHUNKS):
                    evacuate(t, p, PQ)
                c, b = t - 1, (p + 1) % 2
                if live(c, CHUNKS):
                    need(dve, qt_ready, c + 1)
                    need(dve, o_done, c - 1)
                    dve.tensor_tensor(q_dec[b][:, :, :], ps_turn[turn_bank(t, p, TQ)][:, :, :], q_decay[:, :, :],
                                      ALU.mult).then_inc(q_dec_ready, 1)
                c = t + 2
                if live(c, CHUNKS):
                    need(dve, x_in[p], 8 * (c - p) + 16)
                    dve.bn_stats(stats[p][:, :], xin[p][:, :]).then_inc(ln_step, 1)
                    need(dve, ln_step, 2 * c + 1)
                if live(t, CHUNKS):
                    need(dve, k_dec_ready, t - 1)
                    evacuate(t, p, PK)
                if live(c, CHUNKS):
                    dve.bn_aggr(mean_var[p][:, :], stats[p][:, :]).then_inc(ln_step, 1)
                c = t + 1
                if live(c, CHUNKS):
                    need(dve, xt_hi_ready, c + 1)
                    dve.tensor_tensor(xt_lo[(p + 1) % 2][:, :, :], ps_turn[turn_bank(t, p, TX)][:, :, :],
                                      fp32(xt_hi[(p + 1) % 2][:, :, :]), ALU.subtract).then_inc(xt_lo_ready, 1)
                if live(t, CHUNKS):
                    evacuate(t, p, PV)
                c = t + 2
                if live(c, CHUNKS):
                    need(dve, rstd_ready, 2 * c + 2)
                    need(dve, ln_step, 2 * c + 2)
                    need(dve, xt_hi_ready, c - 1)
                    dve.tensor_scalar(xn[p][:, :], xin[p][:, :], mean_var[p][:, 0:1], rstd[p][:, 0:1],
                                      ALU.subtract, ALU.mult).then_inc(xn_ready, 1)
                c, b = t - 1, (p + 1) % 2
                if live(c, CHUNKS):
                    for g in range(GROUPS):
                        need(dve, score_done, GROUPS * c + g + 1)
                        dve.tensor_tensor(masked[b][:, g, :, :], ps_score[g % 2][:, :, :],
                                          decay[:, HPG * g:HPG * g + HPG, :], ALU.mult).then_inc(masked_ready, 1)
                c = t - 2
                if live(c, CHUNKS):
                    need(dve, proj_done, proj_use(t, PO) + 1)
                    need(dve, s_stored[p], 8 * (c - p))
                    dve.tensor_tensor(s_sb[p][:, :], ps_proj[proj_bank(t, p, PO)][:, :], bias_out[:, :],
                                      ALU.add).then_inc(s_ready, 1)
                c, b = t - 1, (p + 1) % 2
                if live(c, CHUNKS):
                    need(dve, upd_done, c + 1)
                    kp = keep[:, bass.ds(c, 1)] if not isinstance(c, int) else keep[:, c:c + 1]
                    dve.scalar_tensor_tensor(out=state_new[:, :, :], in0=ps_state[:, :, :], scalar=kp, in1=own_head[:, :, :],
                                             op0=ALU.mult, op1=ALU.mult).then_inc(st_step, 1)
                    need(dve, state_ready, c)
                    need(dve, o_done, c)
                    dve.scalar_tensor_tensor(out=state[1 - b][:, :, :], in0=state[b][:, :, :], scalar=kp,
                                             in1=blk_decay[:, :].rearrange("p (g a) -> p g a", a=1).to_broadcast([P, GROUPS, P]),
                                             op0=ALU.mult, op1=ALU.mult).then_inc(st_step, 1)
                    need(dve, st_step, 2 * c + 2)
                    dve.tensor_tensor(state[1 - b][:, :, :], state[1 - b][:, :, :], state_new[:, :, :],
                                      ALU.add).then_inc(state_ready, 1)
                    need(dve, ot_hi_ready, c + 1)
                    dve.tensor_tensor(ot_lo[b][:, :, :], ps_o[:, :, :], fp32(ot_hi[b][:, :, :]),
                                      ALU.subtract).then_inc(ot_lo_ready, 1)
            ticks(dve, *sched, tick)

        @block.tensor
        def _(pe):
            def turn(t, p, which, src, waits):
                use = turn_use(t, which)
                for s, n in waits:
                    need(pe, s, n)
                bank = ps_turn[turn_bank(t, p, which)]
                for k in range(4):
                    mm = pe.transpose(bank[:, k, :], src[:, k * P:(k + 1) * P], ident[:, :])
                mm.then_inc(turn_done, 1)

            def project(t, p, which):
                w = slice(DIM * which, DIM * which + DIM)
                three_pass(pe, ps_proj[proj_bank(t, p, which)][:, :],
                           lambda k: xt_hi[p][:, k, :], lambda k: xt_lo[p][:, k, :],
                           lambda k: wq_hi[:, k, w], lambda k: wq_lo[:, k, w], KD, proj_done)

            def tick(t, p):
                q = (p + 1) % 2
                if live(t, CHUNKS):
                    need(pe, xt_lo_ready, t + 1)
                    need(pe, xt_hi_ready, t + 1)
                    need(pe, qkv_ready, 3 * t - 1)
                    need(pe, qkv_ready, 3 * t)
                    need(pe, s_ready, t - 2)
                    project(t, p, PQ)
                c = t - 1
                if live(c, CHUNKS):
                    need(pe, kt_ready, c)
                    need(pe, q_dec_ready, c)
                    need(pe, xt_lo_ready, t if not isinstance(t, int) else min(t, CHUNKS))
                    turn(t, p, TQ, qkv[q][:, 0:DIM], [(qkv_ready, 3 * c + 1)])
                    if not isinstance(t, int) or t < CHUNKS:
                        need(pe, xt_lo_ready, t + 1)
                    turn(t, p, TK, qkv[q][:, DIM:2 * DIM], [(qkv_ready, 3 * c + 2)])
                if live(t, CHUNKS):
                    need(pe, s_ready, t - 2)
                    need(pe, s_ready, t - 2)
                    project(t, p, PK)
                c = t + 1
                if live(c, CHUNKS):
                    need(pe, q_dec_ready, t)
                    need(pe, qt_ready, t)
                    need(pe, xt_lo_ready, t)
                    turn(t, p, TX, xn[q], [(xn_ready, c + 1)])
                c = t - 1
                if live(c, CHUNKS):
                    need(pe, k_dec_ready, c + 1)
                    need(pe, qkv_ready, 3 * c + 3)
                    need(pe, st_step, 2 * c - 1)
                    for g in range(GROUPS):
                        gs = slice(P * g, P * g + P)
                        mm = pe.matmul(ps_state[:, g, :], k_dec[q][:, gs], qkv[q][:, 2 * DIM + P * g:2 * DIM + P * g + P],
                                       start=True, stop=True)
                    mm.then_inc(upd_done, 1)
                if live(t, CHUNKS):
                    need(pe, qkv_ready, 3 * t + 1)
                    project(t, p, PV)
                c = t - 1
                if live(c, CHUNKS):
                    need(pe, qt_ready, c + 1)
                    need(pe, kt_ready, c + 1)
                    for g in range(GROUPS):
                        need(pe, masked_ready, GROUPS * c + g - 1)
                        pe.matmul(ps_score[g % 2][:, :, :], kt[q][:, g, :], q_wide[q][:, g, :, :],
                                  start=True, stop=True).then_inc(score_done, 1)
                c = t - 2
                if live(c, CHUNKS):
                    need(pe, ot_lo_ready, c + 1)
                    need(pe, qkv_ready, 3 * t + 2) if live(t, CHUNKS) else None
                    if isinstance(t, int) and t >= CHUNKS:
                        need(pe, qkv_ready, 3 * CHUNKS)
                        need(pe, s_ready, c - 1)
                    three_pass(pe, ps_proj[proj_bank(t, p, PO)][:, :],
                               lambda k: ot_hi[p][:, k, :], lambda k: ot_lo[p][:, k, :],
                               lambda k: wo_hi[:, k, :], lambda k: wo_lo[:, k, :], KD, proj_done)
                c = t - 1
                if live(c, CHUNKS):
                    need(pe, zeroed, 1)
                    need(pe, state_ready, c)
                    need(pe, q_dec_ready, c + 1)
                    need(pe, ot_lo_ready, c)
                    need(pe, masked_ready, GROUPS * c + GROUPS)
                    for g in range(GROUPS):
                        pe.matmul(ps_o[:, g, :], state[q][:, g, :], q_dec[q][:, g, :], start=True, stop=False,
                                  skip_group_check=True)
                        for h in range(HPG):
                            v = 2 * DIM + P * g + HD * h
                            mm = pe.matmul(ps_o[HD * h:HD * h + HD, g, :], qkv[q][:, v:v + HD], masked[q][:, g, h, :],
                                           start=False, stop=(h == HPG - 1), skip_group_check=True)
                    mm.then_inc(o_done, 1)
            ticks(pe, *sched, tick)


def layer0_ffn(nc, x, s_in, w_fcT, w_projT, x1_out, xt_out):
    x_t = x.rearrange("b (c p) d -> (b c) p d", p=P)
    s_t = s_in.rearrange("(c p) d -> c p d", p=P)
    x1_t = x1_out.rearrange("(c p) d -> c p d", p=P)
    KF = FC // P
    NF = FC // DIM
    Q = 128.0
    with ExitStack() as ctx:
        sb = lambda name, shape, dt=F32: ctx.enter_context(nc.sbuf_tensor(f"l0_ffn_{name}", shape, dt))
        sem = lambda name: ctx.enter_context(nc.semaphore(f"l0_ffn_{name}"))
        t_fc = sb("t_fc", [P, KD, FC], F32R)
        t_proj = sb("t_proj", [P, KF, DIM], F32R)
        gamma_w = sb("gamma_w", [P, 2])
        ident = sb("ident", [P, P])
        eps5, eps6, minus_half, minus_one = (sb(n, [P, 1]) for n in ("eps5", "eps6", "minus_half", "minus_one"))

        with ExitStack() as prep:
            psb = lambda name, shape, dt=F32: prep.enter_context(nc.sbuf_tensor(f"l0_ffn_{name}", shape, dt))
            psem = lambda name: prep.enter_context(nc.semaphore(f"l0_ffn_{name}"))
            raws = [psb("raw_fc", [P, KD, FC]), psb("raw_proj", [P, KF, DIM])]
            parts = psb("parts", [P, 2, KF])
            sums = psb("sums", [P, 2])
            ones = psb("ones", [P, P])
            limit = psb("limit", [P, 2, 2])
            ps_sum = prep.enter_context(nc.psum_tensor("ps_sum", [P, 2], F32))
            raw_in = [psem("raw_fc_in"), psem("raw_proj_in")]
            made, w_step, total_done = psem("made"), psem("w_step"), psem("total_done")
            block = prep.enter_context(nc.Block())

            @block.sync
            def _(sp):
                sp.dma_start(raws[0][:, :, :], w_fcT.rearrange("(k p) n -> p k n", p=P)).then_inc(raw_in[0], 16)
                sp.dma_start(raws[1][:, :, :], w_projT.rearrange("(k p) n -> p k n", p=P)).then_inc(raw_in[1], 16)

            @block.gpsimd
            def _(pool):
                pool.memset(ident[:, :], 0.0).then_inc(made, 1)
                pool.memset(ones[:, :], 1.0).then_inc(made, 1)
                pool.memset(eps5[:, :], 1e-5)
                pool.memset(eps6[:, :], 1e-6)
                pool.memset(minus_half[:, :], -0.5)
                pool.memset(minus_one[:, :], -1.0)
                pool.wait_ge(made, 2)
                pool.affine_select(out=ident[:, :], in_=ident[:, :], compare_op=ALU.not_equal, fill=1.0,
                                   base=0, pattern=[[-1, P]], channel_multiplier=1)

            @block.tensor
            def _(pe):
                pe.wait_ge(made, 2)
                for m in range(2):
                    pe.wait_ge(w_step, 2 * m + 2)
                    pe.matmul(ps_sum[:, m:m + 1], ones[:, :], sums[:, m:m + 1], start=True, stop=True).then_inc(total_done, 1)

            @block.vector
            def _(dve):
                for m in range(2):
                    dve.wait_ge(raw_in[m], 16)
                    flat = raws[m][:, :, :].rearrange("p k n -> p (k n)").rearrange("p (a n) -> p a n", a=KF)
                    dve.tensor_reduce(parts[:, m, :], flat, AX.X, ALU.add, apply_absolute_value=True).then_inc(w_step, 1)
                    dve.wait_ge(w_step, 2 * m + 1)
                    dve.tensor_reduce(sums[:, m:m + 1], parts[:, m, :], AX.X, ALU.add).then_inc(w_step, 1)
                dve.wait_ge(total_done, 2)
                dve.tensor_scalar(gamma_w[:, :], ps_sum[:, :], 1.0 / (DIM * FC), None, ALU.mult).then_inc(w_step, 1)
                dve.wait_ge(w_step, 5)
                dve.tensor_scalar(limit[:, 0, :], gamma_w[:, :], 1e-6, 0.5, ALU.add, ALU.mult)
                dve.tensor_scalar(limit[:, 1, :], gamma_w[:, :], 1e-6, -0.5, ALU.add, ALU.mult).then_inc(w_step, 1)
                for m, t in enumerate((t_fc, t_proj)):
                    dve.wait_ge(w_step, 6 + m)
                    dve.tensor_scalar(t[:, :, :], raws[m][:, :, :], limit[:, 1, m:m + 1], None, ALU.is_lt).then_inc(w_step, 1)
                    dve.wait_ge(w_step, 7 + m)
                    dve.scalar_tensor_tensor(out=t[:, :, :], in0=raws[m][:, :, :], scalar=limit[:, 0, m:m + 1],
                                             in1=fp32(t[:, :, :]), op0=ALU.is_gt, op1=ALU.subtract)

        two = lambda name, shape, dt=F32: [sb(f"{name}{i}", shape, dt) for i in range(2)]
        xa = two("xa", [P, DIM])
        xn = two("xn", [P, DIM])
        xnn = two("xnn", [P, DIM])
        codes = two("codes", [P, DIM])
        ct_hi, ct_lo = two("ct_hi", [P, KD, P], F32R), two("ct_lo", [P, KD, P], F32R)
        h = two("h", [P, FC])
        hn = two("hn", [P, FC])
        ht_hi, ht_lo = two("ht_hi", [P, KF, P], F32R), two("ht_lo", [P, KF, P], F32R)
        xb, s_sb, gate = two("xb", [P, DIM]), two("s_sb", [P, DIM]), two("gate", [P, DIM])
        x1 = two("x1", [P, DIM])
        xn1 = two("xn1", [P, DIM])
        xt1 = two("xt1", [P, 2, KD, P], F32R)
        st_a, st_b, st_f = two("st_a", [P, 6]), two("st_b", [P, 6]), two("st_f", [P, 6])
        st_h = two("st_h", [P, NF, 6])
        mv_a, mv_b, mv_h, mv_f = (two(n, [P, 2]) for n in ("mv_a", "mv_b", "mv_h", "mv_f"))
        r_a, r_b, r_h, r_f = (two(n, [P, 1]) for n in ("r_a", "r_b", "r_h", "r_f"))
        nmr_h = two("nmr_h", [P, 1])
        gam1, inv1, scale1, gam2, inv2, scale2 = (two(n, [P, 1]) for n in ("gam1", "inv1", "scale1", "gam2", "inv2", "scale2"))
        ps = lambda name, shape: ctx.enter_context(nc.psum_tensor(f"l0_ffn_{name}", shape, F32))
        ps_fc = [ps(f"ps_fc{i}", [P, DIM]) for i in range(2)]
        ps_turn = [ps(f"ps_turn{i}", [P, 4, P]) for i in range(2)]
        ps_out = [ps(f"ps_out{i}", [P, DIM]) for i in range(2)]

        xa_in, xs_in, x1_stored, xt_stored = ([sem(f"{n}{i}") for i in range(2)] for n in ("xa_in", "xs_in", "x1_stored", "xt_stored"))
        ln_a, ln_b, ln_h, quant_h, last = (sem(n) for n in ("ln_a", "ln_b", "ln_h", "quant_h", "last"))
        rstd_a, rstd_b, rstd_h, rstd_f = (sem(n) for n in ("rstd_a", "rstd_b", "rstd_h", "rstd_f"))
        c_turned, ct_hi_ready, ct_lo_ready = sem("c_turned"), sem("ct_hi_ready"), sem("ct_lo_ready")
        fc_done, gelu_done, hn_ready, h_scaled, h_clipped = (sem(n) for n in ("fc_done", "gelu_done", "hn_ready", "h_scaled", "h_clipped"))
        h_turned, ht_hi_ready, ht_lo_ready = sem("h_turned"), sem("ht_hi_ready"), sem("ht_lo_ready")
        out_done, gate_ready = sem("out_done"), sem("gate_ready")
        f_turned, xt1_hi_ready, xt1_lo_ready = sem("f_turned"), sem("xt1_hi_ready"), sem("xt1_lo_ready")
        block = ctx.enter_context(nc.Block())
        A_STAT, A_MV, A_XN, A_STAT2, A_MV2, A_N = 1, 2, 3, 4, 5, 5
        B_XNN, B_GAM, B_INV, B_SCALED, B_CODES, B_SC, B_N = 1, 2, 3, 4, 5, 6, 6
        H_N = NF + 1
        G_GAM, G_RCP, G_INV, G_SC, G_N = 1, 2, 3, 4, 4
        F_MUL, F_X1, F_STAT, F_MV, F_XN, F_N = 1, 2, 3, 4, 5, 5
        sched = (-3, 6, CHUNKS - 4, CHUNKS + 3)

        @block.sync
        def _(sp):
            def tick(t, p):
                c, b = t + 4, p
                if live(c, CHUNKS):
                    need(sp, ln_a, A_N * (c - 2) + A_XN)
                    sp.dma_start(xa[b][:, :], x_t[c]).then_inc(xa_in[b], 16)
                c, b = t - 2, p
                if live(c, CHUNKS):
                    need(sp, last, F_N * (c - 2) + F_X1)
                    sp.dma_start(xb[b][:, :], x_t[c]).then_inc(xs_in[b], 16)
                    sp.dma_start(s_sb[b][:, :], s_t[c]).then_inc(xs_in[b], 16)
                c, b = t - 3, 1 - p
                if live(c, CHUNKS):
                    need(sp, last, F_N * c + F_X1)
                    sp.dma_start(x1_t[c], x1[b][:, :]).then_inc(x1_stored[b], 16)
                c, b = t - 4, p
                if live(c, CHUNKS):
                    need(sp, xt1_lo_ready, c + 1)
                    need(sp, xt1_hi_ready, c + 1)
                    sp.dma_start(xt_out[c], fp32(xt1[b][:, :, :, :]).rearrange("p h k n -> p (h k n)")).then_inc(xt_stored[b], 16)
            ticks(sp, -4, 6, CHUNKS - 4, CHUNKS + 3, tick)
            for b in range(2):
                sp.wait_ge(x1_stored[b], 8 * CHUNKS)
                sp.wait_ge(xt_stored[b], 8 * CHUNKS)

        @block.gpsimd
        def _(pool):
            def rstd(c, r, mv, eps, waits, counts, per):
                for w, n in waits:
                    need(pool, w, n)
                pool.tensor_tensor(r[:, :], mv[:, 1:2], eps[:, :], ALU.add).then_inc(counts, 1)
                need(pool, counts, per * c + 1)
                pool.tensor_tensor(r[:, :], r[:, :], minus_half[:, :], ALU.pow).then_inc(counts, 1)

            def tick(t, p):
                c, b = t - 3, 1 - p
                if live(c, CHUNKS):
                    rstd(c, r_f[b], mv_f[b], eps5, [(last, F_N * c + F_MV)], rstd_f, 2)
                c, b = t + 3, 1 - p
                if live(c, CHUNKS):
                    rstd(c, r_a[b], mv_a[b], eps5, [(ln_a, A_N * c + A_MV)], rstd_a, 2)
                    rstd(c, r_b[b], mv_b[b], eps6, [(ln_a, A_N * c + A_MV2), (ln_b, B_N * (c - 2) + B_XNN)], rstd_b, 2)
                c, b = t, p
                if live(c, CHUNKS):
                    rstd(c, r_h[b], mv_h[b], eps6, [(ln_h, H_N * c + H_N), (hn_ready, c - 1)], rstd_h, 4)
                    need(pool, rstd_h, 4 * c + 2)
                    pool.tensor_tensor(nmr_h[b][:, :], mv_h[b][:, 0:1], r_h[b][:, :], ALU.mult).then_inc(rstd_h, 1)
                    need(pool, rstd_h, 4 * c + 3)
                    pool.tensor_tensor(nmr_h[b][:, :], nmr_h[b][:, :], minus_one[:, :], ALU.mult).then_inc(rstd_h, 1)
            ticks(pool, *sched, tick)

        @block.scalar
        def _(act):
            def tick(t, p):
                c, b = t - 3, 1 - p
                if live(c, CHUNKS):
                    need(act, out_done, c + 1)
                    need(act, quant_h, G_N * c + G_SC)
                    need(act, last, F_N * (c - 2) + F_MUL)
                    act.activation(gate[b][:, :], ps_out[b][:, :], ACT.Silu, scale=scale2[b][:, 0:1]).then_inc(gate_ready, 1)
                c, b = t - 1, 1 - p
                if live(c, CHUNKS):
                    need(act, rstd_h, 4 * c + 4)
                    need(act, h_turned, NF * (c - 1))
                    act.activation(hn[b][:, :], h[b][:, :], ACT.Identity, bias=nmr_h[b][:, 0:1], scale=r_h[b][:, 0:1]).then_inc(hn_ready, 1)
                for n in range(NF):
                    if live(t, CHUNKS):
                        need(act, fc_done, NF * t + n + 1)
                        need(act, ln_b, B_N * t + B_SC)
                        need(act, hn_ready, t - 1)
                        act.activation(h[p][:, DIM * n:DIM * n + DIM], ps_fc[n % 2][:, :], ACT.Gelu,
                                       scale=scale1[p][:, 0:1]).then_inc(gelu_done, 1)
                    c = t - 2
                    if live(c, CHUNKS):
                        need(act, h_turned, NF * c + n + 1)
                        need(act, out_done, c - 1)
                        act.activation(ht_hi[p][:, 4 * n:4 * n + 4, :], ps_turn[n % 2][:, :, :], ACT.Copy).then_inc(ht_hi_ready, 1)
                c, b = t + 1, 1 - p
                if live(c, CHUNKS):
                    need(act, c_turned, c + 1)
                    need(act, fc_done, NF * (c - 1))
                    act.activation(ct_hi[b][:, :, :], ps_turn[0][:, :, :], ACT.Copy).then_inc(ct_hi_ready, 1)
                c, b = t - 1, 1 - p
                if live(c, CHUNKS):
                    need(act, quant_h, G_N * c + G_INV)
                    act.activation(hn[b][:, :], hn[b][:, :], ACT.Copy, scale=inv2[b][:, 0:1]).then_inc(h_scaled, 1)
                c, b = t - 4, p
                if live(c, CHUNKS):
                    need(act, f_turned, c + 1)
                    need(act, xt_stored[b], 8 * (c - b))
                    act.activation(xt1[b][:, 0, :, :], ps_turn[1][:, :, :], ACT.Copy).then_inc(xt1_hi_ready, 1)
            ticks(act, *sched, tick)

        @block.vector
        def _(dve):
            def tick(t, p):
                f, fb = t - 3, 1 - p
                a, ab = t + 3, 1 - p
                q, qb = t + 2, p
                if live(f, CHUNKS):
                    need(dve, gate_ready, f + 1)
                    need(dve, xs_in[fb], 16 * (f - fb) + 32)
                    dve.tensor_tensor(gate[fb][:, :], gate[fb][:, :], s_sb[fb][:, :], ALU.mult).then_inc(last, 1)
                    need(dve, last, F_N * f + F_MUL)
                    need(dve, x1_stored[fb], 8 * (f - fb))
                    dve.tensor_tensor(x1[fb][:, :], gate[fb][:, :], xb[fb][:, :], ALU.add).then_inc(last, 1)
                    need(dve, last, F_N * f + F_X1)
                    dve.bn_stats(st_f[fb][:, :], x1[fb][:, :]).then_inc(last, 1)
                if live(a, CHUNKS):
                    need(dve, xa_in[ab], 8 * (a - ab) + 16)
                    dve.bn_stats(st_a[ab][:, :], xa[ab][:, :]).then_inc(ln_a, 1)
                if live(f, CHUNKS):
                    need(dve, last, F_N * f + F_STAT)
                if live(a, CHUNKS):
                    need(dve, ln_a, A_N * a + A_STAT)
                if live(q, CHUNKS):
                    need(dve, rstd_b, 2 * q + 2)
                    need(dve, ln_b, B_N * (q - 1))
                    dve.tensor_scalar(xnn[qb][:, :], xn[qb][:, :], mv_b[qb][:, 0:1], r_b[qb][:, 0:1],
                                      ALU.subtract, ALU.mult).then_inc(ln_b, 1)
                if live(f, CHUNKS):
                    dve.bn_aggr(mv_f[fb][:, :], st_f[fb][:, :]).then_inc(last, 1)
                if live(a, CHUNKS):
                    dve.bn_aggr(mv_a[ab][:, :], st_a[ab][:, :]).then_inc(ln_a, 1)
                if live(q, CHUNKS):
                    need(dve, ln_b, B_N * q + B_XNN)
                    dve.tensor_reduce(gam1[qb][:, :], xnn[qb][:, :], AX.X, ALU.max, apply_absolute_value=True).then_inc(ln_b, 1)
                    need(dve, ln_b, B_N * q + B_GAM)
                    dve.reciprocal(inv1[qb][:, :], gam1[qb][:, :]).then_inc(ln_b, 1)
                    need(dve, ln_b, B_N * q + B_INV)
                    dve.tensor_scalar(xnn[qb][:, :], xnn[qb][:, :], inv1[qb][:, 0:1], Q, ALU.mult, ALU.mult).then_inc(ln_b, 1)
                    need(dve, ln_b, B_N * q + B_SCALED)
                    need(dve, c_turned, q - 1)
                    dve.tensor_scalar(codes[qb][:, :], xnn[qb][:, :], Q, -Q, ALU.min, ALU.max).then_inc(ln_b, 1)
                g, gb = t - 1, 1 - p
                if live(g, CHUNKS):
                    need(dve, hn_ready, g + 1)
                    dve.tensor_reduce(gam2[gb][:, :], hn[gb][:, :], AX.X, ALU.max, apply_absolute_value=True).then_inc(quant_h, 1)
                    need(dve, quant_h, G_N * g + G_GAM)
                    dve.reciprocal(inv2[gb][:, :], gam2[gb][:, :]).then_inc(quant_h, 1)
                    need(dve, quant_h, G_N * g + G_RCP)
                    dve.tensor_scalar(inv2[gb][:, :], inv2[gb][:, :], Q, None, ALU.mult).then_inc(quant_h, 1)
                    need(dve, gate_ready, g - 1)
                    dve.tensor_scalar(scale2[gb][:, :], gam2[gb][:, :], gamma_w[:, 1:2], 1.0 / Q, ALU.mult, ALU.mult).then_inc(quant_h, 1)
                for n in range(NF):
                    c = t - 2
                    if live(c, CHUNKS):
                        need(dve, ht_hi_ready, NF * c + n + 1)
                        dve.tensor_tensor(ht_lo[p][:, 4 * n:4 * n + 4, :], ps_turn[n % 2][:, :, :],
                                          fp32(ht_hi[p][:, 4 * n:4 * n + 4, :]), ALU.subtract).then_inc(ht_lo_ready, 1)
                    if live(t, CHUNKS):
                        need(dve, gelu_done, NF * t + n + 1)
                        dve.bn_stats(st_h[p][:, n, :], h[p][:, DIM * n:DIM * n + DIM]).then_inc(ln_h, 1)
                if live(a, CHUNKS):
                    need(dve, rstd_a, 2 * a + 2)
                    need(dve, ln_b, B_N * (a - 2) + B_XNN)
                    dve.tensor_scalar(xn[ab][:, :], xa[ab][:, :], mv_a[ab][:, 0:1], r_a[ab][:, 0:1],
                                      ALU.subtract, ALU.mult).then_inc(ln_a, 1)
                    need(dve, ln_a, A_N * a + A_XN)
                    dve.bn_stats(st_b[ab][:, :], xn[ab][:, :]).then_inc(ln_a, 1)
                if live(t, CHUNKS):
                    need(dve, ln_h, H_N * t + NF)
                if live(a, CHUNKS):
                    need(dve, ln_a, A_N * a + A_STAT2)
                c = t + 1
                if live(c, CHUNKS):
                    need(dve, ct_hi_ready, c + 1)
                    dve.tensor_tensor(ct_lo[1 - p][:, :, :], ps_turn[0][:, :, :], fp32(ct_hi[1 - p][:, :, :]),
                                      ALU.subtract).then_inc(ct_lo_ready, 1)
                if live(t, CHUNKS):
                    dve.bn_aggr(mv_h[p][:, :], st_h[p][:, :, :].rearrange("p n s -> p (n s)")).then_inc(ln_h, 1)
                if live(a, CHUNKS):
                    dve.bn_aggr(mv_b[ab][:, :], st_b[ab][:, :]).then_inc(ln_a, 1)
                if live(q, CHUNKS):
                    need(dve, gelu_done, NF * (q - 1))
                    dve.tensor_scalar(scale1[qb][:, :], gam1[qb][:, :], gamma_w[:, 0:1], 1.0 / Q, ALU.mult, ALU.mult).then_inc(ln_b, 1)
                if live(f, CHUNKS):
                    need(dve, rstd_f, 2 * f + 2)
                    need(dve, f_turned, f - 1)
                    dve.tensor_scalar(xn1[fb][:, :], x1[fb][:, :], mv_f[fb][:, 0:1], r_f[fb][:, 0:1],
                                      ALU.subtract, ALU.mult).then_inc(last, 1)
                if live(g, CHUNKS):
                    need(dve, h_scaled, g + 1)
                    dve.tensor_scalar(hn[gb][:, :], hn[gb][:, :], Q, -Q, ALU.min, ALU.max).then_inc(h_clipped, 1)
                c = t - 4
                if live(c, CHUNKS):
                    need(dve, xt1_hi_ready, c + 1)
                    dve.tensor_tensor(xt1[p][:, 1, :, :], ps_turn[1][:, :, :], fp32(xt1[p][:, 0, :, :]),
                                      ALU.subtract).then_inc(xt1_lo_ready, 1)
            ticks(dve, *sched, tick)

        @block.tensor
        def _(pe):
            def turn(bank, src, done):
                for k in range(4):
                    mm = pe.transpose(bank[:, k, :], src[:, k * P:(k + 1) * P], ident[:, :])
                mm.then_inc(done, 1)

            def tick(t, p):
                for n in range(NF):
                    if live(t, CHUNKS):
                        need(pe, ct_hi_ready, t + 1)
                        need(pe, ct_lo_ready, t + 1)
                        need(pe, gelu_done, NF * t + n - 1)
                        two_pass(pe, ps_fc[n % 2][:, :], lambda k: ct_hi[p][:, k, :], lambda k: ct_lo[p][:, k, :],
                                 lambda k: t_fc[:, k, DIM * n:DIM * n + DIM], range(KD), True, True).then_inc(fc_done, 1)
                    c = t - 2
                    if live(c, CHUNKS):
                        need(pe, h_clipped, c + 1)
                        if n == 0:
                            need(pe, ct_lo_ready, cap(t + 1, CHUNKS))
                        elif n == 1:
                            need(pe, xt1_lo_ready, t - 4)
                        else:
                            need(pe, ht_lo_ready, NF * c + n - 1)
                        turn(ps_turn[n % 2], hn[p][:, DIM * n:DIM * n + DIM], h_turned)
                c = t + 1
                if live(c, CHUNKS):
                    need(pe, ln_b, B_N * c + B_CODES)
                    need(pe, ct_lo_ready, c)
                    need(pe, ht_lo_ready, NF * (t - 2) + 3)
                    turn(ps_turn[0], codes[1 - p], c_turned)
                c = t - 2
                if live(c, CHUNKS):
                    need(pe, gate_ready, c - 1)
                    for n in range(NF):
                        need(pe, ht_lo_ready, NF * c + n + 1)
                        mm = two_pass(pe, ps_out[p][:, :], lambda k: ht_hi[p][:, k, :], lambda k: ht_lo[p][:, k, :],
                                      lambda k: t_proj[:, k, :], range(4 * n, 4 * n + 4), n == 0, n == NF - 1)
                    mm.then_inc(out_done, 1)
                c = t - 4
                if live(c, CHUNKS):
                    need(pe, last, F_N * c + F_XN)
                    need(pe, xt1_lo_ready, c)
                    need(pe, ht_lo_ready, NF * cap(t - 1, CHUNKS))
                    turn(ps_turn[1], xn1[p], f_turned)
            ticks(pe, *sched, tick)


def layer1_attention(nc, xt_in, wqkvT, rope_cos, rope_sin, yt_out):
    NT = BATCH * GROUPS
    G3 = 3 * P
    QB = SEQ // DIM
    UNITS = QB * CPB * 2
    PVS = UNITS // 2
    LAST = 2 * CPB
    PIECES = 4
    ADDS = 2 * (CPB - 1)
    AUG = 3 * HD
    with ExitStack() as ctx:
        sb = lambda name, shape, dt=F32: ctx.enter_context(nc.sbuf_tensor(f"l1_attn_{name}", shape, dt))
        sem = lambda name: ctx.enter_context(nc.semaphore(f"l1_attn_{name}"))
        w_hi, w_lo = (sb(f"wqkv_{n}", [P, KD, GROUPS, G3], F32R) for n in ("hi", "lo"))
        cos_t, sin_t = sb("cos_t", [P, CPB, HD // 2]), sb("sin_t", [P, CPB, HD // 2])
        ident, ones = sb("ident", [P, P]), sb("ones", [P, HD])
        two = lambda name, shape, dt=F32: [sb(f"{name}{i}", shape, dt) for i in range(2)]
        q_tok, k_tok = two("q_tok", [P, HPG, P]), two("k_tok", [P, HPG, P])
        minus_max = sb("minus_max", [P, CPB, P])
        with ExitStack() as prep:
            psb = lambda name, shape, dt=F32: prep.enter_context(nc.sbuf_tensor(f"l1_attn_{name}", shape, dt))
            psem = lambda name: prep.enter_context(nc.semaphore(f"l1_attn_{name}"))
            raw = psb("raw", [P, KD, GROUPS, G3])
            raw_in, made, split, tabs_in = psem("raw_in"), psem("made"), psem("split"), psem("tabs_in")
            block = prep.enter_context(nc.Block())

            @block.sync
            def _(sp):
                sp.dma_start(raw[:, :, :, :], wqkvT.rearrange("(k p) g n -> p k g n", p=P)).then_inc(raw_in, 16)
                sp.dma_start(cos_t[:, :, :], rope_cos.rearrange("(c p) f -> p c f", p=P)).then_inc(tabs_in, 16)
                sp.dma_start(sin_t[:, :, :], rope_sin.rearrange("(c p) f -> p c f", p=P)).then_inc(tabs_in, 16)
                sp.wait_ge(tabs_in, 32)

            @block.gpsimd
            def _(pool):
                pool.memset(ident[:, :], 0.0).then_inc(made, 1)
                pool.memset(ones[:, :], 1.0)
                pool.memset(minus_max[:, :, :], 0.0)
                for b in range(2):
                    pool.memset(q_tok[b][:, :, :], 0.0)
                    pool.memset(k_tok[b][:, :, :], 0.0).then_inc(made, 1)
                pool.wait_ge(made, 3)
                for b in range(2):
                    for h in range(HPG):
                        pool.memset(k_tok[b][:, h, AUG + h:AUG + h + 1], 1.0)
                pool.affine_select(out=ident[:, :], in_=ident[:, :], compare_op=ALU.not_equal, fill=1.0,
                                   base=0, pattern=[[-1, P]], channel_multiplier=1)

            @block.vector
            def _(dve):
                dve.wait_ge(raw_in, 16)
                dve.tensor_copy(w_hi[:, :, :, :], raw[:, :, :, :]).then_inc(split, 1)
                dve.wait_ge(split, 1)
                dve.tensor_tensor(w_lo[:, :, :, :], raw[:, :, :, :], fp32(w_hi[:, :, :, :]), ALU.subtract)

        xt = two("xt", [P, 2, KD, P], F32R)
        qk = two("qk", [P, 2, HPG, HD])
        turned_part, swapped = sb("turned_part", [P, 2, HPG, HD // 2]), sb("swapped", [P, 2, HPG, HD // 2])
        q_st, k_st = two("q_st", [P, HPG, SEQ], F32R), two("k_st", [P, HPG, SEQ], F32R)
        v = two("v", [P, CPB, P])
        maxima = sb("maxima", [P, CPB, HPG, 2])
        probs = [sb(f"probs{i}", [P, 2, DIM]) for i in range(4)]
        summed = [[sb(f"summed{qb}_{pair}", [P, 2, DIM]) for pair in range(2)] for qb in range(QB)]
        den, inv_den = sb("den", [P, DIM]), sb("inv_den", [P, DIM])
        y_sb, y_out = two("y_sb", [P, DIM]), two("y_out", [P, DIM])
        ps = lambda name, shape: ctx.enter_context(nc.psum_tensor(f"l1_attn_{name}", shape, F32))
        ps_prep = ps("ps_prep", [P, 4, P])
        ps_max = [ps(f"ps_max{i}", [P, 4, P]) for i in range(2)]
        ps_sc = [ps(f"ps_sc{i}", [P, 2, DIM]) for i in range(2)]
        ps_y = ps("ps_y", [P, DIM])

        xt_ld, y_stored = ([sem(f"{n}{i}") for i in range(2)] for n in ("xt_ld", "y_stored"))
        prep_done, prep_read = sem("prep_done"), sem("prep_read")
        max_done, max_read = ([sem(f"{n}{i}") for i in range(2)] for n in ("max_done", "max_read"))
        qk_copied, rope_step, stacked, max_ready = (sem(n) for n in ("qk_copied", "rope_step", "stacked", "max_ready"))
        score_done, exp_done, pv_done = sem("score_done"), sem("exp_done"), sem("pv_done")
        added, y_copied, y_ready = sem("added"), sem("y_copied"), sem("y_ready")
        inverted = sem("inverted")
        block = ctx.enter_context(nc.Block())

        N_MAX = CPB * HPG
        PREP_STEP, PREP_AT = 4, (0, 5, 7)
        DEN_AT = [2 * (LAST + 3), 2 * 3]
        INVERT_AT = [LAST + 5, 5]
        MAX_UNITS = [(2 * CPB + 2, UNITS - 2), (0, LAST - 3)]
        TURN_UNIT = [UNITS - 1, LAST - 2]

        def preps(u):
            halves = [None] * (2 * UNITS)
            for c in range(CPB):
                for at, kind in zip(PREP_AT, ("proj", "q", "k")):
                    assert halves[PREP_STEP * c + at] is None
                    halves[PREP_STEP * c + at] = kind, c
            for qb in range(QB):
                assert halves[DEN_AT[qb]] is None
                halves[DEN_AT[qb]] = "den", qb
            return halves[2 * u:2 * u + 2]

        def maxes(u):
            out = []
            for qb in range(QB):
                lo, hi = MAX_UNITS[qb]
                for a in range(N_MAX):
                    if u == lo + a * (hi - lo) // N_MAX:
                        out.append(("max", qb * N_MAX + a))
                if u == TURN_UNIT[qb]:
                    out.append(("turn", qb))
            return out

        def back(e):
            if e[0] == "den":
                return 1 + e[1]
            return 1 if e == ("turn", 1) or e[0] == "max" and e[1] >= N_MAX else 0

        def exists(m, e):
            return e is not None and live(m - back(e), NT)

        def ring(uses, banks):
            of_tick = lambda m: [e for e in uses if exists(m, e)]
            before = lambda m: sum(len(of_tick(i)) for i in range(m))
            assert len(uses) % banks == 0

            def use(m, e):
                if isinstance(m, int):
                    n = before(m) + of_tick(m).index(e)
                    return n % banks, n // banks
                n = before(2) + uses.index(e)
                return n % banks, len(uses) // banks * (m - 2) + n // banks
            return use

        prep_use = ring([e for u in range(UNITS) for e in preps(u) if e], 1)
        max_use = ring([e for u in range(UNITS) for e in maxes(u)], 2)

        def adds_with(g, u):
            if u < 0:
                g, u = g - 1, u + UNITS
            return ADDS * (QB * g + u // LAST) + 2 * (max(u // 2 % CPB, 1) - 1) + u % 2 + 1

        sched = (0, 4, NT, NT)

        @block.sync
        def _(sp):
            def tick(m, p):
                for c in range(CPB):
                    if live(m, NT):
                        b = c % 2
                        src = sp.snap(m // GROUPS * CPB + c) if not isinstance(m, int) else m // GROUPS * CPB + c
                        need(sp, qk_copied, CPB * m + c - 1)
                        sp.dma_start(fp32(xt[b][:, :, :, :]).rearrange("p h k n -> p (h k n)"), xt_in[src]).then_inc(xt_ld[b], 16)
                if live(m - 2, NT):
                    store(m - 2, 1)
                if live(m - 1, NT):
                    store(m - 1, 0)

            def store(g, qb):
                four = SEQ // P // QB
                at = g // GROUPS * CPB + qb * four
                grp = g % GROUPS
                if not isinstance(g, int):
                    at, grp = sp.snap(at), sp.snap(grp)
                need(sp, y_ready, QB * g + qb + 1)
                sp.dma_start(yt_out[bass.ds(at, four), :, bass.ds(grp, 1), :].rearrange("c p a n -> p c (a n)"),
                             y_out[qb][:, :].rearrange("p (c n) -> p c n", n=P)).then_inc(y_stored[qb], 16)
            ticks(sp, *sched, tick)
            store(NT - 1, 1)
            for b in range(2):
                sp.wait_ge(y_stored[b], 16 * NT)

        @block.scalar
        def _(act):
            def copy_out(g, qb):
                need(act, pv_done, PVS * g + CPB * (qb + 1))
                if live(g - 1, NT):
                    need(act, y_ready, QB * (g - 1) + qb + 1)
                act.activation(y_sb[qb][:, :], ps_y[:, :], ACT.Copy).then_inc(y_copied, 1)

            def copy_den(g, qb):
                need(act, inverted, PIECES * (QB * g + qb))
                act.activation(den[:, :], ps_prep[:, :, :].rearrange("p a n -> p (a n)"), ACT.Copy).then_inc(prep_read, 1)

            def tick(m, p):
                a = m - 1
                for u in range(UNITS):
                    if live(a, NT):
                        need(act, score_done, UNITS * a + u + 1)
                        need(act, pv_done, PVS * a + u // 2 - 1)
                        if u >= 4 or live(a - 1, NT):
                            need(act, added, adds_with(a, u - 4))
                        act.activation(probs[u % 4][:, :, :], ps_sc[u % 2][:, :, :], ACT.Exp, scale=ATT_SCALE).then_inc(exp_done, 1)
                    if u == 1 and live(a - 1, NT):
                        copy_out(a - 1, 1)
                    if u == LAST + 1 and live(a, NT):
                        copy_out(a, 0)
                    for e in preps(u):
                        if not exists(m, e):
                            continue
                        kind, c = e
                        need(act, prep_done, prep_use(m, e)[1] + 1)
                        if kind == "proj":
                            need(act, stacked, 2 * (CPB * m + c - 1))
                            act.activation(qk[c % 2][:, :, :, :].rearrange("p a h d -> p (a h d)"), ps_prep[:, 0:2, :].rearrange("p a n -> p (a n)"), ACT.Copy).then_inc(qk_copied, 1)
                            act.activation(v[p][:, c, :], ps_prep[:, 2, :], ACT.Copy).then_inc(prep_read, 1)
                        elif kind == "den":
                            copy_den(m - back(e), c)
                        else:
                            rows = slice(0, AUG) if kind == "q" else slice(0, P)
                            dst = (q_st if kind == "q" else k_st)[p]
                            act.activation(dst[rows, :, P * c:P * c + P], ps_prep[rows, :, :], ACT.Copy).then_inc(prep_read, 1)
                    for e in maxes(u):
                        if e[0] == "turn" and exists(m, e):
                            qb = e[1]
                            bank, before = max_use(m, e)
                            dst = q_st[(p + back(e)) % 2]
                            need(act, max_done[bank], before + 1)
                            for h in range(HPG):
                                ins = act.activation(dst[AUG:P, h, DIM * qb:DIM * qb + DIM], ps_max[bank][AUG:P, :, :].rearrange("p a n -> p (a n)"), ACT.Copy)
                            ins.then_inc(max_read[bank], 1)
            ticks(act, *sched, tick)
            copy_out(NT - 1, 1)
            need(act, prep_done, prep_use(NT + 1, ("den", 1))[1] + 1)
            copy_den(NT - 1, 1)

        @block.gpsimd
        def _(pool):
            def tick(m, p):
                for u in range(UNITS):
                    g, kt, n = m - 1, u // 2 % CPB, adds_with(m - 1, u)
                    if kt and live(g, NT):
                        total, new = summed[u // LAST][u % 2], probs[u % 4]
                        need(pool, exp_done, UNITS * g + u + 1)
                        if kt > 1:
                            need(pool, added, n - 2)
                        elif live(g - 1, NT):
                            need(pool, prep_done, prep_use(*((m, ("den", 1)) if u >= LAST else (m - 1, ("den", 0))))[1] + 1)
                        old = probs[(u - 2) % 4] if kt == 1 else total
                        pool.tensor_tensor(total[:, :, :], old[:, :, :], new[:, :, :], ALU.add).then_inc(added, 1)
            ticks(pool, *sched, tick)

        @block.vector
        def _(dve):
            R = HD // 2
            S = 5

            def chunk(m, p, c, step):
                b, n = c % 2, CPB * m + c
                x = qk[b]
                sc = lambda t, lo, hi: t[:, c, lo:hi].rearrange("p (a f) -> p a f", a=1)
                flat = lambda ap: ap.rearrange("p a h d -> p (a h) d")
                qs, ks = q_tok[b], k_tok[b]
                if step == 0:
                    need(dve, qk_copied, n + 1)
                    dve.tensor_tensor(flat(turned_part[:, :, :, :]), flat(x[:, :, :, 0:R]), sc(cos_t, 0, R).to_broadcast([P, 2 * HPG, R]), ALU.mult).then_inc(rope_step, 1)
                    dve.tensor_tensor(flat(swapped[:, :, :, 0:R // 2]), flat(x[:, :, :, R // 2:R]), sc(sin_t, 0, R // 2).to_broadcast([P, 2 * HPG, R // 2]), ALU.mult).then_inc(rope_step, 1)
                    dve.tensor_tensor(flat(swapped[:, :, :, R // 2:R]), flat(x[:, :, :, 0:R // 2]), sc(sin_t, R // 2, R).to_broadcast([P, 2 * HPG, R // 2]), ALU.mult).then_inc(rope_step, 1)
                elif step == 1:
                    need(dve, rope_step, S * n + 3)
                    dve.tensor_tensor(flat(x[:, :, :, 0:R]), flat(turned_part[:, :, :, :]), flat(swapped[:, :, :, :]), ALU.add).then_inc(rope_step, 1)
                elif step == 2:
                    if not (isinstance(m, int) and m == 0 and c < 2):
                        use = prep_use(m, ("k", c - 2)) if c >= 2 else prep_use(m - 1, ("k", CPB + c - 2))
                        need(dve, prep_done, use[1] + 1)
                    need(dve, rope_step, S * n + 4)
                    q2 = qs[:, :, 0:2 * HD].bitcast(F32R).rearrange("p h (t d) -> p h t d", t=2)
                    dve.tensor_copy(q2, x[:, 0, :, :].rearrange("p h (t d) -> p h t d", t=1).to_broadcast([P, HPG, 2, HD]))
                    k2 = ks[:, :, 0:4 * HD].bitcast(F32R).rearrange("p h (t d) -> p h t d", t=4)[:, :, 0:3:2, :]
                    dve.tensor_copy(k2, x[:, 1, :, :].rearrange("p h (t d) -> p h t d", t=1).to_broadcast([P, HPG, 2, HD])).then_inc(rope_step, 1)
                else:
                    need(dve, rope_step, S * n + 5)
                    dve.tensor_tensor(qs[:, :, 2 * HD:3 * HD].bitcast(F32R), x[:, 0, :, :], qs[:, :, 0:HD], ALU.subtract).then_inc(stacked, 1)
                    dve.tensor_tensor(ks[:, :, HD:2 * HD].bitcast(F32R), x[:, 1, :, :], ks[:, :, 0:HD], ALU.subtract).then_inc(stacked, 1)

            def normalise(g, qb, step):
                if step < PIECES:
                    cols = slice(DIM // PIECES * step, DIM // PIECES * (step + 1))
                    need(dve, prep_read, prep_use(g + 1 + qb, ("den", qb))[1] + 1)
                    need(dve, y_ready, QB * g + qb)
                    dve.reciprocal(inv_den[:, cols], den[:, cols]).then_inc(inverted, 1)
                    return
                need(dve, y_copied, QB * g + qb + 1)
                need(dve, inverted, PIECES * (QB * g + qb + 1))
                need(dve, y_stored[qb], 16 * g)
                dve.tensor_tensor(y_out[qb][:, :], y_sb[qb][:, :], inv_den[:, :], ALU.mult).then_inc(y_ready, 1)

            def maximum(m, c):
                bank, before = max_use(m, ("max", c))
                j, h, half = c // (2 * HPG), c // 2 % HPG, c % 2
                need(dve, max_done[bank], before + 1)
                dve.tensor_reduce(maxima[:, j, h, half:half + 1], ps_max[bank][:, :, :].rearrange("p a n -> p (a n)"),
                                  AX.X, ALU.max).then_inc(max_read[bank], 1)
                if c % N_MAX == N_MAX - 1:
                    qb = c // N_MAX
                    js = slice(CPB // QB * qb, CPB // QB * (qb + 1))
                    for done in (c - 1, c):
                        bk, bf = max_use(m, ("max", done))
                        need(dve, max_read[bk], bf + 1)
                    if not isinstance(m, int) or m > qb:
                        bk, bf = max_use(m - 1, ("turn", qb))
                        need(dve, max_done[bk], bf + 1)
                    dve.tensor_reduce(minus_max[:, js, AUG:AUG + HPG], maxima[:, js, :, :], AX.X, ALU.max,
                                      negate=True).then_inc(max_ready, 1)

            def tick(m, p):
                for u in range(UNITS):
                    todo = [e[1] for e in maxes(u) if e[0] == "max" and exists(m, e)]
                    for c in range(CPB):
                        if u == PREP_STEP * c // 2 + 1 and live(m, NT):
                            for step in range(4):
                                chunk(m, p, c, step)
                                if todo:
                                    maximum(m, todo.pop(0))
                    for a in todo:
                        maximum(m, a)
                    for qb in range(QB):
                        if 0 <= u - INVERT_AT[qb] <= PIECES and live(m - 1 - qb, NT):
                            normalise(m - 1 - qb, qb, u - INVERT_AT[qb])
            ticks(dve, *sched, tick)
            for step in range(PIECES + 1):
                normalise(NT - 1, 1, step)

        @block.tensor
        def _(pe):
            def pv(g, p, j):
                qb, kt = j // CPB, j % CPB
                need(pe, exp_done, UNITS * g + 2 * j + 2)
                if kt == 0:
                    need(pe, y_copied, QB * g + qb)
                for h in range(HPG):
                    mm = pe.matmul(ps_y[HD * h:HD * h + HD, :], v[p][:, kt, HD * h:HD * h + HD], probs[(2 * j + h // 2) % 4][:, h % 2, :],
                                   start=(kt == 0), stop=(kt == CPB - 1), skip_group_check=True)
                mm.then_inc(pv_done, 1)

            def scores(g, p, u):
                qb, kt, pair = u // LAST, u // 2 % CPB, u % 2
                need(pe, exp_done, UNITS * g + u - 1)
                if u % LAST == 0:
                    m = g + 1 if qb else g
                    bank, before = max_use(m, ("turn", qb))
                    need(pe, max_read[bank], before + 1)
                for i in range(2):
                    h = 2 * pair + i
                    mm = pe.matmul(ps_sc[u % 2][:, i, :], k_st[p][:, h, P * kt:P * kt + P], q_st[p][:, h, DIM * qb:DIM * qb + DIM],
                                   start=True, stop=True)
                mm.then_inc(score_done, 1)

            def prepare(m, p, e):
                kind, c = e
                need(pe, prep_read, prep_use(m, e)[1])
                n = CPB * m + c
                if kind == "proj":
                    b = c % 2
                    g = m % GROUPS
                    need(pe, xt_ld[b], 16 * (CPB // 2 * m + c // 2 + 1))
                    cols = lambda w: (lambda k: w[:, k, bass.ds(g, 1), :].rearrange("p a n -> p (a n)"))
                    three_pass(pe, ps_prep[:, 0:3, :].rearrange("p a n -> p (a n)"), lambda k: xt[b][:, 0, k, :], lambda k: xt[b][:, 1, k, :],
                               cols(w_hi), cols(w_lo), KD, prep_done)
                elif kind == "den":
                    need(pe, added, ADDS * (QB * (m - back(e)) + c + 1))
                    for h in range(HPG):
                        mm = pe.matmul(ps_prep[HD * h:HD * h + HD, :, :].rearrange("p a n -> p (a n)"), ones[:, :], summed[c][h // 2][:, h % 2, :],
                                       start=True, stop=True, skip_group_check=True)
                    mm.then_inc(prep_done, 1)
                else:
                    need(pe, stacked, 2 * n + 2)
                    src, cols = (q_tok[c % 2], AUG) if kind == "q" else (k_tok[c % 2], P)
                    for h in range(HPG):
                        mm = pe.transpose(ps_prep[0:cols, h, :], src[:, h, 0:cols], ident[:, :])
                    mm.then_inc(prep_done, 1)

            def maximum(m, p, e):
                kind, c = e
                bank, before = max_use(m, e)
                dst, b = ps_max[bank], (p + back(e)) % 2
                need(pe, max_read[bank], before)
                if kind == "max":
                    j, h, half = c // (2 * HPG), c // 2 % HPG, c % 2
                    if c == 0:
                        need(pe, prep_read, prep_use(m, ("k", CPB - 1))[1] + 1)
                    pe.matmul(dst[:, :, :].rearrange("p a n -> p (a n)"), q_st[b][0:AUG, h, P * j:P * j + P], k_st[b][0:AUG, h, DIM * half:DIM * half + DIM],
                              start=True, stop=True).then_inc(max_done[bank], 1)
                else:
                    need(pe, max_ready, QB * (m - c) + c + 1)
                    for j in range(4):
                        mm = pe.transpose(dst[:, j, :], minus_max[:, 4 * c + j, :], ident[:, :])
                    mm.then_inc(max_done[bank], 1)

            def tick(m, p):
                q = 1 - p
                for u in range(UNITS):
                    if live(m - 1, NT):
                        scores(m - 1, q, u)
                    todo = [e for e in maxes(u) if exists(m, e)]
                    per_slot = -(-len(todo) // 4)
                    for slot in range(4):
                        if slot % 2 and exists(m, preps(u)[slot // 2]):
                            prepare(m, p, preps(u)[slot // 2])
                        if slot == 2 and u and u % 2 == 0 and live(m - 1, NT):
                            pv(m - 1, q, u // 2 - 1)
                        if slot == 2 and u == 0 and live(m - 2, NT):
                            pv(m - 2, p, PVS - 1)
                        for e in todo[per_slot * slot:per_slot * (slot + 1)]:
                            maximum(m, p, e)
            ticks(pe, *sched, tick)
            pv(NT - 1, (NT - 1) % 2, PVS - 1)
            prepare(NT + 1, (NT + 1) % 2, ("den", 1))


def layer1_ffn(nc, x1_in, xt_in, yt_in, woT, gateT, upT, downT, s_gate, s_up, s_down, out):
    x1_t = x1_in.rearrange("(c p) d -> c p d", p=P)
    out_t = out.rearrange("b (c p) d -> (b c) p d", p=P)
    KH = HID // P
    cuts = [(0, DIM), (DIM, 2 * DIM), (2 * DIM, HID)]
    with ExitStack() as ctx:
        sb = lambda name, shape, dt=F32: ctx.enter_context(nc.sbuf_tensor(f"l1_ffn_{name}", shape, dt))
        sem = lambda name: ctx.enter_context(nc.semaphore(f"l1_ffn_{name}"))
        wo_hi, wo_lo = (sb(f"wo_{n}", [P, KD, DIM], F32R) for n in ("hi", "lo"))
        w_gu = sb("w_gu", [P, 2, KD, HID], F32R)
        w_down = sb("w_down", [P, KH, DIM], F32R)
        sc_gu = sb("sc_gu", [P, 2, HID])
        sc_down = sb("sc_down", [P, DIM])
        ident = sb("ident", [P, P])
        with ExitStack() as prep:
            psb = lambda name, shape, dt=F32: prep.enter_context(nc.sbuf_tensor(f"l1_ffn_{name}", shape, dt))
            psem = lambda name: prep.enter_context(nc.semaphore(f"l1_ffn_{name}"))
            raw_gu = psb("raw_gu", [P, 2, KD, HID], I32)
            raw_down = psb("raw_down", [P, KH, DIM], I32)
            raw_o = psb("raw_o", [P, KD, DIM])
            raw_in = [psem(f"raw_in{i}") for i in range(4)]
            made, split = psem("made"), psem("split")
            scales_in = psem("scales_in")
            block = prep.enter_context(nc.Block())

            @block.sync
            def _(sp):
                sp.dma_start(raw_gu[:, 0, :, :], gateT.rearrange("(k p) n -> p k n", p=P)).then_inc(raw_in[0], 16)
                sp.dma_start(raw_gu[:, 1, :, :], upT.rearrange("(k p) n -> p k n", p=P)).then_inc(raw_in[1], 16)
                sp.dma_start(raw_down[:, :, :], downT.rearrange("(k p) n -> p k n", p=P)).then_inc(raw_in[2], 16)
                sp.dma_start(raw_o[:, :, :], woT.rearrange("(k p) n -> p k n", p=P)).then_inc(raw_in[3], 16)
                sp.wait_ge(scales_in, 48)

            @block.scalar
            def _(act):
                act.dma_start(sc_gu[:, 0, :], s_gate.rearrange("(a n) -> a n", a=1).to_broadcast([P, HID])).then_inc(scales_in, 16)
                act.dma_start(sc_gu[:, 1, :], s_up.rearrange("(a n) -> a n", a=1).to_broadcast([P, HID])).then_inc(scales_in, 16)
                act.dma_start(sc_down[:, :], s_down.rearrange("(a n) -> a n", a=1).to_broadcast([P, DIM])).then_inc(scales_in, 16)

            @block.gpsimd
            def _(pool):
                pool.memset(ident[:, :], 0.0).then_inc(made, 1)
                pool.wait_ge(made, 1)
                pool.affine_select(out=ident[:, :], in_=ident[:, :], compare_op=ALU.not_equal, fill=1.0,
                                   base=0, pattern=[[-1, P]], channel_multiplier=1)

            @block.vector
            def _(dve):
                for i in range(2):
                    dve.wait_ge(raw_in[i], 16)
                    dve.tensor_scalar(w_gu[:, i, :, :], raw_gu[:, i, :, :], ZERO_POINT, None, ALU.subtract)
                dve.wait_ge(raw_in[2], 16)
                dve.tensor_scalar(w_down[:, :, :], raw_down[:, :, :], ZERO_POINT, None, ALU.subtract)
                dve.wait_ge(raw_in[3], 16)
                dve.tensor_copy(wo_hi[:, :, :], raw_o[:, :, :]).then_inc(split, 1)
                dve.wait_ge(split, 1)
                dve.tensor_tensor(wo_lo[:, :, :], raw_o[:, :, :], fp32(wo_hi[:, :, :]), ALU.subtract)

        two = lambda name, shape, dt=F32: [sb(f"{name}{i}", shape, dt) for i in range(2)]
        xt = two("xt", [P, 2, KD, P], F32R)
        yt = two("yt", [P, GROUPS, P])
        yt_hi, yt_lo = two("yt_hi", [P, GROUPS, P], F32R), two("yt_lo", [P, GROUPS, P], F32R)
        x1 = two("x1", [P, DIM])
        gate, up, mixed = two("gate", [P, HID]), two("up", [P, HID]), two("mixed", [P, HID])
        ht_hi, ht_lo = two("ht_hi", [P, KH, P], F32R), two("ht_lo", [P, KH, P], F32R)
        s_sb, g_sb, res = two("s_sb", [P, DIM]), two("g_sb", [P, DIM]), two("res", [P, DIM])
        ps = lambda name, shape: ctx.enter_context(nc.psum_tensor(f"l1_ffn_{name}", shape, F32))
        ps_gu = [ps(f"ps_gu{i}", [P, DIM]) for i in range(3)]
        ps_turn = [ps(f"ps_turn{i}", [P, 4, P]) for i in range(2)]
        ps_s = ps("ps_s", [P, DIM])
        ps_down = [ps(f"ps_down{i}", [P, DIM]) for i in range(2)]

        xt_ld, yt_ld, x1_ld, stored = ([sem(f"{n}{i}") for i in range(2)] for n in ("xt_ld", "yt_ld", "x1_ld", "stored"))
        yt_hi_ready, yt_lo_ready = sem("yt_hi_ready"), sem("yt_lo_ready")
        gu_done, gate_scaled, up_scaled, silu_done, mixed_ready = (sem(n) for n in ("gu_done", "gate_scaled", "up_scaled", "silu_done", "mixed_ready"))
        turned, ht_hi_ready, ht_lo_ready = sem("turned"), sem("ht_hi_ready"), sem("ht_lo_ready")
        s_done, s_ready, down_done, final, g_ready = (sem(n) for n in ("s_done", "s_ready", "down_done", "final", "g_ready"))
        block = ctx.enter_context(nc.Block())
        N = len(cuts)
        F_SCALED, F_MUL, F_ADD, F_N = 1, 2, 3, 3
        sched = (-1, 4, CHUNKS - 2, CHUNKS + 1)

        @block.sync
        def _(sp):
            def tick(t, p):
                c, b = t + 2, p
                if live(c, CHUNKS):
                    need(sp, gu_done, 2 * N * (c - 1))
                    sp.dma_start(fp32(xt[b][:, :, :, :]).rearrange("p h k n -> p (h k n)"), xt_in[c]).then_inc(xt_ld[b], 16)
                    need(sp, yt_lo_ready, c - 1)
                    sp.dma_start(yt[b][:, :, :], yt_in[c]).then_inc(yt_ld[b], 16)
                c, b = t, p
                if live(c, CHUNKS):
                    need(sp, final, F_N * (c - 1))
                    sp.dma_start(x1[b][:, :], x1_t[c]).then_inc(x1_ld[b], 16)
                c, b = t - 2, p
                if live(c, CHUNKS):
                    need(sp, final, F_N * c + F_ADD)
                    sp.dma_start(out_t[c], res[b][:, :]).then_inc(stored[b], 16)
            ticks(sp, -2, 4, CHUNKS - 2, CHUNKS + 1, tick)
            for b in range(2):
                sp.wait_ge(stored[b], 8 * CHUNKS)

        @block.gpsimd
        def _(pool):
            def tick(t, p):
                if live(t, CHUNKS):
                    for n, (lo, hi) in enumerate(cuts):
                        need(pool, silu_done, N * t + n + 1)
                        need(pool, up_scaled, N * t + n + 1)
                        need(pool, turned, N * (t - 1))
                        pool.tensor_tensor(mixed[p][:, lo:hi], gate[p][:, lo:hi], up[p][:, lo:hi], ALU.mult).then_inc(mixed_ready, 1)
            ticks(pool, *sched, tick)

        @block.scalar
        def _(act):
            def tick(t, p):
                c, b = t - 2, p
                if live(c, CHUNKS):
                    need(act, final, F_N * c + F_SCALED)
                    act.activation(g_sb[b][:, :], g_sb[b][:, :], ACT.Silu).then_inc(g_ready, 1)
                c, b = t + 1, 1 - p
                if live(c, CHUNKS):
                    need(act, yt_ld[b], 8 * (c - b) + 16)
                    need(act, s_done, c - 1)
                    act.activation(yt_hi[b][:, :, :], yt[b][:, :, :], ACT.Copy).then_inc(yt_hi_ready, 1)
                for n, (lo, hi) in enumerate(cuts):
                    if live(t, CHUNKS):
                        need(act, gate_scaled, N * t + n + 1)
                        act.activation(gate[p][:, lo:hi], gate[p][:, lo:hi], ACT.Silu).then_inc(silu_done, 1)
                    c, b = t - 1, 1 - p
                    if live(c, CHUNKS):
                        need(act, turned, N * c + n + 1)
                        need(act, down_done, c - 1)
                        act.activation(ht_hi[b][:, lo // P:hi // P, :], ps_turn[(N * b + n) % 2][:, 0:(hi - lo) // P, :], ACT.Copy).then_inc(ht_hi_ready, 1)
                if live(t, CHUNKS):
                    need(act, s_done, t + 1)
                    need(act, final, F_N * (t - 2) + F_MUL)
                    act.activation(s_sb[p][:, :], ps_s[:, :], ACT.Copy).then_inc(s_ready, 1)
            ticks(act, *sched, tick)

        @block.vector
        def _(dve):
            def tick(t, p):
                c, b = t - 2, p
                if live(c, CHUNKS):
                    need(dve, down_done, c + 1)
                    dve.tensor_tensor(g_sb[b][:, :], ps_down[b][:, :], sc_down[:, :], ALU.mult).then_inc(final, 1)
                cy, by = t + 1, 1 - p
                if live(cy, CHUNKS):
                    need(dve, yt_hi_ready, cy + 1)
                    need(dve, s_done, cy - 1)
                    dve.tensor_tensor(yt_lo[by][:, :, :], yt[by][:, :, :], fp32(yt_hi[by][:, :, :]), ALU.subtract).then_inc(yt_lo_ready, 1)
                for n, (lo, hi) in enumerate(cuts):
                    if live(t, CHUNKS):
                        if n == 0:
                            need(dve, mixed_ready, N * (t - 1))
                        need(dve, gu_done, 2 * (N * t + n) + 1)
                        dve.tensor_tensor(gate[p][:, lo:hi], ps_gu[2 * n % 3][:, 0:hi - lo], sc_gu[:, 0, lo:hi], ALU.mult).then_inc(gate_scaled, 1)
                        need(dve, gu_done, 2 * (N * t + n) + 2)
                        dve.tensor_tensor(up[p][:, lo:hi], ps_gu[(2 * n + 1) % 3][:, 0:hi - lo], sc_gu[:, 1, lo:hi], ALU.mult).then_inc(up_scaled, 1)
                    ct, bt = t - 1, 1 - p
                    if live(ct, CHUNKS):
                        need(dve, ht_hi_ready, N * ct + n + 1)
                        dve.tensor_tensor(ht_lo[bt][:, lo // P:hi // P, :], ps_turn[(N * bt + n) % 2][:, 0:(hi - lo) // P, :],
                                          fp32(ht_hi[bt][:, lo // P:hi // P, :]), ALU.subtract).then_inc(ht_lo_ready, 1)
                    if live(c, CHUNKS) and n == 0:
                        need(dve, g_ready, c + 1)
                        need(dve, s_ready, c + 1)
                        dve.tensor_tensor(g_sb[b][:, :], g_sb[b][:, :], s_sb[b][:, :], ALU.mult).then_inc(final, 1)
                    if live(c, CHUNKS) and n == 1:
                        need(dve, final, F_N * c + F_MUL)
                        need(dve, x1_ld[b], 8 * (c - b) + 16)
                        need(dve, stored[b], 8 * (c - b))
                        dve.tensor_tensor(res[b][:, :], g_sb[b][:, :], x1[b][:, :], ALU.add).then_inc(final, 1)
            ticks(dve, *sched, tick)

        @block.tensor
        def _(pe):
            def tick(t, p):
                q = 1 - p
                for n, (lo, hi) in enumerate(cuts):
                    if live(t, CHUNKS):
                        need(pe, xt_ld[p], 8 * (t - p) + 16)
                        for w in range(2):
                            use = 2 * n + w - 3
                            need(pe, (gate_scaled, up_scaled)[use % 2], N * t + (use // 2) + 1)
                            two_pass(pe, ps_gu[(2 * n + w) % 3][:, 0:hi - lo], lambda k: xt[p][:, 0, k, :], lambda k: xt[p][:, 1, k, :],
                                     lambda k: w_gu[:, w, k, lo:hi], range(KD), True, True).then_inc(gu_done, 1)
                    c = t - 1
                    if live(c, CHUNKS):
                        need(pe, mixed_ready, N * c + n + 1)
                        need(pe, ht_lo_ready, N * c + n - 1)
                        for k in range(lo // P, hi // P):
                            mm = pe.transpose(ps_turn[(N * q + n) % 2][:, k - lo // P, :], mixed[q][:, k * P:(k + 1) * P], ident[:, :])
                        mm.then_inc(turned, 1)
                if live(t, CHUNKS):
                    need(pe, yt_hi_ready, t + 1)
                    need(pe, yt_lo_ready, t + 1)
                    need(pe, s_ready, t)
                    three_pass(pe, ps_s[:, :], lambda k: yt_hi[p][:, k, :], lambda k: yt_lo[p][:, k, :],
                               lambda k: wo_hi[:, k, :], lambda k: wo_lo[:, k, :], KD, s_done)
                c = t - 1
                if live(c, CHUNKS):
                    need(pe, final, F_N * (c - 2) + F_SCALED)
                    for n, (lo, hi) in enumerate(cuts):
                        need(pe, ht_lo_ready, N * c + n + 1)
                        mm = two_pass(pe, ps_down[q][:, :], lambda k: ht_hi[q][:, k, :], lambda k: ht_lo[q][:, k, :],
                                      lambda k: w_down[:, k, :], range(lo // P, hi // P), n == 0, n == N - 1)
                    mm.then_inc(down_done, 1)
            ticks(pe, *sched, tick)


def layers(nc, x, Wqkv, bqkv, Wout, bout, slopes, w_fcT, w_projT, wqkvT, rope_cos, rope_sin, woT,
           gateT, s_gate, upT, s_up, downT, s_down, out):
    dram = lambda name, shape: nc.dram_tensor(name, shape, F32, kind="Internal").ap()
    s0 = dram("s0", [TOKENS, DIM])
    x1 = dram("x1_rows", [TOKENS, DIM])
    xt = dram("xt_chunks", [CHUNKS, P, 2 * KD * P])
    yt = dram("yt_chunks", [CHUNKS, P, GROUPS, P])
    layer0_attention(nc, x, Wqkv, bqkv, Wout, bout, slopes, s0)
    layer0_ffn(nc, x, s0, w_fcT, w_projT, x1, xt)
    layer1_attention(nc, xt, wqkvT, rope_cos, rope_sin, yt)
    layer1_ffn(nc, x1, xt, yt, woT, gateT, upT, downT, s_gate, s_up, s_down, out)


def rope_tables(np):
    inv_freq = (np.float32(1.0) / np.float32(10000.0) ** (np.arange(0, HD, 2, dtype=np.float32) / np.float32(HD))).astype(np.float32)
    angle = np.arange(SEQ, dtype=np.float32)[:, None] * inv_freq[None, :]
    sign = np.where(np.arange(HD // 2) < HD // 4, -1.0, 1.0).astype(np.float32)
    return np.cos(angle), np.sin(angle) * sign


def kernel(**inputs):
    import numpy as np
    import concourse.bacc as bacc
    from concourse import mybir as mb
    from concourse.bass_utils import run_bass_kernel_spmd

    a = {name: np.asarray(value) for name, value in inputs.items()}
    turned = lambda name: np.ascontiguousarray(a[name].T)
    wqkvT = np.stack([a[f"L1_attn_{n}"].T.reshape(DIM, GROUPS, P) for n in ("wq", "wk", "wv")], 2).reshape(DIM, GROUPS, 3 * P)
    cos, sin = rope_tables(np)
    laid_out = {
        "x": a["L0_attn_x"], "Wqkv": a["L0_attn_Wqkv"], "bqkv": a["L0_attn_bqkv"], "Wout": a["L0_attn_Wout"],
        "bout": a["L0_attn_bout"], "slopes": a["L0_attn_slopes"], "w_fcT": turned("L0_ffn_w_fc"),
        "w_projT": turned("L0_ffn_w_proj"), "wqkvT": wqkvT, "rope_cos": cos, "rope_sin": sin,
        "woT": turned("L1_attn_wo"), "gateT": turned("L1_ffn_wq_gate"), "s_gate": a["L1_ffn_s_gate"],
        "upT": turned("L1_ffn_wq_up"), "s_up": a["L1_ffn_s_up"], "downT": turned("L1_ffn_wq_down"),
        "s_down": a["L1_ffn_s_down"]}
    nc = bacc.Bacc("TRN2", target_bir_lowering=False, num_devices=1)
    arrays, args = {}, []
    for name, value in laid_out.items():
        arrays[f"in_{name}"] = np.ascontiguousarray(value)
        args.append(nc.dram_tensor(f"in_{name}", value.shape, mb.dt.from_np(value.dtype), kind="ExternalInput").ap())
    out = nc.dram_tensor("out_x", (BATCH, SEQ, DIM), mb.dt.float32, kind="ExternalOutput").ap()
    layers(nc, *args, out)
    result = run_bass_kernel_spmd(nc, [arrays], core_ids=[0])
    return result.results[0]["out_x"]
```

```python
import concourse.bass as bass
from concourse import mybir
from contextlib import ExitStack

F32 = mybir.dt.float32
F32R = mybir.dt.float32r
I32 = mybir.dt.int32
ALU = mybir.AluOpType
ACT = mybir.ActivationFunctionType
AX = mybir.AxisListType

P = 128
BATCH, SEQ, DIM, HEADS = 4, 1024, 512, 16
HD = DIM // HEADS
TOKENS = BATCH * SEQ
CHUNKS = TOKENS // P
CPB = SEQ // P
KD = DIM // P
HPG = P // HD
GROUPS = HEADS // HPG
FC = 4 * DIM
HID = 1408
ZERO_POINT = 128.0
ATT_SCALE = HD ** -0.5


def need(eng, sem, count):
    if isinstance(count, int) and count <= 0:
        return
    eng.wait_ge(sem, count)


def live(c, n):
    return not isinstance(c, int) or 0 <= c < n


def ticks(eng, first, loop_from, loop_to, last, tick):
    for t in range(first, loop_from):
        tick(t, t % 2)
    with eng.Fori(0, (loop_to - loop_from) // 2) as i:
        for p in range(2):
            tick(2 * i + (loop_from + p), (loop_from + p) % 2)
    for t in range(loop_to, last + 1):
        tick(t, t % 2)


def fp32(ap):
    return ap.bitcast(F32)


def three_pass(pe, out, a_hi, a_lo, w_hi, w_lo, slices, bank_done):
    n = 0
    for k in range(slices):
        for a, w in ((a_hi, w_hi), (a_lo, w_hi), (a_hi, w_lo)):
            mm = pe.matmul(out, a(k), w(k), start=(n == 0), stop=(n == 3 * slices - 1))
            n += 1
    mm.then_inc(bank_done, 1)


def two_pass(pe, out, a_hi, a_lo, w, ks, first, last):
    for k in ks:
        for n, a in enumerate((a_hi, a_lo)):
            mm = pe.matmul(out, a(k), w(k), start=(first and k == ks[0] and n == 0),
                           stop=(last and k == ks[-1] and n == 1))
    return mm


def cap(count, most):
    return min(count, most) if isinstance(count, int) else count


def layer0_attention(nc, x, Wqkv, bqkv, Wout, bout, slopes, s_out):
    x_t = x.rearrange("b (c p) d -> (b c) p d", p=P)
    s_t = s_out.rearrange("(c p) d -> c p d", p=P)
    QKV = 3 * DIM
    with ExitStack() as ctx:
        sb = lambda name, shape, dt=F32: ctx.enter_context(nc.sbuf_tensor(f"l0_attn_{name}", shape, dt))
        sem = lambda name: ctx.enter_context(nc.semaphore(f"l0_attn_{name}"))
        wq_hi, wq_lo = (sb(f"wqkv_{n}", [P, KD, QKV], F32R) for n in ("hi", "lo"))
        wo_hi, wo_lo = (sb(f"wout_{n}", [P, KD, DIM], F32R) for n in ("hi", "lo"))
        bias = sb("bias", [P, QKV])
        bias_out = sb("bias_out", [P, DIM])
        ident = sb("ident", [P, P])
        decay = sb("decay", [P, HEADS, P])
        q_decay = sb("q_decay", [P, GROUPS, P])
        k_decay = sb("k_decay", [P, HEADS])
        blk_decay = sb("blk_decay", [P, GROUPS])
        own_head = sb("own_head", [P, GROUPS, P])
        keep = sb("keep", [P, CHUNKS])
        bn_eps = sb("ln_eps", [P, 1])
        minus_half = sb("minus_half", [P, 1])

        with ExitStack() as prep:
            psb = lambda name, shape, dt=F32: prep.enter_context(nc.sbuf_tensor(f"l0_attn_{name}", shape, dt))
            raw_q = psb("raw_q", [P, KD, QKV])
            raw_o = psb("raw_o", [P, KD, DIM])
            dist = psb("dist", [P, P])
            pos = psb("pos", [P, P])
            left = psb("left", [P, 1])
            slope_row = psb("slope_row", [P, HEADS])
            slope_col = psb("slope_col", [P, GROUPS])
            psem = lambda name: prep.enter_context(nc.semaphore(f"l0_attn_{name}"))
            raw_in = [psem(f"raw_in{k}") for k in range(KD)]
            raw_o_in, slopes_in, bias_in = psem("raw_o_in"), psem("slopes_in"), psem("bias_in")
            w_hi_made, iotas, scaled, decays = (psem(n) for n in ("w_hi_made", "iotas", "scaled", "decays"))
            made = psem("made")
            block = prep.enter_context(nc.Block())
            wq_t = Wqkv.rearrange("(k p) n -> p k n", p=P)

            @block.sync
            def _(sp):
                for k in range(KD):
                    sp.dma_start(raw_q[:, k, :], wq_t[:, k, :]).then_inc(raw_in[k], 16)
                sp.dma_start(raw_o[:, :, :], Wout.rearrange("(k p) n -> p k n", p=P)).then_inc(raw_o_in, 16)

            @block.scalar
            def _(act):
                act.dma_start(slope_row[:, :], slopes.rearrange("(a h) -> a h", a=1).to_broadcast([P, HEADS])).then_inc(slopes_in, 16)
                for h in range(HPG):
                    act.dma_start(slope_col[HD * h:HD * h + HD, :],
                                  slopes.rearrange("(a g h) -> h a g", a=1, h=HPG)[h].to_broadcast([HD, GROUPS]),
                                  allow_slow_non_contiguous=True).then_inc(slopes_in, 16)
                act.dma_start(bias[:, :], bqkv.rearrange("(a n) -> a n", a=1).to_broadcast([P, QKV])).then_inc(bias_in, 16)
                act.dma_start(bias_out[:, :], bout.rearrange("(a n) -> a n", a=1).to_broadcast([P, DIM])).then_inc(bias_in, 16)
                for k in range(KD):
                    act.wait_ge(raw_in[k], 16)
                    act.activation(wq_hi[:, k, :], raw_q[:, k, :], ACT.Copy).then_inc(w_hi_made, 1)
                act.wait_ge(raw_o_in, 16)
                act.activation(wo_hi[:, :, :], raw_o[:, :, :], ACT.Copy).then_inc(w_hi_made, 1)
                act.wait_ge(slopes_in, 16 * (HPG + 1))
                act.wait_ge(iotas, 4)
                act.wait_ge(scaled, 1)
                for h in range(HEADS):
                    act.activation(decay[:, h, :], dist[:, :], ACT.Exp, scale=slope_row[:, h:h + 1]).then_inc(decays, 1)
                for g in range(GROUPS):
                    act.activation(q_decay[:, g, :], pos[:, :], ACT.Exp, scale=slope_col[:, g:g + 1]).then_inc(decays, 1)
                act.activation(k_decay[:, :], slope_row[:, :], ACT.Exp, scale=left[:, 0:1]).then_inc(decays, 1)
                act.activation(blk_decay[:, :], slope_col[:, :], ACT.Exp, scale=float(P)).then_inc(decays, 1)
                act.wait_ge(bias_in, 32)

            @block.gpsimd
            def _(pool):
                pool.iota(dist[:, :], [[1, P]], base=0, channel_multiplier=-1,
                          allow_small_or_imprecise_dtypes=True).then_inc(made, 1)
                pool.wait_ge(made, 1)
                pool.tensor_scalar(dist[:, :], dist[:, :], 0.0, None, ALU.max).then_inc(iotas, 1)
                pool.iota(pos[:, :], [[1, P]], base=0, channel_multiplier=0,
                          allow_small_or_imprecise_dtypes=True).then_inc(iotas, 1)
                pool.iota(left[:, :], [[0, 1]], base=P, channel_multiplier=-1,
                          allow_small_or_imprecise_dtypes=True).then_inc(iotas, 1)
                pool.memset(ident[:, :], 0.0).then_inc(made, 1)
                pool.memset(own_head[:, :, :], 1.0).then_inc(made, 1)
                pool.memset(bn_eps[:, :], 1e-5)
                pool.memset(minus_half[:, :], -0.5)
                pool.memset(keep[:, :], 1.0).then_inc(iotas, 1)
                pool.wait_ge(made, 3)
                pool.wait_ge(iotas, 4)
                pool.memset(keep[:, CPB - 1::CPB], 0.0)
                pool.affine_select(out=ident[:, :], in_=ident[:, :], compare_op=ALU.not_equal, fill=1.0,
                                   base=0, pattern=[[-1, P]], channel_multiplier=1)
                v = own_head[:, :, :].rearrange("p g (h e) -> p g h e", h=HPG)
                pool.affine_select(out=v, in_=v, compare_op=ALU.is_ge, fill=0.0, base=0,
                                   pattern=[[0, GROUPS], [-HD, HPG], [0, HD]], channel_multiplier=1).then_inc(made, 1)
                pool.wait_ge(made, 4)
                pool.affine_select(out=v, in_=v, compare_op=ALU.is_ge, fill=0.0, base=HD - 1,
                                   pattern=[[0, GROUPS], [HD, HPG], [0, HD]], channel_multiplier=-1)
                pool.wait_ge(slopes_in, 16 * (HPG + 1))
                pool.tensor_scalar(slope_row[:, :], slope_row[:, :], -1.0, None, ALU.mult)
                pool.tensor_scalar(slope_col[:, :], slope_col[:, :], -1.0, None, ALU.mult).then_inc(scaled, 1)
                pool.wait_ge(decays, HEADS)
                pool.affine_select(out=decay[:, :, :], in_=decay[:, :, :], compare_op=ALU.is_ge, fill=0.0,
                                   base=0, pattern=[[0, HEADS], [1, P]], channel_multiplier=-1)

            @block.vector
            def _(dve):
                for k in range(KD):
                    dve.wait_ge(w_hi_made, k + 1)
                    dve.tensor_tensor(wq_lo[:, k, :], raw_q[:, k, :], fp32(wq_hi[:, k, :]), ALU.subtract)
                dve.wait_ge(w_hi_made, KD + 1)
                dve.tensor_tensor(wo_lo[:, :, :], raw_o[:, :, :], fp32(wo_hi[:, :, :]), ALU.subtract)

        two = lambda name, shape, dt=F32: [sb(f"{name}{i}", shape, dt) for i in range(2)]
        xin = two("xin", [P, DIM])
        stats = two("stats", [P, 6])
        mean_var = two("mean_var", [P, 2])
        rstd = two("rstd", [P, 1])
        xn = two("xn", [P, DIM])
        xt_hi, xt_lo = two("xt_hi", [P, KD, P], F32R), two("xt_lo", [P, KD, P], F32R)
        qkv = two("qkv", [P, QKV])
        k_dec = two("k_dec", [P, DIM])
        q_dec = two("q_dec", [P, GROUPS, P])
        kt = two("kt", [P, GROUPS, P])
        q_wide = two("q_wide", [P, GROUPS, HPG, P])
        masked = two("masked", [P, GROUPS, HPG, P])
        state = two("state", [P, GROUPS, P])
        state_new = sb("state_new", [P, GROUPS, P])
        ot_hi, ot_lo = two("ot_hi", [P, GROUPS, P], F32R), two("ot_lo", [P, GROUPS, P], F32R)
        s_sb = two("s_sb", [P, DIM])
        ps = lambda name, shape: ctx.enter_context(nc.psum_tensor(f"l0_attn_{name}", shape, F32))
        ps_proj = [ps(f"ps_proj{i}", [P, DIM]) for i in range(2)]
        ps_turn = [ps(f"ps_turn{i}", [P, 4, P]) for i in range(2)]
        ps_score = [ps(f"ps_score{i}", [P, HPG, P]) for i in range(2)]
        ps_state = ps("ps_state", [P, GROUPS, P])
        ps_o = ps("ps_o", [P, GROUPS, P])

        x_in = [sem(f"x_in{i}") for i in range(2)]
        s_stored = [sem(f"s_stored{i}") for i in range(2)]
        zeroed, ln_step, rstd_ready, xn_ready = sem("zeroed"), sem("ln_step"), sem("rstd_ready"), sem("xn_ready")
        proj_done = sem("proj_done")
        turn_done = sem("turn_done")
        xt_hi_ready, xt_lo_ready = sem("xt_hi_ready"), sem("xt_lo_ready")
        qkv_ready, k_dec_ready, qt_ready, kt_ready, q_dec_ready = (sem(n) for n in ("qkv_ready", "k_dec_ready", "qt_ready", "kt_ready", "q_dec_ready"))
        score_done, masked_ready = sem("score_done"), sem("masked_ready")
        upd_done, st_step, state_ready = sem("upd_done"), sem("st_step"), sem("state_ready")
        o_done, ot_hi_ready, ot_lo_ready = sem("o_done"), sem("ot_hi_ready"), sem("ot_lo_ready")
        s_ready = sem("s_ready")
        block = ctx.enter_context(nc.Block())
        sched = (-2, 4, CHUNKS - 2, CHUNKS + 1)
        PQ, PK, PV, PO = range(4)
        TQ, TK, TX = range(3)

        def proj_use(t, which):
            early = 3 * t + which if isinstance(t, int) and t < 2 else 4 * t + which - 2
            if isinstance(t, int) and t >= CHUNKS:
                early = 4 * CHUNKS - 2 + (t - CHUNKS)
            return early

        def turn_use(t, which):
            if isinstance(t, int) and t < 1:
                return t + 1
            if isinstance(t, int) and t == CHUNKS - 1:
                return 2 + 3 * (t - 1) + which
            if isinstance(t, int) and t >= CHUNKS:
                return 2 + 3 * (CHUNKS - 2) + 2 * (t - CHUNKS + 1) + which
            return 3 * t - 1 + which

        def proj_bank(t, p, which):
            return (proj_use(t, which) if isinstance(t, int) else 4 * p + which - 2) % 2

        def turn_bank(t, p, which):
            return (turn_use(t, which) if isinstance(t, int) else 3 * p - 1 + which) % 2

        @block.sync
        def _(sp):
            def tick(t, p):
                c = t + 3
                if live(c, CHUNKS):
                    need(sp, xn_ready, c - 1)
                    sp.dma_start(xin[(p + 1) % 2][:, :], x_t[c]).then_inc(x_in[(p + 1) % 2], 16)
                c = t - 2
                if live(c, CHUNKS):
                    need(sp, s_ready, c + 1)
                    sp.dma_start(s_t[c], s_sb[p][:, :]).then_inc(s_stored[p], 16)
            ticks(sp, -3, 4, CHUNKS - 4, CHUNKS + 1, tick)
            for p in range(2):
                sp.wait_ge(s_stored[p], 16 * CHUNKS // 2)

        @block.gpsimd
        def _(pool):
            def tick(t, p):
                c = t + 2
                if live(c, CHUNKS):
                    b = p
                    need(pool, ln_step, 2 * c + 2)
                    pool.tensor_tensor(rstd[b][:, :], mean_var[b][:, 1:2], bn_eps[:, :], ALU.add).then_inc(rstd_ready, 1)
                    need(pool, rstd_ready, 2 * c + 1)
                    pool.tensor_tensor(rstd[b][:, :], rstd[b][:, :], minus_half[:, :], ALU.pow).then_inc(rstd_ready, 1)
                c = t
                if live(c, CHUNKS):
                    need(pool, qkv_ready, 3 * c + 2)
                    need(pool, upd_done, c - 1)
                    kh = qkv[p][:, DIM:2 * DIM].rearrange("p (h d) -> p h d", h=HEADS)
                    pool.tensor_tensor(k_dec[p][:, :].rearrange("p (h d) -> p h d", h=HEADS), kh,
                                       k_decay[:, :].rearrange("p (h a) -> p h a", a=1).to_broadcast([P, HEADS, HD]),
                                       ALU.mult).then_inc(k_dec_ready, 1)
            ticks(pool, *sched, tick)

        @block.scalar
        def _(act):
            def tick(t, p):
                c, b = t - 1, (p + 1) % 2
                if live(c, CHUNKS):
                    use = turn_use(t, TQ)
                    need(act, turn_done, use + 1)
                    need(act, zeroed, 1)
                    need(act, score_done, GROUPS * (c - 1))
                    src = ps_turn[turn_bank(t, p, TQ)]
                    for h in range(HPG):
                        r = slice(HD * h, HD * h + HD)
                        ins = act.activation(q_wide[b][r, :, h, :], src[r, :, :], ACT.Copy)
                    ins.then_inc(qt_ready, 1)
                    need(act, turn_done, use + 2)
                    act.activation(kt[b][:, :, :], ps_turn[turn_bank(t, p, TK)][:, :, :], ACT.Copy).then_inc(kt_ready, 1)
                c, b = t + 1, (p + 1) % 2
                if live(c, CHUNKS):
                    need(act, turn_done, turn_use(t, TX) + 1)
                    need(act, qkv_ready, 3 * (c - 1))
                    act.activation(xt_hi[b][:, :, :], ps_turn[turn_bank(t, p, TX)][:, :, :], ACT.Copy).then_inc(xt_hi_ready, 1)
                c, b = t - 1, (p + 1) % 2
                if live(c, CHUNKS):
                    need(act, o_done, c + 1)
                    need(act, s_ready, c - 1)
                    act.activation(ot_hi[b][:, :, :], ps_o[:, :, :], ACT.Copy).then_inc(ot_hi_ready, 1)
            ticks(act, *sched, tick)

        @block.vector
        def _(dve):
            def evacuate(t, p, which):
                need(dve, proj_done, proj_use(t, which) + 1)
                if which == PV:
                    need(dve, o_done, t - 1)
                cols = slice(DIM * which, DIM * which + DIM)
                dve.tensor_tensor(qkv[p][:, cols], ps_proj[proj_bank(t, p, which)][:, :], bias[:, cols],
                                  ALU.add).then_inc(qkv_ready, 1)

            def tick(t, p):
                if isinstance(t, int) and t == 0:
                    for b in range(2):
                        dve.memset(q_wide[b][:, :, :, :], 0.0)
                    dve.memset(state[1][:, :, :], 0.0)
                    dve.memset(state[0][:, :, :], 0.0).then_inc(zeroed, 1)
                if live(t, CHUNKS):
                    evacuate(t, p, PQ)
                c, b = t - 1, (p + 1) % 2
                if live(c, CHUNKS):
                    need(dve, qt_ready, c + 1)
                    need(dve, o_done, c - 1)
                    dve.tensor_tensor(q_dec[b][:, :, :], ps_turn[turn_bank(t, p, TQ)][:, :, :], q_decay[:, :, :],
                                      ALU.mult).then_inc(q_dec_ready, 1)
                c = t + 2
                if live(c, CHUNKS):
                    need(dve, x_in[p], 8 * (c - p) + 16)
                    dve.bn_stats(stats[p][:, :], xin[p][:, :]).then_inc(ln_step, 1)
                    need(dve, ln_step, 2 * c + 1)
                if live(t, CHUNKS):
                    need(dve, k_dec_ready, t - 1)
                    evacuate(t, p, PK)
                if live(c, CHUNKS):
                    dve.bn_aggr(mean_var[p][:, :], stats[p][:, :]).then_inc(ln_step, 1)
                c = t + 1
                if live(c, CHUNKS):
                    need(dve, xt_hi_ready, c + 1)
                    dve.tensor_tensor(xt_lo[(p + 1) % 2][:, :, :], ps_turn[turn_bank(t, p, TX)][:, :, :],
                                      fp32(xt_hi[(p + 1) % 2][:, :, :]), ALU.subtract).then_inc(xt_lo_ready, 1)
                if live(t, CHUNKS):
                    evacuate(t, p, PV)
                c = t + 2
                if live(c, CHUNKS):
                    need(dve, rstd_ready, 2 * c + 2)
                    need(dve, ln_step, 2 * c + 2)
                    need(dve, xt_hi_ready, c - 1)
                    dve.tensor_scalar(xn[p][:, :], xin[p][:, :], mean_var[p][:, 0:1], rstd[p][:, 0:1],
                                      ALU.subtract, ALU.mult).then_inc(xn_ready, 1)
                c, b = t - 1, (p + 1) % 2
                if live(c, CHUNKS):
                    for g in range(GROUPS):
                        need(dve, score_done, GROUPS * c + g + 1)
                        dve.tensor_tensor(masked[b][:, g, :, :], ps_score[g % 2][:, :, :],
                                          decay[:, HPG * g:HPG * g + HPG, :], ALU.mult).then_inc(masked_ready, 1)
                c = t - 2
                if live(c, CHUNKS):
                    need(dve, proj_done, proj_use(t, PO) + 1)
                    need(dve, s_stored[p], 8 * (c - p))
                    dve.tensor_tensor(s_sb[p][:, :], ps_proj[proj_bank(t, p, PO)][:, :], bias_out[:, :],
                                      ALU.add).then_inc(s_ready, 1)
                c, b = t - 1, (p + 1) % 2
                if live(c, CHUNKS):
                    need(dve, upd_done, c + 1)
                    kp = keep[:, bass.ds(c, 1)] if not isinstance(c, int) else keep[:, c:c + 1]
                    dve.scalar_tensor_tensor(out=state_new[:, :, :], in0=ps_state[:, :, :], scalar=kp, in1=own_head[:, :, :],
                                             op0=ALU.mult, op1=ALU.mult).then_inc(st_step, 1)
                    need(dve, state_ready, c)
                    need(dve, o_done, c)
                    dve.scalar_tensor_tensor(out=state[1 - b][:, :, :], in0=state[b][:, :, :], scalar=kp,
                                             in1=blk_decay[:, :].rearrange("p (g a) -> p g a", a=1).to_broadcast([P, GROUPS, P]),
                                             op0=ALU.mult, op1=ALU.mult).then_inc(st_step, 1)
                    need(dve, st_step, 2 * c + 2)
                    dve.tensor_tensor(state[1 - b][:, :, :], state[1 - b][:, :, :], state_new[:, :, :],
                                      ALU.add).then_inc(state_ready, 1)
                    need(dve, ot_hi_ready, c + 1)
                    dve.tensor_tensor(ot_lo[b][:, :, :], ps_o[:, :, :], fp32(ot_hi[b][:, :, :]),
                                      ALU.subtract).then_inc(ot_lo_ready, 1)
            ticks(dve, *sched, tick)

        @block.tensor
        def _(pe):
            def turn(t, p, which, src, waits):
                use = turn_use(t, which)
                for s, n in waits:
                    need(pe, s, n)
                bank = ps_turn[turn_bank(t, p, which)]
                for k in range(4):
                    mm = pe.transpose(bank[:, k, :], src[:, k * P:(k + 1) * P], ident[:, :])
                mm.then_inc(turn_done, 1)

            def project(t, p, which):
                w = slice(DIM * which, DIM * which + DIM)
                three_pass(pe, ps_proj[proj_bank(t, p, which)][:, :],
                           lambda k: xt_hi[p][:, k, :], lambda k: xt_lo[p][:, k, :],
                           lambda k: wq_hi[:, k, w], lambda k: wq_lo[:, k, w], KD, proj_done)

            def tick(t, p):
                q = (p + 1) % 2
                if live(t, CHUNKS):
                    need(pe, xt_lo_ready, t + 1)
                    need(pe, xt_hi_ready, t + 1)
                    need(pe, qkv_ready, 3 * t - 1)
                    need(pe, qkv_ready, 3 * t)
                    need(pe, s_ready, t - 2)
                    project(t, p, PQ)
                c = t - 1
                if live(c, CHUNKS):
                    need(pe, kt_ready, c)
                    need(pe, q_dec_ready, c)
                    need(pe, xt_lo_ready, t if not isinstance(t, int) else min(t, CHUNKS))
                    turn(t, p, TQ, qkv[q][:, 0:DIM], [(qkv_ready, 3 * c + 1)])
                    if not isinstance(t, int) or t < CHUNKS:
                        need(pe, xt_lo_ready, t + 1)
                    turn(t, p, TK, qkv[q][:, DIM:2 * DIM], [(qkv_ready, 3 * c + 2)])
                if live(t, CHUNKS):
                    need(pe, s_ready, t - 2)
                    need(pe, s_ready, t - 2)
                    project(t, p, PK)
                c = t + 1
                if live(c, CHUNKS):
                    need(pe, q_dec_ready, t)
                    need(pe, qt_ready, t)
                    need(pe, xt_lo_ready, t)
                    turn(t, p, TX, xn[q], [(xn_ready, c + 1)])
                c = t - 1
                if live(c, CHUNKS):
                    need(pe, k_dec_ready, c + 1)
                    need(pe, qkv_ready, 3 * c + 3)
                    need(pe, st_step, 2 * c - 1)
                    for g in range(GROUPS):
                        gs = slice(P * g, P * g + P)
                        mm = pe.matmul(ps_state[:, g, :], k_dec[q][:, gs], qkv[q][:, 2 * DIM + P * g:2 * DIM + P * g + P],
                                       start=True, stop=True)
                    mm.then_inc(upd_done, 1)
                if live(t, CHUNKS):
                    need(pe, qkv_ready, 3 * t + 1)
                    project(t, p, PV)
                c = t - 1
                if live(c, CHUNKS):
                    need(pe, qt_ready, c + 1)
                    need(pe, kt_ready, c + 1)
                    for g in range(GROUPS):
                        need(pe, masked_ready, GROUPS * c + g - 1)
                        pe.matmul(ps_score[g % 2][:, :, :], kt[q][:, g, :], q_wide[q][:, g, :, :],
                                  start=True, stop=True).then_inc(score_done, 1)
                c = t - 2
                if live(c, CHUNKS):
                    need(pe, ot_lo_ready, c + 1)
                    need(pe, qkv_ready, 3 * t + 2) if live(t, CHUNKS) else None
                    if isinstance(t, int) and t >= CHUNKS:
                        need(pe, qkv_ready, 3 * CHUNKS)
                        need(pe, s_ready, c - 1)
                    three_pass(pe, ps_proj[proj_bank(t, p, PO)][:, :],
                               lambda k: ot_hi[p][:, k, :], lambda k: ot_lo[p][:, k, :],
                               lambda k: wo_hi[:, k, :], lambda k: wo_lo[:, k, :], KD, proj_done)
                c = t - 1
                if live(c, CHUNKS):
                    need(pe, zeroed, 1)
                    need(pe, state_ready, c)
                    need(pe, q_dec_ready, c + 1)
                    need(pe, ot_lo_ready, c)
                    need(pe, masked_ready, GROUPS * c + GROUPS)
                    for g in range(GROUPS):
                        pe.matmul(ps_o[:, g, :], state[q][:, g, :], q_dec[q][:, g, :], start=True, stop=False,
                                  skip_group_check=True)
                        for h in range(HPG):
                            v = 2 * DIM + P * g + HD * h
                            mm = pe.matmul(ps_o[HD * h:HD * h + HD, g, :], qkv[q][:, v:v + HD], masked[q][:, g, h, :],
                                           start=False, stop=(h == HPG - 1), skip_group_check=True)
                    mm.then_inc(o_done, 1)
            ticks(pe, *sched, tick)


def layer0_ffn(nc, x, s_in, w_fcT, w_projT, x1_out, xt_out):
    x_t = x.rearrange("b (c p) d -> (b c) p d", p=P)
    s_t = s_in.rearrange("(c p) d -> c p d", p=P)
    x1_t = x1_out.rearrange("(c p) d -> c p d", p=P)
    KF = FC // P
    NF = FC // DIM
    PIECES = KD
    Q = 128.0
    with ExitStack() as ctx:
        sb = lambda name, shape, dt=F32: ctx.enter_context(nc.sbuf_tensor(f"l0_ffn_{name}", shape, dt))
        sem = lambda name: ctx.enter_context(nc.semaphore(f"l0_ffn_{name}"))
        t_fc = sb("t_fc", [P, KD, FC], F32R)
        t_proj = sb("t_proj", [P, KF, DIM], F32R)
        gamma_w = sb("gamma_w", [P, 2])
        ident = sb("ident", [P, P])
        eps5, eps6, minus_half, minus_one = (sb(n, [P, 1]) for n in ("eps5", "eps6", "minus_half", "minus_one"))

        with ExitStack() as prep:
            psb = lambda name, shape, dt=F32: prep.enter_context(nc.sbuf_tensor(f"l0_ffn_{name}", shape, dt))
            psem = lambda name: prep.enter_context(nc.semaphore(f"l0_ffn_{name}"))
            raws = [psb("raw_fc", [P, KD, FC]), psb("raw_proj", [P, KF, DIM])]
            parts = psb("parts", [P, 2, PIECES])
            sums = psb("sums", [P, 2])
            ones = psb("ones", [P, P])
            limit = psb("limit", [P, 2, 2])
            ps_sum = [prep.enter_context(nc.psum_tensor(f"l0_ffn_ps_sum{m}", [P, DIM], F32)) for m in range(2)]
            raw_in = [[psem(f"raw_{n}_in{i}") for i in range(PIECES)] for n in ("fc", "proj")]
            made, part_done, sum_done, total_done = psem("made"), psem("part_done"), psem("sum_done"), psem("total_done")
            gamma_done, limit_done, pool_below, dve_below = (psem(n) for n in ("gamma_done", "limit_done", "pool_below", "dve_below"))
            block = prep.enter_context(nc.Block())
            PC = KD * FC // PIECES

            def piece(t, i):
                return t[:, :, :].rearrange("p k n -> p (k n)")[:, PC * i:PC * (i + 1)]

            BY_POOL = [(0, 1), (0, 2), (0, 3), (1, 2), (1, 3)]

            def below(eng, m, i):
                return eng.tensor_scalar(piece((t_fc, t_proj)[m], i), piece(raws[m], i), limit[:, 1, m:m + 1], None, ALU.is_lt)

            @block.sync
            def _(sp):
                for i in range(PIECES):
                    sp.dma_start(piece(raws[0], i), w_fcT.rearrange("(k p) n -> p k n", p=P)[:, i, :]).then_inc(raw_in[0][i], 16)
                for i in range(PIECES):
                    rows = slice(KF // PIECES * i, KF // PIECES * (i + 1))
                    sp.dma_start(raws[1][:, rows, :], w_projT.rearrange("(k p) n -> p k n", p=P)[:, rows, :]).then_inc(raw_in[1][i], 16)

            @block.gpsimd
            def _(pool):
                pool.memset(ident[:, :], 0.0).then_inc(made, 1)
                pool.memset(ones[:, :], 1.0).then_inc(made, 1)
                pool.memset(eps5[:, :], 1e-5)
                pool.memset(eps6[:, :], 1e-6)
                pool.memset(minus_half[:, :], -0.5)
                pool.memset(minus_one[:, :], -1.0)
                pool.wait_ge(made, 2)
                pool.affine_select(out=ident[:, :], in_=ident[:, :], compare_op=ALU.not_equal, fill=1.0,
                                   base=0, pattern=[[-1, P]], channel_multiplier=1)
                for m, i in BY_POOL:
                    pool.wait_ge(limit_done, 2 * m + 1)
                    below(pool, m, i).then_inc(pool_below, 1)

            @block.tensor
            def _(pe):
                pe.wait_ge(made, 2)
                for m in range(2):
                    pe.wait_ge(sum_done, m + 1)
                    pe.matmul(ps_sum[m][:, 0:1], ones[:, :], sums[:, m:m + 1], start=True, stop=True).then_inc(total_done, 1)

            @block.vector
            def _(dve):
                for m in range(2):
                    for i in range(PIECES):
                        dve.wait_ge(raw_in[m][i], 16)
                        dve.tensor_reduce(parts[:, m, i:i + 1], piece(raws[m], i), AX.X, ALU.add, apply_absolute_value=True).then_inc(part_done, 1)
                    dve.wait_ge(part_done, PIECES * (m + 1))
                    dve.tensor_reduce(sums[:, m:m + 1], parts[:, m, :], AX.X, ALU.add).then_inc(sum_done, 1)
                    dve.wait_ge(total_done, m + 1)
                    dve.tensor_scalar(gamma_w[:, m:m + 1], ps_sum[m][:, 0:1], 1.0 / (DIM * FC), None, ALU.mult).then_inc(gamma_done, 1)
                    dve.wait_ge(gamma_done, m + 1)
                    dve.tensor_scalar(limit[:, 1, m:m + 1], gamma_w[:, m:m + 1], 1e-6, -0.5, ALU.add, ALU.mult).then_inc(limit_done, 1)
                    dve.tensor_scalar(limit[:, 0, m:m + 1], gamma_w[:, m:m + 1], 1e-6, 0.5, ALU.add, ALU.mult).then_inc(limit_done, 1)
                dve.wait_ge(limit_done, 4)
                own = 0
                for m, t in enumerate((t_fc, t_proj)):
                    for i in range(PIECES):
                        if (m, i) in BY_POOL:
                            dve.wait_ge(pool_below, BY_POOL.index((m, i)) + 1)
                        else:
                            below(dve, m, i).then_inc(dve_below, 1)
                            own += 1
                            dve.wait_ge(dve_below, own)
                        dve.scalar_tensor_tensor(out=piece(t, i), in0=piece(raws[m], i), scalar=limit[:, 0, m:m + 1],
                                                 in1=fp32(piece(t, i)), op0=ALU.is_gt, op1=ALU.subtract)

        two = lambda name, shape, dt=F32: [sb(f"{name}{i}", shape, dt) for i in range(2)]
        xa = two("xa", [P, DIM])
        xn = two("xn", [P, DIM])
        xnn = two("xnn", [P, DIM])
        codes = two("codes", [P, DIM])
        ct_hi, ct_lo = two("ct_hi", [P, KD, P], F32R), two("ct_lo", [P, KD, P], F32R)
        h = two("h", [P, FC])
        hn = two("hn", [P, FC])
        ht_hi, ht_lo = two("ht_hi", [P, KF, P], F32R), two("ht_lo", [P, KF, P], F32R)
        xb, s_sb, gate = two("xb", [P, DIM]), two("s_sb", [P, DIM]), two("gate", [P, DIM])
        x1 = two("x1", [P, DIM])
        xn1 = two("xn1", [P, DIM])
        xt1 = two("xt1", [P, 2, KD, P], F32R)
        st_a, st_b, st_f = two("st_a", [P, 6]), two("st_b", [P, 6]), two("st_f", [P, 6])
        st_h = two("st_h", [P, NF, 6])
        mv_a, mv_b, mv_h, mv_f = (two(n, [P, 2]) for n in ("mv_a", "mv_b", "mv_h", "mv_f"))
        r_a, r_b, r_h, r_f = (two(n, [P, 1]) for n in ("r_a", "r_b", "r_h", "r_f"))
        nmr_h = two("nmr_h", [P, 1])
        gam1, inv1, scale1, gam2, inv2, scale2 = (two(n, [P, 1]) for n in ("gam1", "inv1", "scale1", "gam2", "inv2", "scale2"))
        ps = lambda name, shape: ctx.enter_context(nc.psum_tensor(f"l0_ffn_{name}", shape, F32))
        ps_fc = [ps(f"ps_fc{i}", [P, DIM]) for i in range(NF)]
        ps_turn = [ps(f"ps_turn{i}", [P, 4, P]) for i in range(2)]
        ps_turn_x = ps("ps_turn_x", [P, 4, P])
        ps_out = ps("ps_out", [P, DIM])

        xa_in, xs_in, x1_stored, xt_stored = ([sem(f"{n}{i}") for i in range(2)] for n in ("xa_in", "xs_in", "x1_stored", "xt_stored"))
        ln_a, ln_b, ln_h, quant_h, mixed, ln_f = (sem(n) for n in ("ln_a", "ln_b", "ln_h", "quant_h", "mixed", "ln_f"))
        rstd_a, rstd_b, rstd_h, rstd_f = (sem(n) for n in ("rstd_a", "rstd_b", "rstd_h", "rstd_f"))
        c_turned, ct_hi_ready, ct_lo_ready = sem("c_turned"), sem("ct_hi_ready"), sem("ct_lo_ready")
        fc_done, gelu_done, hn_ready, h_scaled, h_clipped = (sem(n) for n in ("fc_done", "gelu_done", "hn_ready", "h_scaled", "h_clipped"))
        h_turned, ht_hi_ready, ht_lo_ready = sem("h_turned"), sem("ht_hi_ready"), sem("ht_lo_ready")
        out_done, gate_ready = sem("out_done"), sem("gate_ready")
        f_turned, xt1_hi_ready, xt1_lo_ready = sem("f_turned"), sem("xt1_hi_ready"), sem("xt1_lo_ready")
        block = ctx.enter_context(nc.Block())
        A_STAT, A_MV, A_XN, A_STAT2, A_MV2, A_N = 1, 2, 3, 4, 5, 5
        B_XNN, B_GAM, B_INV, B_SCALED, B_CODES, B_SC, B_N = 1, 2, 3, 4, 5, 6, 6
        H_N = NF + 1
        G_GAM, G_RCP, G_INV, G_SC, G_N = 1, 2, 3, 4, 4
        F_STAT, F_MV, F_XN, F_N = 1, 2, 3, 3
        M_MUL, M_X1, M_N = 1, 2, 2
        HN_AFTER = 1
        sched = (-3, 6, CHUNKS - 4, CHUNKS + 3)

        @block.sync
        def _(sp):
            def tick(t, p):
                c, b = t + 4, p
                if live(c, CHUNKS):
                    need(sp, ln_a, A_N * (c - 2) + A_XN)
                    sp.dma_start(xa[b][:, :], x_t[c]).then_inc(xa_in[b], 16)
                c, b = t - 2, p
                if live(c, CHUNKS):
                    need(sp, mixed, M_N * (c - 2) + M_X1)
                    sp.dma_start(xb[b][:, :], x_t[c]).then_inc(xs_in[b], 16)
                    sp.dma_start(s_sb[b][:, :], s_t[c]).then_inc(xs_in[b], 16)
                c, b = t - 3, 1 - p
                if live(c, CHUNKS):
                    need(sp, mixed, M_N * c + M_X1)
                    sp.dma_start(x1_t[c], x1[b][:, :]).then_inc(x1_stored[b], 16)
                c, b = t - 4, p
                if live(c, CHUNKS):
                    need(sp, xt1_lo_ready, c + 1)
                    need(sp, xt1_hi_ready, c + 1)
                    sp.dma_start(xt_out[c], fp32(xt1[b][:, :, :, :]).rearrange("p h k n -> p (h k n)")).then_inc(xt_stored[b], 16)
            ticks(sp, -4, 6, CHUNKS - 4, CHUNKS + 3, tick)
            for b in range(2):
                sp.wait_ge(x1_stored[b], 8 * CHUNKS)
                sp.wait_ge(xt_stored[b], 8 * CHUNKS)

        @block.gpsimd
        def _(pool):
            def rstd(c, r, mv, eps, waits, counts, per):
                for w, n in waits:
                    need(pool, w, n)
                pool.tensor_tensor(r[:, :], mv[:, 1:2], eps[:, :], ALU.add).then_inc(counts, 1)
                need(pool, counts, per * c + 1)
                pool.tensor_tensor(r[:, :], r[:, :], minus_half[:, :], ALU.pow).then_inc(counts, 1)

            def tick(t, p):
                f, fb = t - 3, 1 - p
                if live(f, CHUNKS):
                    need(pool, gate_ready, f + 1)
                    need(pool, xs_in[fb], 16 * (f - fb) + 32)
                    pool.tensor_tensor(gate[fb][:, :], gate[fb][:, :], s_sb[fb][:, :], ALU.mult).then_inc(mixed, 1)
                    need(pool, mixed, M_N * f + M_MUL)
                    need(pool, x1_stored[fb], 8 * (f - fb))
                    need(pool, ln_f, F_N * (f - 2) + F_XN)
                    pool.tensor_tensor(x1[fb][:, :], gate[fb][:, :], xb[fb][:, :], ALU.add).then_inc(mixed, 1)
                c, b = t + 3, 1 - p
                if live(c, CHUNKS):
                    rstd(c, r_a[b], mv_a[b], eps5, [(ln_a, A_N * c + A_MV), (ln_a, A_N * (c - 2) + A_XN)], rstd_a, 2)
                if live(f, CHUNKS):
                    rstd(f, r_f[fb], mv_f[fb], eps5, [(ln_f, F_N * f + F_MV)], rstd_f, 2)
                c, b = t, p
                if live(c, CHUNKS):
                    rstd(c, r_h[b], mv_h[b], eps6, [(ln_h, H_N * c + H_N), (hn_ready, c - 1)], rstd_h, 4)
                    need(pool, rstd_h, 4 * c + 2)
                    pool.tensor_tensor(nmr_h[b][:, :], mv_h[b][:, 0:1], r_h[b][:, :], ALU.mult).then_inc(rstd_h, 1)
                    need(pool, rstd_h, 4 * c + 3)
                    pool.tensor_tensor(nmr_h[b][:, :], nmr_h[b][:, :], minus_one[:, :], ALU.mult).then_inc(rstd_h, 1)
                c, b = t + 3, 1 - p
                if live(c, CHUNKS):
                    rstd(c, r_b[b], mv_b[b], eps6, [(ln_a, A_N * c + A_MV2), (ln_b, B_N * (c - 2) + B_XNN)], rstd_b, 2)
            ticks(pool, *sched, tick)

        @block.scalar
        def _(act):
            def tick(t, p):
                c, b = t - 4, p
                if live(c, CHUNKS):
                    need(act, f_turned, c + 1)
                    need(act, xt_stored[b], 8 * (c - b))
                    act.activation(xt1[b][:, 0, :, :], ps_turn_x[:, :, :], ACT.Copy).then_inc(xt1_hi_ready, 1)
                c, b = t - 3, 1 - p
                if live(c, CHUNKS):
                    need(act, out_done, c + 1)
                    need(act, quant_h, G_N * c + G_SC)
                    need(act, mixed, M_N * (c - 2) + M_X1)
                    act.activation(gate[b][:, :], ps_out[:, :], ACT.Silu, scale=scale2[b][:, 0:1]).then_inc(gate_ready, 1)
                for n in range(NF):
                    c = t - 2
                    if live(c, CHUNKS):
                        need(act, h_turned, NF * c + n + 1)
                        need(act, out_done, c - 1)
                        act.activation(ht_hi[p][:, 4 * n:4 * n + 4, :], ps_turn[n % 2][:, :, :], ACT.Copy).then_inc(ht_hi_ready, 1)
                    if live(t, CHUNKS):
                        need(act, fc_done, NF * t + n + 1)
                        need(act, ln_b, B_N * t + B_SC)
                        need(act, hn_ready, t - 1)
                        act.activation(h[p][:, DIM * n:DIM * n + DIM], ps_fc[n][:, :], ACT.Gelu,
                                       scale=scale1[p][:, 0:1]).then_inc(gelu_done, 1)
                    c, b = t - 1, 1 - p
                    if n == HN_AFTER and live(c, CHUNKS):
                        need(act, rstd_h, 4 * c + 4)
                        need(act, h_turned, NF * (c - 1))
                        act.activation(hn[b][:, :], h[b][:, :], ACT.Identity, bias=nmr_h[b][:, 0:1], scale=r_h[b][:, 0:1]).then_inc(hn_ready, 1)
                c, b = t + 1, 1 - p
                if live(c, CHUNKS):
                    need(act, c_turned, c + 1)
                    need(act, fc_done, NF * (c - 1))
                    act.activation(ct_hi[b][:, :, :], ps_turn_x[:, :, :], ACT.Copy).then_inc(ct_hi_ready, 1)
                c, b = t - 1, 1 - p
                if live(c, CHUNKS):
                    need(act, quant_h, G_N * c + G_INV)
                    act.activation(hn[b][:, :], hn[b][:, :], ACT.Copy, scale=inv2[b][:, 0:1]).then_inc(h_scaled, 1)
            ticks(act, *sched, tick)

        @block.vector
        def _(dve):
            def tick(t, p):
                f, fb = t - 3, 1 - p
                a, ab = t + 3, 1 - p
                q, qb = t + 2, p
                g, gb = t - 1, 1 - p

                def ht_low(n):
                    c = t - 2
                    if live(c, CHUNKS):
                        need(dve, ht_hi_ready, NF * c + n + 1)
                        dve.tensor_tensor(ht_lo[p][:, 4 * n:4 * n + 4, :], ps_turn[n % 2][:, :, :],
                                          fp32(ht_hi[p][:, 4 * n:4 * n + 4, :]), ALU.subtract).then_inc(ht_lo_ready, 1)

                def h_stats(n):
                    if live(t, CHUNKS):
                        need(dve, gelu_done, NF * t + n + 1)
                        dve.bn_stats(st_h[p][:, n, :], h[p][:, DIM * n:DIM * n + DIM]).then_inc(ln_h, 1)

                c = t - 4
                if live(c, CHUNKS):
                    need(dve, xt1_hi_ready, c + 1)
                    dve.tensor_tensor(xt1[p][:, 1, :, :], ps_turn_x[:, :, :], fp32(xt1[p][:, 0, :, :]),
                                      ALU.subtract).then_inc(xt1_lo_ready, 1)
                if live(a, CHUNKS):
                    need(dve, xa_in[ab], 8 * (a - ab) + 16)
                    dve.bn_stats(st_a[ab][:, :], xa[ab][:, :]).then_inc(ln_a, 1)
                ht_low(0)
                if live(a, CHUNKS):
                    need(dve, ln_a, A_N * a + A_STAT)
                if live(q, CHUNKS):
                    need(dve, rstd_b, 2 * q + 2)
                    need(dve, ln_b, B_N * (q - 1))
                    dve.tensor_scalar(xnn[qb][:, :], xn[qb][:, :], mv_b[qb][:, 0:1], r_b[qb][:, 0:1],
                                      ALU.subtract, ALU.mult).then_inc(ln_b, 1)
                if live(a, CHUNKS):
                    dve.bn_aggr(mv_a[ab][:, :], st_a[ab][:, :]).then_inc(ln_a, 1)
                h_stats(0)
                ht_low(1)
                if live(q, CHUNKS):
                    need(dve, ln_b, B_N * q + B_XNN)
                    dve.tensor_reduce(gam1[qb][:, :], xnn[qb][:, :], AX.X, ALU.max, apply_absolute_value=True).then_inc(ln_b, 1)
                    need(dve, ln_b, B_N * q + B_GAM)
                    dve.reciprocal(inv1[qb][:, :], gam1[qb][:, :]).then_inc(ln_b, 1)
                    need(dve, ln_b, B_N * q + B_INV)
                    dve.tensor_scalar(xnn[qb][:, :], xnn[qb][:, :], inv1[qb][:, 0:1], Q, ALU.mult, ALU.mult).then_inc(ln_b, 1)
                    need(dve, ln_b, B_N * q + B_SCALED)
                    need(dve, c_turned, q - 1)
                    dve.tensor_scalar(codes[qb][:, :], xnn[qb][:, :], Q, -Q, ALU.min, ALU.max).then_inc(ln_b, 1)
                if live(f, CHUNKS):
                    need(dve, mixed, M_N * f + M_X1)
                    dve.bn_stats(st_f[fb][:, :], x1[fb][:, :]).then_inc(ln_f, 1)
                ht_low(2)
                if live(f, CHUNKS):
                    need(dve, ln_f, F_N * f + F_STAT)
                if live(a, CHUNKS):
                    need(dve, rstd_a, 2 * a + 2)
                    need(dve, ln_b, B_N * (a - 2) + B_XNN)
                    dve.tensor_scalar(xn[ab][:, :], xa[ab][:, :], mv_a[ab][:, 0:1], r_a[ab][:, 0:1],
                                      ALU.subtract, ALU.mult).then_inc(ln_a, 1)
                if live(f, CHUNKS):
                    dve.bn_aggr(mv_f[fb][:, :], st_f[fb][:, :]).then_inc(ln_f, 1)
                ht_low(3)
                if live(g, CHUNKS):
                    need(dve, hn_ready, g + 1)
                    dve.tensor_reduce(gam2[gb][:, :], hn[gb][:, :], AX.X, ALU.max, apply_absolute_value=True).then_inc(quant_h, 1)
                    need(dve, quant_h, G_N * g + G_GAM)
                    dve.reciprocal(inv2[gb][:, :], gam2[gb][:, :]).then_inc(quant_h, 1)
                    need(dve, quant_h, G_N * g + G_RCP)
                    dve.tensor_scalar(inv2[gb][:, :], inv2[gb][:, :], Q, None, ALU.mult).then_inc(quant_h, 1)
                    need(dve, gate_ready, g - 1)
                    dve.tensor_scalar(scale2[gb][:, :], gam2[gb][:, :], gamma_w[:, 1:2], 1.0 / Q, ALU.mult, ALU.mult).then_inc(quant_h, 1)
                h_stats(1)
                if live(a, CHUNKS):
                    need(dve, ln_a, A_N * a + A_XN)
                    dve.bn_stats(st_b[ab][:, :], xn[ab][:, :]).then_inc(ln_a, 1)
                h_stats(2)
                if live(f, CHUNKS):
                    need(dve, rstd_f, 2 * f + 2)
                    need(dve, f_turned, f - 1)
                    dve.tensor_scalar(xn1[fb][:, :], x1[fb][:, :], mv_f[fb][:, 0:1], r_f[fb][:, 0:1],
                                      ALU.subtract, ALU.mult).then_inc(ln_f, 1)
                h_stats(3)
                if live(t, CHUNKS):
                    need(dve, ln_h, H_N * t + NF)
                if live(a, CHUNKS):
                    need(dve, ln_a, A_N * a + A_STAT2)
                c = t + 1
                if live(c, CHUNKS):
                    need(dve, ct_hi_ready, c + 1)
                    dve.tensor_tensor(ct_lo[1 - p][:, :, :], ps_turn_x[:, :, :], fp32(ct_hi[1 - p][:, :, :]),
                                      ALU.subtract).then_inc(ct_lo_ready, 1)
                if live(t, CHUNKS):
                    dve.bn_aggr(mv_h[p][:, :], st_h[p][:, :, :].rearrange("p n s -> p (n s)")).then_inc(ln_h, 1)
                if live(a, CHUNKS):
                    dve.bn_aggr(mv_b[ab][:, :], st_b[ab][:, :]).then_inc(ln_a, 1)
                if live(q, CHUNKS):
                    need(dve, gelu_done, NF * (q - 1))
                    dve.tensor_scalar(scale1[qb][:, :], gam1[qb][:, :], gamma_w[:, 0:1], 1.0 / Q, ALU.mult, ALU.mult).then_inc(ln_b, 1)
                if live(g, CHUNKS):
                    need(dve, h_scaled, g + 1)
                    dve.tensor_scalar(hn[gb][:, :], hn[gb][:, :], Q, -Q, ALU.min, ALU.max).then_inc(h_clipped, 1)
            ticks(dve, *sched, tick)

        @block.tensor
        def _(pe):
            def turn(bank, src, done):
                for k in range(4):
                    mm = pe.transpose(bank[:, k, :], src[:, k * P:(k + 1) * P], ident[:, :])
                mm.then_inc(done, 1)

            def tick(t, p):
                for n in range(NF):
                    if live(t, CHUNKS):
                        need(pe, ct_hi_ready, t + 1)
                        need(pe, ct_lo_ready, t + 1)
                        need(pe, gelu_done, NF * (t - 1) + n + 1)
                        two_pass(pe, ps_fc[n][:, :], lambda k: ct_hi[p][:, k, :], lambda k: ct_lo[p][:, k, :],
                                 lambda k: t_fc[:, k, DIM * n:DIM * n + DIM], range(KD), True, True).then_inc(fc_done, 1)
                    c = t - 2
                    if live(c, CHUNKS):
                        need(pe, h_clipped, c + 1)
                        need(pe, ht_lo_ready, NF * c + n - 1)
                        turn(ps_turn[n % 2], hn[p][:, DIM * n:DIM * n + DIM], h_turned)
                c = t + 1
                if live(c, CHUNKS):
                    need(pe, ln_b, B_N * c + B_CODES)
                    need(pe, xt1_lo_ready, t - 3)
                    turn(ps_turn_x, codes[1 - p], c_turned)
                c = t - 2
                if live(c, CHUNKS):
                    need(pe, gate_ready, c)
                    for n in range(NF):
                        need(pe, ht_lo_ready, NF * c + n + 1)
                        mm = two_pass(pe, ps_out[:, :], lambda k: ht_hi[p][:, k, :], lambda k: ht_lo[p][:, k, :],
                                      lambda k: t_proj[:, k, :], range(4 * n, 4 * n + 4), n == 0, n == NF - 1)
                    mm.then_inc(out_done, 1)
                c = t - 3
                if live(c, CHUNKS):
                    need(pe, ln_f, F_N * c + F_XN)
                    need(pe, ct_lo_ready, cap(t + 2, CHUNKS))
                    need(pe, xt1_lo_ready, c)
                    turn(ps_turn_x, xn1[1 - p], f_turned)
            ticks(pe, *sched, tick)


def layer1_attention(nc, xt_in, wqkvT, rope_cos, rope_sin, yt_out):
    NT = BATCH * GROUPS
    G3 = 3 * P
    QB = SEQ // DIM
    UNITS = QB * CPB * 2
    PVS = UNITS // 2
    LAST = 2 * CPB
    MAX_BANKS = 4
    RING = 8
    PIECES = 4
    ADDS = 2 * (CPB - 1)
    AUG = 3 * HD
    with ExitStack() as ctx:
        sb = lambda name, shape, dt=F32: ctx.enter_context(nc.sbuf_tensor(f"l1_attn_{name}", shape, dt))
        sem = lambda name: ctx.enter_context(nc.semaphore(f"l1_attn_{name}"))
        w_hi, w_lo = (sb(f"wqkv_{n}", [P, KD, GROUPS, G3], F32R) for n in ("hi", "lo"))
        cos_t, sin_t = sb("cos_t", [P, CPB, HD // 2]), sb("sin_t", [P, CPB, HD // 2])
        ident, ones = sb("ident", [P, P]), sb("ones", [P, HD])
        two = lambda name, shape, dt=F32: [sb(f"{name}{i}", shape, dt) for i in range(2)]
        ident_r = sb("ident_r", [P, P], F32R)
        q_tok, k_tok = two("q_tok", [P, HPG, AUG], F32R), two("k_tok", [P, HPG, P], F32R)
        minus_max = sb("minus_max", [P, CPB, P])
        with ExitStack() as prep:
            psb = lambda name, shape, dt=F32: prep.enter_context(nc.sbuf_tensor(f"l1_attn_{name}", shape, dt))
            psem = lambda name: prep.enter_context(nc.semaphore(f"l1_attn_{name}"))
            raw = psb("raw", [P, KD, GROUPS, G3])
            one_hot = psb("one_hot", [P, HPG, HD])
            raw_in = [psem(f"raw_in{k}") for k in range(KD)]
            made, w_hi_made, tabs_in = psem("made"), psem("w_hi_made"), psem("tabs_in")
            block = prep.enter_context(nc.Block())

            @block.sync
            def _(sp):
                for k in range(KD):
                    sp.dma_start(raw[:, k, :, :], wqkvT.rearrange("(k p) g n -> p k g n", p=P)[:, k, :, :]).then_inc(raw_in[k], 16)
                sp.dma_start(cos_t[:, :, :], rope_cos.rearrange("(c p) f -> p c f", p=P)).then_inc(tabs_in, 16)
                sp.dma_start(sin_t[:, :, :], rope_sin.rearrange("(c p) f -> p c f", p=P)).then_inc(tabs_in, 16)
                sp.wait_ge(tabs_in, 32)

            @block.gpsimd
            def _(pool):
                pool.memset(ident[:, :], 0.0).then_inc(made, 1)
                pool.memset(ones[:, :], 1.0)
                pool.memset(minus_max[:, :, :], 0.0)
                pool.memset(one_hot[:, :, :], 0.0).then_inc(made, 1)
                pool.wait_ge(made, 2)
                for h in range(HPG):
                    pool.memset(one_hot[:, h, h:h + 1], 1.0)
                pool.affine_select(out=ident[:, :], in_=ident[:, :], compare_op=ALU.not_equal, fill=1.0,
                                   base=0, pattern=[[-1, P]], channel_multiplier=1).then_inc(made, 1)

            @block.scalar
            def _(act):
                for k in range(KD):
                    act.wait_ge(raw_in[k], 16)
                    act.activation(w_hi[:, k, :, :], raw[:, k, :, :], ACT.Copy).then_inc(w_hi_made, 1)

            @block.vector
            def _(dve):
                for k in range(KD):
                    dve.wait_ge(w_hi_made, k + 1)
                    dve.tensor_tensor(w_lo[:, k, :, :], raw[:, k, :, :], fp32(w_hi[:, k, :, :]), ALU.subtract)
                dve.wait_ge(made, 3)
                dve.tensor_copy(ident_r[:, :], ident[:, :])
                for b in range(2):
                    dve.tensor_copy(k_tok[b][:, :, AUG:P], one_hot[:, :, :])

        xt = two("xt", [P, 2, KD, P], F32R)
        qk = two("qk", [P, 2, HPG, HD])
        turned_part, swapped = sb("turned_part", [P, 2, HPG, HD // 2]), sb("swapped", [P, 2, HPG, HD // 2])
        q_st, k_st = two("q_st", [P, HPG, SEQ], F32R), two("k_st", [P, HPG, SEQ], F32R)
        v = two("v", [P, CPB, P])
        maxima = sb("maxima", [P, CPB, HPG, 2])
        probs = [sb(f"probs{i}", [P, 2, DIM]) for i in range(RING)]
        summed = [[sb(f"summed{qb}_{pair}", [P, 2, DIM]) for pair in range(2)] for qb in range(QB)]
        den, inv_den = sb("den", [P, DIM]), sb("inv_den", [P, DIM])
        y_sb, y_out = two("y_sb", [P, DIM]), two("y_out", [P, DIM])
        ps = lambda name, shape: ctx.enter_context(nc.psum_tensor(f"l1_attn_{name}", shape, F32))
        ps_prep = ps("ps_prep", [P, 4, P])
        ps_max = [ps(f"ps_max{i}", [P, DIM]) for i in range(MAX_BANKS)]
        ps_sc = [ps(f"ps_sc{i}", [P, 4, P]) for i in range(2)]
        ps_y = ps("ps_y", [P, DIM])

        xt_ld, y_stored = ([sem(f"{n}{i}") for i in range(2)] for n in ("xt_ld", "y_stored"))
        prep_done, prep_read = sem("prep_done"), sem("prep_read")
        max_done, max_read = ([sem(f"{n}{i}") for i in range(MAX_BANKS)] for n in ("max_done", "max_read"))
        qk_copied, rope_step, stacked, max_ready = (sem(n) for n in ("qk_copied", "rope_step", "stacked", "max_ready"))
        score_done, exp_done, pv_done = sem("score_done"), sem("exp_done"), sem("pv_done")
        added, dve_added, y_copied, y_ready = (sem(n) for n in ("added", "dve_added", "y_copied", "y_ready"))
        inverted, first_pair_ready = sem("inverted"), sem("first_pair_ready")
        block = ctx.enter_context(nc.Block())

        N_MAX = CPB * HPG
        PREP_STEP, PREP_AT = 4, (0, 5, 7)
        DEN_AT = [2 * (LAST + 5), 2 * 7]
        TURN_AT = [2 * (UNITS - 1), 2 * (LAST - 1)]
        INVERT_AT = [LAST + 7, 11]
        MAX_UNITS = [(0, N_MAX // 2, LAST - 2, LAST + 3), (N_MAX // 2, N_MAX, LAST + 3, UNITS - 2), (N_MAX, 2 * N_MAX, 0, LAST - 2)]
        SECOND_HEAD = 1

        def preps(u):
            halves = [None] * (2 * UNITS)
            for c in range(CPB):
                for at, kind in zip(PREP_AT, ("proj", "q", "k")):
                    assert halves[PREP_STEP * c + at] is None
                    halves[PREP_STEP * c + at] = kind, c
            for at, kind in ((DEN_AT, "den"), (TURN_AT, "turn")):
                for qb in range(QB):
                    assert halves[at[qb]] is None
                    halves[at[qb]] = kind, qb
            return halves[2 * u:2 * u + 2]

        def maxes(u):
            out = []
            for first, last, lo, hi in MAX_UNITS:
                n = last - first
                for a in range(n):
                    if u == lo + a * (hi - lo) // n:
                        out.append(("max", first + a))
            return out

        def max_of(c):
            qb, a = c // N_MAX, c % N_MAX
            return CPB // QB * qb + a % (N_MAX // 2) // HPG, a % HPG, a // (N_MAX // 2)

        def back(e):
            if e[0] == "den":
                return 1 + e[1]
            return 1 if e == ("turn", 1) or e[0] == "max" and e[1] >= N_MAX else 0

        def exists(m, e):
            return e is not None and live(m - back(e), NT)

        def ring(uses, banks):
            of_tick = lambda m: [e for e in uses if exists(m, e)]
            before = lambda m: sum(len(of_tick(i)) for i in range(m))
            assert len(uses) % banks == 0

            def use(m, e):
                if isinstance(m, int):
                    n = before(m) + of_tick(m).index(e)
                    return n % banks, n // banks
                n = before(2) + uses.index(e)
                return n % banks, len(uses) // banks * (m - 2) + n // banks
            return use

        prep_use = ring([e for u in range(UNITS) for e in preps(u) if e], 1)
        max_use = ring([e for u in range(UNITS) for e in maxes(u)], MAX_BANKS)

        def prep_bank(m, e):
            banks = [ps_prep] + ps_sc if isinstance(m, int) and m == 0 else [ps_prep]
            n = prep_use(m, e)[1]
            return banks[n % len(banks)] if len(banks) > 1 else ps_prep, n - len(banks) + 1

        def adds_with(g, u):
            if u < 0:
                g, u = g - 1, u + UNITS
            qb, kt, pair = u // LAST, max(u // 2 % CPB, 1), u % 2
            if isinstance(g, int) and g == NT - 1:
                n = (CPB - 1) * qb + kt
                return (dve_added, n) if pair else (added, ADDS * QB * g + n)
            return added, ADDS * (QB * g + qb) + 2 * (kt - 1) + pair + 1

        def add(eng, m, u):
            g, kt, total = m - 1, u // 2 % CPB, summed[u // LAST][u % 2]
            need(eng, exp_done, 2 * (UNITS * g + u + 1))
            if kt > 1:
                need(eng, *adds_with(g, u - 2))
            elif live(g - 1, NT):
                need(eng, prep_done, prep_use(*((m, ("den", 1)) if u >= LAST else (m - 1, ("den", 0))))[1] + 1)
            old = probs[(u - 2) % RING] if kt == 1 else total
            eng.tensor_tensor(total[:, :, :], old[:, :, :], probs[u % RING][:, :, :], ALU.add).then_inc(adds_with(g, u)[0], 1)

        sched = (0, 4, NT, NT)

        @block.sync
        def _(sp):
            def tick(m, p):
                for c in range(CPB):
                    if live(m, NT):
                        b = c % 2
                        src = sp.snap(m // GROUPS * CPB + c) if not isinstance(m, int) else m // GROUPS * CPB + c
                        need(sp, qk_copied, CPB * m + c - 1)
                        sp.dma_start(fp32(xt[b][:, :, :, :]).rearrange("p h k n -> p (h k n)"), xt_in[src]).then_inc(xt_ld[b], 16)
                if live(m - 2, NT):
                    store(m - 2, 1)
                if live(m - 1, NT):
                    store(m - 1, 0)

            def store(g, qb):
                four = SEQ // P // QB
                at = g // GROUPS * CPB + qb * four
                grp = g % GROUPS
                if not isinstance(g, int):
                    at, grp = sp.snap(at), sp.snap(grp)
                need(sp, y_ready, QB * g + qb + 1)
                sp.dma_start(yt_out[bass.ds(at, four), :, bass.ds(grp, 1), :].rearrange("c p a n -> p c (a n)"),
                             y_out[qb][:, :].rearrange("p (c n) -> p c n", n=P)).then_inc(y_stored[qb], 16)
            ticks(sp, *sched, tick)
            store(NT - 1, 1)
            for b in range(2):
                sp.wait_ge(y_stored[b], 16 * NT)

        @block.scalar
        def _(act):
            def copy_out(g, qb):
                need(act, pv_done, PVS * g + CPB * (qb + 1))
                if live(g - 1, NT):
                    need(act, y_ready, QB * (g - 1) + qb + 1)
                act.activation(y_sb[qb][:, :], ps_y[:, :], ACT.Copy).then_inc(y_copied, 1)

            def copy_den(g, qb):
                need(act, inverted, PIECES * (QB * g + qb))
                act.activation(den[:, :], ps_prep[:, :, :].rearrange("p a n -> p (a n)"), ACT.Copy).then_inc(prep_read, 1)

            def tick(m, p):
                a = m - 1
                for u in range(UNITS):
                    if live(a, NT):
                        need(act, pv_done, PVS * a + (u - RING) // 2 + 1)
                        if u >= RING or live(a - 1, NT):
                            need(act, *adds_with(a, u - RING))
                        for i in range(2):
                            need(act, score_done, 2 * (UNITS * a + u) + i + 1)
                            act.activation(probs[u % RING][:, i, :], ps_sc[i][:, :, :].rearrange("p a n -> p (a n)"), ACT.Exp, scale=ATT_SCALE).then_inc(exp_done, 1)
                    if u == 1 and live(a - 1, NT):
                        copy_out(a - 1, 1)
                    if u == LAST + 1 and live(a, NT):
                        copy_out(a, 0)
                    for e in preps(u):
                        if not exists(m, e):
                            continue
                        kind, c = e
                        need(act, prep_done, prep_use(m, e)[1] + 1)
                        bank, _ = prep_bank(m, e)
                        if kind == "proj":
                            need(act, stacked, 2 * (CPB * m + c - 1))
                            act.activation(qk[c % 2][:, :, :, :].rearrange("p a h d -> p (a h d)"), bank[:, 0:2, :].rearrange("p a n -> p (a n)"), ACT.Copy).then_inc(qk_copied, 1)
                            act.activation(v[p][:, c, :], bank[:, 2, :], ACT.Copy).then_inc(prep_read, 1)
                        elif kind == "den":
                            copy_den(m - back(e), c)
                        elif kind == "turn":
                            for h in range(HPG):
                                ins = act.activation(q_st[(p + back(e)) % 2][AUG:P, h, DIM * c:DIM * c + DIM], bank[AUG:P, :, :].rearrange("p a n -> p (a n)"), ACT.Copy)
                                if h == 1:
                                    ins.then_inc(first_pair_ready, 1)
                            ins.then_inc(prep_read, 1)
                        else:
                            rows = slice(0, AUG) if kind == "q" else slice(0, P)
                            dst = (q_st if kind == "q" else k_st)[p]
                            act.activation(dst[rows, :, P * c:P * c + P], bank[rows, :, :], ACT.Copy).then_inc(prep_read, 1)
            ticks(act, *sched, tick)
            copy_out(NT - 1, 1)
            need(act, prep_done, prep_use(NT + 1, ("den", 1))[1] + 1)
            copy_den(NT - 1, 1)

        @block.gpsimd
        def _(pool):
            def tick(m, p):
                for u in range(UNITS):
                    last = isinstance(m, int) and m == NT
                    if u // 2 % CPB and live(m - 1, NT) and not (last and u % 2):
                        add(pool, m, u)
            ticks(pool, *sched, tick)

        @block.vector
        def _(dve):
            R = HD // 2
            S = 5

            def chunk(m, p, c, step):
                b, n = c % 2, CPB * m + c
                x = qk[b]
                sc = lambda t, lo, hi: t[:, c, lo:hi].rearrange("p (a f) -> p a f", a=1)
                flat = lambda ap: ap.rearrange("p a h d -> p (a h) d")
                qs, ks = q_tok[b], k_tok[b]
                if step == 0:
                    need(dve, qk_copied, n + 1)
                    dve.tensor_tensor(flat(turned_part[:, :, :, :]), flat(x[:, :, :, 0:R]), sc(cos_t, 0, R).to_broadcast([P, 2 * HPG, R]), ALU.mult).then_inc(rope_step, 1)
                    dve.tensor_tensor(flat(swapped[:, :, :, 0:R // 2]), flat(x[:, :, :, R // 2:R]), sc(sin_t, 0, R // 2).to_broadcast([P, 2 * HPG, R // 2]), ALU.mult).then_inc(rope_step, 1)
                    dve.tensor_tensor(flat(swapped[:, :, :, R // 2:R]), flat(x[:, :, :, 0:R // 2]), sc(sin_t, R // 2, R).to_broadcast([P, 2 * HPG, R // 2]), ALU.mult).then_inc(rope_step, 1)
                elif step == 1:
                    need(dve, rope_step, S * n + 3)
                    dve.tensor_tensor(flat(x[:, :, :, 0:R]), flat(turned_part[:, :, :, :]), flat(swapped[:, :, :, :]), ALU.add).then_inc(rope_step, 1)
                elif step == 2:
                    if not (isinstance(m, int) and m == 0 and c < 2):
                        use = prep_use(m, ("k", c - 2)) if c >= 2 else prep_use(m - 1, ("k", CPB + c - 2))
                        need(dve, prep_done, use[1] + 1)
                    need(dve, rope_step, S * n + 4)
                    q2 = qs[:, :, 0:2 * HD].rearrange("p h (t d) -> p h t d", t=2)
                    dve.tensor_copy(q2, x[:, 0, :, :].rearrange("p h (t d) -> p h t d", t=1).to_broadcast([P, HPG, 2, HD]))
                    k2 = ks[:, :, :].rearrange("p h (t d) -> p h t d", t=4)[:, :, 0:3:2, :]
                    dve.tensor_copy(k2, x[:, 1, :, :].rearrange("p h (t d) -> p h t d", t=1).to_broadcast([P, HPG, 2, HD])).then_inc(rope_step, 1)
                else:
                    need(dve, rope_step, S * n + 5)
                    dve.tensor_tensor(qs[:, :, 2 * HD:3 * HD], x[:, 0, :, :], fp32(qs[:, :, 0:HD]), ALU.subtract).then_inc(stacked, 1)
                    dve.tensor_tensor(ks[:, :, HD:2 * HD], x[:, 1, :, :], fp32(ks[:, :, 0:HD]), ALU.subtract).then_inc(stacked, 1)

            def normalise(g, qb, step):
                if step < PIECES:
                    cols = slice(DIM // PIECES * step, DIM // PIECES * (step + 1))
                    need(dve, prep_read, prep_use(g + 1 + qb, ("den", qb))[1] + 1)
                    need(dve, y_ready, QB * g + qb)
                    dve.reciprocal(inv_den[:, cols], den[:, cols]).then_inc(inverted, 1)
                    return
                need(dve, y_copied, QB * g + qb + 1)
                need(dve, inverted, PIECES * (QB * g + qb + 1))
                need(dve, y_stored[qb], 16 * g)
                dve.tensor_tensor(y_out[qb][:, :], y_sb[qb][:, :], inv_den[:, :], ALU.mult).then_inc(y_ready, 1)

            def maximum(m, c):
                bank, before = max_use(m, ("max", c))
                j, h, half = max_of(c)
                need(dve, max_done[bank], before + 1)
                dve.tensor_reduce(maxima[:, j, h, half:half + 1], ps_max[bank][:, :],
                                  AX.X, ALU.max).then_inc(max_read[bank], 1)
                if c % N_MAX == N_MAX - 1:
                    qb = c // N_MAX
                    js = slice(CPB // QB * qb, CPB // QB * (qb + 1))
                    for done in range(c - MAX_BANKS + 1, c + 1):
                        bk, bf = max_use(m, ("max", done))
                        need(dve, max_read[bk], bf + 1)
                    if not isinstance(m, int) or m > qb:
                        need(dve, prep_done, prep_use(m - 1, ("turn", qb))[1] + 1)
                    dve.tensor_reduce(minus_max[:, js, AUG:AUG + HPG], maxima[:, js, :, :], AX.X, ALU.max,
                                      negate=True).then_inc(max_ready, 1)

            def tick(m, p):
                for u in range(UNITS):
                    if isinstance(m, int) and m == NT and u % 2 == 0 and u and (u - 1) // 2 % CPB:
                        add(dve, m, u - 1)
                    todo = [e[1] for e in maxes(u) if exists(m, e)]
                    for c in range(CPB):
                        if u == PREP_STEP * c // 2 + 1 and live(m, NT):
                            for step in range(4):
                                chunk(m, p, c, step)
                                if todo:
                                    maximum(m, todo.pop(0))
                    for a in todo:
                        maximum(m, a)
                    for qb in range(QB):
                        if 0 <= u - INVERT_AT[qb] <= PIECES and live(m - 1 - qb, NT):
                            normalise(m - 1 - qb, qb, u - INVERT_AT[qb])
            ticks(dve, *sched, tick)
            add(dve, NT, UNITS - 1)
            for step in range(PIECES + 1):
                normalise(NT - 1, 1, step)

        @block.tensor
        def _(pe):
            def pv(g, p, j):
                qb, kt = j // CPB, j % CPB
                need(pe, exp_done, 2 * (UNITS * g + 2 * j + 2))
                if kt == 0:
                    need(pe, y_copied, QB * g + qb)
                for h in range(HPG):
                    mm = pe.matmul(ps_y[HD * h:HD * h + HD, :], v[p][:, kt, HD * h:HD * h + HD], probs[(2 * j + h // 2) % RING][:, h % 2, :],
                                   start=(kt == 0), stop=(kt == CPB - 1), skip_group_check=True)
                mm.then_inc(pv_done, 1)

            def scores(g, p, u, i):
                qb, kt, pair = u // LAST, u // 2 % CPB, u % 2
                if kt == 0 and pair == 0 and i == 0:
                    need(pe, first_pair_ready, QB * g + qb + 1)
                elif kt == 0 and i == 0:
                    m = g + 1 if qb else g
                    need(pe, prep_read, prep_use(m, ("turn", qb))[1] + 1)
                h = 2 * pair + i
                need(pe, exp_done, 2 * (UNITS * g + u - 1) + i + 1)
                pe.matmul(ps_sc[i][:, :, :].rearrange("p a n -> p (a n)"), k_st[p][:, h, P * kt:P * kt + P], q_st[p][:, h, DIM * qb:DIM * qb + DIM],
                          start=True, stop=True).then_inc(score_done, 1)

            def prepare(m, p, e):
                kind, c = e
                bank, read_before = prep_bank(m, e)
                need(pe, prep_read, read_before)
                n = CPB * m + c
                if kind == "proj":
                    b = c % 2
                    g = m % GROUPS
                    need(pe, xt_ld[b], 16 * (CPB // 2 * m + c // 2 + 1))
                    cols = lambda w: (lambda k: w[:, k, bass.ds(g, 1), :].rearrange("p a n -> p (a n)"))
                    three_pass(pe, bank[:, 0:3, :].rearrange("p a n -> p (a n)"), lambda k: xt[b][:, 0, k, :], lambda k: xt[b][:, 1, k, :],
                               cols(w_hi), cols(w_lo), KD, prep_done)
                elif kind == "den":
                    for pair in range(2):
                        need(pe, *adds_with(m - back(e), LAST * c + LAST - 2 + pair))
                    for h in range(HPG):
                        mm = pe.matmul(bank[HD * h:HD * h + HD, :, :].rearrange("p a n -> p (a n)"), ones[:, :], summed[c][h // 2][:, h % 2, :],
                                       start=True, stop=True, skip_group_check=True)
                    mm.then_inc(prep_done, 1)
                elif kind == "turn":
                    need(pe, max_ready, QB * (m - c) + c + 1)
                    for j in range(4):
                        mm = pe.transpose(bank[:, j, :], minus_max[:, 4 * c + j, :], ident[:, :])
                    mm.then_inc(prep_done, 1)
                else:
                    need(pe, stacked, 2 * n + 2)
                    src, cols = (q_tok[c % 2], AUG) if kind == "q" else (k_tok[c % 2], P)
                    for h in range(HPG):
                        mm = pe.transpose(bank[0:cols, h, :].bitcast(F32R), src[:, h, 0:cols], ident_r[:, :])
                    mm.then_inc(prep_done, 1)

            def maximum(m, p, e):
                kind, c = e
                bank, before = max_use(m, e)
                dst, b = ps_max[bank], (p + back(e)) % 2
                need(pe, max_read[bank], before)
                j, h, half = max_of(c)
                if c % (N_MAX // 2) == 0 and c < N_MAX:
                    need(pe, prep_read, prep_use(m, ("k", CPB // 2 * (half + 1) - 1))[1] + 1)
                pe.matmul(dst[:, :], q_st[b][0:AUG, h, P * j:P * j + P], k_st[b][0:AUG, h, DIM * half:DIM * half + DIM],
                          start=True, stop=True).then_inc(max_done[bank], 1)

            def tick(m, p):
                q = 1 - p
                for u in range(UNITS):
                    if u == 0 and live(m - 2, NT):
                        pv(m - 2, p, PVS - 1)
                    if u == LAST and live(m - 1, NT):
                        pv(m - 1, q, CPB - 1)
                    if live(m - 1, NT):
                        scores(m - 1, q, u, 0)
                    todo = [e for e in maxes(u) if exists(m, e)]
                    per_slot = -(-len(todo) // 4)
                    for slot in range(4):
                        if slot == SECOND_HEAD and live(m - 1, NT):
                            scores(m - 1, q, u, 1)
                        if slot % 2 and exists(m, preps(u)[slot // 2]):
                            prepare(m, p, preps(u)[slot // 2])
                        if slot == 2 and u % LAST and u % 2 == 0 and live(m - 1, NT):
                            pv(m - 1, q, u // 2 - 1)
                        for e in todo[per_slot * slot:per_slot * (slot + 1)]:
                            maximum(m, p, e)
            ticks(pe, *sched, tick)
            pv(NT - 1, (NT - 1) % 2, PVS - 1)
            prepare(NT + 1, (NT + 1) % 2, ("den", 1))


def layer1_ffn(nc, x1_in, xt_in, yt_in, woT, gateT, upT, downT, s_gate, s_up, s_down, out):
    x1_t = x1_in.rearrange("(c p) d -> c p d", p=P)
    out_t = out.rearrange("b (c p) d -> (b c) p d", p=P)
    KH = HID // P
    cuts = [(0, DIM), (DIM, 2 * DIM), (2 * DIM, HID)]
    with ExitStack() as ctx:
        sb = lambda name, shape, dt=F32: ctx.enter_context(nc.sbuf_tensor(f"l1_ffn_{name}", shape, dt))
        sem = lambda name: ctx.enter_context(nc.semaphore(f"l1_ffn_{name}"))
        wo_hi, wo_lo = (sb(f"wo_{n}", [P, KD, DIM], F32R) for n in ("hi", "lo"))
        w_gu = sb("w_gu", [P, 2, KD, HID], F32R)
        w_down = sb("w_down", [P, KH, DIM], F32R)
        sc_gu = sb("sc_gu", [P, 2, HID])
        sc_down = sb("sc_down", [P, DIM])
        ident = sb("ident", [P, P])
        with ExitStack() as prep:
            psb = lambda name, shape, dt=F32: prep.enter_context(nc.sbuf_tensor(f"l1_ffn_{name}", shape, dt))
            psem = lambda name: prep.enter_context(nc.semaphore(f"l1_ffn_{name}"))
            raw_gu = psb("raw_gu", [P, 2, KD, HID], I32)
            raw_down = psb("raw_down", [P, KH, DIM], I32)
            raw_o = psb("raw_o", [P, KD, DIM])
            raw_in = [psem(f"raw_in{i}") for i in range(4)]
            made, split = psem("made"), psem("split")
            scales_in = psem("scales_in")
            block = prep.enter_context(nc.Block())

            @block.sync
            def _(sp):
                sp.dma_start(raw_o[:, :, :], woT.rearrange("(k p) n -> p k n", p=P)).then_inc(raw_in[3], 16)
                sp.dma_start(raw_gu[:, 0, :, :], gateT.rearrange("(k p) n -> p k n", p=P)).then_inc(raw_in[0], 16)
                sp.dma_start(raw_gu[:, 1, :, :], upT.rearrange("(k p) n -> p k n", p=P)).then_inc(raw_in[1], 16)
                sp.dma_start(raw_down[:, :, :], downT.rearrange("(k p) n -> p k n", p=P)).then_inc(raw_in[2], 16)
                sp.wait_ge(scales_in, 48)

            @block.scalar
            def _(act):
                act.dma_start(sc_gu[:, 0, :], s_gate.rearrange("(a n) -> a n", a=1).to_broadcast([P, HID])).then_inc(scales_in, 16)
                act.dma_start(sc_gu[:, 1, :], s_up.rearrange("(a n) -> a n", a=1).to_broadcast([P, HID])).then_inc(scales_in, 16)
                act.dma_start(sc_down[:, :], s_down.rearrange("(a n) -> a n", a=1).to_broadcast([P, DIM])).then_inc(scales_in, 16)

            @block.gpsimd
            def _(pool):
                pool.memset(ident[:, :], 0.0).then_inc(made, 1)
                pool.wait_ge(made, 1)
                pool.affine_select(out=ident[:, :], in_=ident[:, :], compare_op=ALU.not_equal, fill=1.0,
                                   base=0, pattern=[[-1, P]], channel_multiplier=1)

            @block.vector
            def _(dve):
                dve.wait_ge(raw_in[3], 16)
                dve.tensor_copy(wo_hi[:, :, :], raw_o[:, :, :]).then_inc(split, 1)
                dve.wait_ge(split, 1)
                dve.tensor_tensor(wo_lo[:, :, :], raw_o[:, :, :], fp32(wo_hi[:, :, :]), ALU.subtract)
                for i in range(2):
                    dve.wait_ge(raw_in[i], 16)
                    dve.tensor_scalar(w_gu[:, i, :, :], raw_gu[:, i, :, :], ZERO_POINT, None, ALU.subtract)
                dve.wait_ge(raw_in[2], 16)
                dve.tensor_scalar(w_down[:, :, :], raw_down[:, :, :], ZERO_POINT, None, ALU.subtract)

        two = lambda name, shape, dt=F32: [sb(f"{name}{i}", shape, dt) for i in range(2)]
        xt = two("xt", [P, 2, KD, P], F32R)
        yt = two("yt", [P, GROUPS, P])
        yt_hi, yt_lo = two("yt_hi", [P, GROUPS, P], F32R), two("yt_lo", [P, GROUPS, P], F32R)
        x1 = two("x1", [P, DIM])
        gate, up, mixed = two("gate", [P, HID]), two("up", [P, HID]), two("mixed", [P, HID])
        ht_hi, ht_lo = two("ht_hi", [P, KH, P], F32R), two("ht_lo", [P, KH, P], F32R)
        s_sb, g_sb, res = two("s_sb", [P, DIM]), two("g_sb", [P, DIM]), two("res", [P, DIM])
        ps = lambda name, shape: ctx.enter_context(nc.psum_tensor(f"l1_ffn_{name}", shape, F32))
        ps_gu = [ps(f"ps_gu{i}", [P, DIM]) for i in range(3)]
        ps_turn = [ps(f"ps_turn{i}", [P, 4, P]) for i in range(2)]
        ps_s = ps("ps_s", [P, DIM])
        ps_down = [ps(f"ps_down{i}", [P, DIM]) for i in range(2)]

        xt_ld, yt_ld, x1_ld, stored = ([sem(f"{n}{i}") for i in range(2)] for n in ("xt_ld", "yt_ld", "x1_ld", "stored"))
        yt_hi_ready, yt_lo_ready = sem("yt_hi_ready"), sem("yt_lo_ready")
        gu_done, gate_scaled, up_scaled, silu_done, mixed_ready = (sem(n) for n in ("gu_done", "gate_scaled", "up_scaled", "silu_done", "mixed_ready"))
        turned, ht_hi_ready, ht_lo_ready = sem("turned"), sem("ht_hi_ready"), sem("ht_lo_ready")
        s_done, s_ready, down_done, final, g_ready = (sem(n) for n in ("s_done", "s_ready", "down_done", "final", "g_ready"))
        block = ctx.enter_context(nc.Block())
        N = len(cuts)
        F_SCALED, F_MUL, F_ADD, F_N = 1, 2, 3, 3
        sched = (-1, 4, CHUNKS - 2, CHUNKS + 1)

        @block.sync
        def _(sp):
            def tick(t, p):
                c, b = t + 2, p
                if live(c, CHUNKS):
                    need(sp, gu_done, 2 * N * (c - 1))
                    sp.dma_start(fp32(xt[b][:, :, :, :]).rearrange("p h k n -> p (h k n)"), xt_in[c]).then_inc(xt_ld[b], 16)
                    need(sp, yt_lo_ready, c - 1)
                    sp.dma_start(yt[b][:, :, :], yt_in[c]).then_inc(yt_ld[b], 16)
                c, b = t, p
                if live(c, CHUNKS):
                    need(sp, final, F_N * (c - 1))
                    sp.dma_start(x1[b][:, :], x1_t[c]).then_inc(x1_ld[b], 16)
                c, b = t - 2, p
                if live(c, CHUNKS):
                    need(sp, final, F_N * c + F_ADD)
                    sp.dma_start(out_t[c], res[b][:, :]).then_inc(stored[b], 16)
            ticks(sp, -2, 4, CHUNKS - 2, CHUNKS + 1, tick)
            for b in range(2):
                sp.wait_ge(stored[b], 8 * CHUNKS)

        @block.gpsimd
        def _(pool):
            def tick(t, p):
                if live(t, CHUNKS):
                    for n, (lo, hi) in enumerate(cuts):
                        need(pool, silu_done, N * t + n + 1)
                        need(pool, up_scaled, N * t + n + 1)
                        need(pool, turned, N * (t - 1))
                        pool.tensor_tensor(mixed[p][:, lo:hi], gate[p][:, lo:hi], up[p][:, lo:hi], ALU.mult).then_inc(mixed_ready, 1)
            ticks(pool, *sched, tick)

        @block.scalar
        def _(act):
            def tick(t, p):
                c, b = t - 2, p
                if live(c, CHUNKS):
                    need(act, final, F_N * c + F_SCALED)
                    act.activation(g_sb[b][:, :], g_sb[b][:, :], ACT.Silu).then_inc(g_ready, 1)
                c, b = t + 1, 1 - p
                if live(c, CHUNKS):
                    need(act, yt_ld[b], 8 * (c - b) + 16)
                    need(act, s_done, c - 1)
                    act.activation(yt_hi[b][:, :, :], yt[b][:, :, :], ACT.Copy).then_inc(yt_hi_ready, 1)
                for n, (lo, hi) in enumerate(cuts):
                    if live(t, CHUNKS):
                        need(act, gate_scaled, N * t + n + 1)
                        act.activation(gate[p][:, lo:hi], gate[p][:, lo:hi], ACT.Silu).then_inc(silu_done, 1)
                    c, b = t - 1, 1 - p
                    if live(c, CHUNKS):
                        need(act, turned, N * c + n + 1)
                        need(act, down_done, c - 1)
                        act.activation(ht_hi[b][:, lo // P:hi // P, :], ps_turn[(N * b + n) % 2][:, 0:(hi - lo) // P, :], ACT.Copy).then_inc(ht_hi_ready, 1)
                if live(t, CHUNKS):
                    need(act, s_done, t + 1)
                    need(act, final, F_N * (t - 2) + F_MUL)
                    act.activation(s_sb[p][:, :], ps_s[:, :], ACT.Copy).then_inc(s_ready, 1)
            ticks(act, *sched, tick)

        @block.vector
        def _(dve):
            def tick(t, p):
                c, b = t - 2, p
                if live(c, CHUNKS):
                    need(dve, down_done, c + 1)
                    dve.tensor_tensor(g_sb[b][:, :], ps_down[b][:, :], sc_down[:, :], ALU.mult).then_inc(final, 1)
                cy, by = t + 1, 1 - p
                if live(cy, CHUNKS):
                    need(dve, yt_hi_ready, cy + 1)
                    need(dve, s_done, cy - 1)
                    dve.tensor_tensor(yt_lo[by][:, :, :], yt[by][:, :, :], fp32(yt_hi[by][:, :, :]), ALU.subtract).then_inc(yt_lo_ready, 1)
                for n, (lo, hi) in enumerate(cuts):
                    if live(t, CHUNKS):
                        if n == 0:
                            need(dve, mixed_ready, N * (t - 1))
                        need(dve, gu_done, 2 * (N * t + n) + 1)
                        dve.tensor_tensor(gate[p][:, lo:hi], ps_gu[2 * n % 3][:, 0:hi - lo], sc_gu[:, 0, lo:hi], ALU.mult).then_inc(gate_scaled, 1)
                        need(dve, gu_done, 2 * (N * t + n) + 2)
                        dve.tensor_tensor(up[p][:, lo:hi], ps_gu[(2 * n + 1) % 3][:, 0:hi - lo], sc_gu[:, 1, lo:hi], ALU.mult).then_inc(up_scaled, 1)
                    ct, bt = t - 1, 1 - p
                    if live(ct, CHUNKS):
                        need(dve, ht_hi_ready, N * ct + n + 1)
                        dve.tensor_tensor(ht_lo[bt][:, lo // P:hi // P, :], ps_turn[(N * bt + n) % 2][:, 0:(hi - lo) // P, :],
                                          fp32(ht_hi[bt][:, lo // P:hi // P, :]), ALU.subtract).then_inc(ht_lo_ready, 1)
                    if live(c, CHUNKS) and n == 0:
                        need(dve, g_ready, c + 1)
                        need(dve, s_ready, c + 1)
                        dve.tensor_tensor(g_sb[b][:, :], g_sb[b][:, :], s_sb[b][:, :], ALU.mult).then_inc(final, 1)
                    if live(c, CHUNKS) and n == 1:
                        need(dve, final, F_N * c + F_MUL)
                        need(dve, x1_ld[b], 8 * (c - b) + 16)
                        need(dve, stored[b], 8 * (c - b))
                        dve.tensor_tensor(res[b][:, :], g_sb[b][:, :], x1[b][:, :], ALU.add).then_inc(final, 1)
            ticks(dve, *sched, tick)

        @block.tensor
        def _(pe):
            def tick(t, p):
                q = 1 - p
                for n, (lo, hi) in enumerate(cuts):
                    if live(t, CHUNKS):
                        need(pe, xt_ld[p], 8 * (t - p) + 16)
                        for w in range(2):
                            use = 2 * n + w - 3
                            need(pe, (gate_scaled, up_scaled)[use % 2], N * t + (use // 2) + 1)
                            two_pass(pe, ps_gu[(2 * n + w) % 3][:, 0:hi - lo], lambda k: xt[p][:, 0, k, :], lambda k: xt[p][:, 1, k, :],
                                     lambda k: w_gu[:, w, k, lo:hi], range(KD), True, True).then_inc(gu_done, 1)
                    c = t - 1
                    if live(c, CHUNKS):
                        need(pe, mixed_ready, N * c + n + 1)
                        need(pe, ht_lo_ready, N * c + n - 1)
                        for k in range(lo // P, hi // P):
                            mm = pe.transpose(ps_turn[(N * q + n) % 2][:, k - lo // P, :], mixed[q][:, k * P:(k + 1) * P], ident[:, :])
                        mm.then_inc(turned, 1)
                if live(t, CHUNKS):
                    need(pe, yt_hi_ready, t + 1)
                    need(pe, yt_lo_ready, t + 1)
                    need(pe, s_ready, t)
                    three_pass(pe, ps_s[:, :], lambda k: yt_hi[p][:, k, :], lambda k: yt_lo[p][:, k, :],
                               lambda k: wo_hi[:, k, :], lambda k: wo_lo[:, k, :], KD, s_done)
                c = t - 1
                if live(c, CHUNKS):
                    need(pe, final, F_N * (c - 2) + F_SCALED)
                    for n, (lo, hi) in enumerate(cuts):
                        need(pe, ht_lo_ready, N * c + n + 1)
                        mm = two_pass(pe, ps_down[q][:, :], lambda k: ht_hi[q][:, k, :], lambda k: ht_lo[q][:, k, :],
                                      lambda k: w_down[:, k, :], range(lo // P, hi // P), n == 0, n == N - 1)
                    mm.then_inc(down_done, 1)
            ticks(pe, *sched, tick)


def layers(nc, x, Wqkv, bqkv, Wout, bout, slopes, w_fcT, w_projT, wqkvT, rope_cos, rope_sin, woT,
           gateT, s_gate, upT, s_up, downT, s_down, out):
    dram = lambda name, shape: nc.dram_tensor(name, shape, F32, kind="Internal").ap()
    s0 = dram("s0", [TOKENS, DIM])
    x1 = dram("x1_rows", [TOKENS, DIM])
    xt = dram("xt_chunks", [CHUNKS, P, 2 * KD * P])
    yt = dram("yt_chunks", [CHUNKS, P, GROUPS, P])
    layer0_attention(nc, x, Wqkv, bqkv, Wout, bout, slopes, s0)
    layer0_ffn(nc, x, s0, w_fcT, w_projT, x1, xt)
    layer1_attention(nc, xt, wqkvT, rope_cos, rope_sin, yt)
    layer1_ffn(nc, x1, xt, yt, woT, gateT, upT, downT, s_gate, s_up, s_down, out)


def rope_tables(np):
    inv_freq = (np.float32(1.0) / np.float32(10000.0) ** (np.arange(0, HD, 2, dtype=np.float32) / np.float32(HD))).astype(np.float32)
    angle = np.arange(SEQ, dtype=np.float32)[:, None] * inv_freq[None, :]
    sign = np.where(np.arange(HD // 2) < HD // 4, -1.0, 1.0).astype(np.float32)
    return np.cos(angle), np.sin(angle) * sign


def kernel(**inputs):
    import numpy as np
    import concourse.bacc as bacc
    from concourse import mybir as mb
    from concourse.bass_utils import run_bass_kernel_spmd

    a = {name: np.asarray(value) for name, value in inputs.items()}
    turned = lambda name: np.ascontiguousarray(a[name].T)
    wqkvT = np.stack([a[f"L1_attn_{n}"].T.reshape(DIM, GROUPS, P) for n in ("wq", "wk", "wv")], 2).reshape(DIM, GROUPS, 3 * P)
    cos, sin = rope_tables(np)
    laid_out = {
        "x": a["L0_attn_x"], "Wqkv": a["L0_attn_Wqkv"], "bqkv": a["L0_attn_bqkv"], "Wout": a["L0_attn_Wout"],
        "bout": a["L0_attn_bout"], "slopes": a["L0_attn_slopes"], "w_fcT": turned("L0_ffn_w_fc"),
        "w_projT": turned("L0_ffn_w_proj"), "wqkvT": wqkvT, "rope_cos": cos, "rope_sin": sin,
        "woT": turned("L1_attn_wo"), "gateT": turned("L1_ffn_wq_gate"), "s_gate": a["L1_ffn_s_gate"],
        "upT": turned("L1_ffn_wq_up"), "s_up": a["L1_ffn_s_up"], "downT": turned("L1_ffn_wq_down"),
        "s_down": a["L1_ffn_s_down"]}
    nc = bacc.Bacc("TRN2", target_bir_lowering=False, num_devices=1)
    arrays, args = {}, []
    for name, value in laid_out.items():
        arrays[f"in_{name}"] = np.ascontiguousarray(value)
        args.append(nc.dram_tensor(f"in_{name}", value.shape, mb.dt.from_np(value.dtype), kind="ExternalInput").ap())
    out = nc.dram_tensor("out_x", (BATCH, SEQ, DIM), mb.dt.float32, kind="ExternalOutput").ap()
    layers(nc, *args, out)
    result = run_bass_kernel_spmd(nc, [arrays], core_ids=[0])
    return result.results[0]["out_x"]
```
